# Optimizing a Trainium2 kernel written in Bass

```python
import numpy as np
import jax
import jax.numpy as jnp

def _softmax(x, axis=-1):
    return jax.nn.softmax(x, axis=axis)

def _gelu(x):
    return jax.nn.gelu(x, approximate=True)

def _silu(x):
    return jax.nn.silu(x)

def _sigmoid(x):
    return jax.nn.sigmoid(x)

def _layernorm(x, axis=-1, eps=1e-05):
    m = jnp.mean(x, axis=axis, keepdims=True)
    v = jnp.var(x, axis=axis, keepdims=True)
    return (x - m) / jnp.sqrt(v + eps)

def _scatter_add(tgt, idx, src, axis=0):
    return tgt.at[idx].add(src)

def _segment_sum(src, seg, n):
    return jax.ops.segment_sum(src, seg, n)
kernel_name = 'mk_xattn_seq_d4_seqx_r8_168a00'

def setup_inputs(seed: int=0):
    np.random.seed(seed)
    _w = jnp.asarray

    def _rec_inputs():
        import jax
        import jax.numpy as jnp
        _rk = jax.random.key(seed)
        x = -0.0002928 + 1 * jax.random.normal(jax.random.fold_in(_rk, 1), (4, 256, 128), jnp.float32)
        _lenS = 256 - jax.random.randint(jax.random.fold_in(_rk, 7), (4,), 0, max(1, 256 // 4) + 1, jnp.int32)
        _lenS2 = 256 - jax.random.randint(jax.random.fold_in(_rk, 8), (4,), 0, max(1, 256 // 4) + 1, jnp.int32)
        _ctx_1024P = jax.random.normal(jax.random.fold_in(_rk, 11), (4, 16, 128), jnp.float32)
        _ctx_1024c = jax.random.dirichlet(jax.random.fold_in(_rk, 511), 0.3 * jnp.ones((16,), jnp.float32), (4, 256))
        _ctx_1024t = jnp.einsum('bsk,bkd->bsd', _ctx_1024c, _ctx_1024P)
        _ctx_1024t = _ctx_1024t * jax.lax.rsqrt(jnp.mean(jnp.square(_ctx_1024t)) + 1e-12) * 0.953939
        ctx_1024 = -1.39393e-06 + 0.999914 * (_ctx_1024t + 0.3 * jax.random.normal(jax.random.fold_in(_rk, 611), (4, 256, 128), jnp.float32))
        pos_BxS2 = jnp.broadcast_to(jnp.arange(256, dtype=jnp.int32), (4, 256))
        return (x, ctx_1024, pos_BxS2)
    x, ctx_1024, pos_BxS2 = _rec_inputs()

    def _L0_xattn_setup():
        import jax, jax.numpy as jnp
        import numpy as np
        NUM_HEADS = 16
        ROPE_BASE = 10000.0
        MAX_POS = 512

        def _rope_tables(head_dim):
            inv_freq = 1.0 / ROPE_BASE ** (np.arange(0, head_dim, 2, dtype=np.float32) / head_dim)
            freqs = np.arange(MAX_POS, dtype=np.float32)[:, None] * inv_freq[None, :]
            emb = np.concatenate([freqs, freqs], axis=-1)
            return (jnp.asarray(np.cos(emb)), jnp.asarray(np.sin(emb)))

        def _rotate_half(x):
            d = x.shape[-1] // 2
            return jnp.concatenate([-x[..., d:], x[..., :d]], axis=-1)

        def _apply_rope(x, pos, cos_t, sin_t):
            cos = cos_t[pos][:, None]
            sin = sin_t[pos][:, None]
            return x * cos + _rotate_half(x) * sin
        key = jax.random.key(seed)
        ks = jax.random.split(key, 8)
        B, N, M, C = (2, 256, 256, 128)
        s = 1.0 / np.sqrt(C)
        return {'query': jax.random.normal(ks[0], (B, N, C), jnp.float32), 'key': jax.random.normal(ks[1], (B, M, C), jnp.float32), 'query_pos': jnp.broadcast_to(jnp.arange(N, dtype=jnp.int32), (B, N)), 'key_pos': jnp.broadcast_to(jnp.arange(M, dtype=jnp.int32), (B, M)), 'Wq': jax.random.normal(ks[2], (C, C), jnp.float32) * s, 'bq': jnp.zeros((C,), jnp.float32), 'Wk': jax.random.normal(ks[3], (C, C), jnp.float32) * s, 'Wv': jax.random.normal(ks[4], (C, C), jnp.float32) * s, 'bv': jnp.zeros((C,), jnp.float32), 'Wo': jax.random.normal(ks[5], (C, C), jnp.float32) * s, 'bo': jnp.zeros((C,), jnp.float32)}
    _L0_xattn_all = _L0_xattn_setup()
    _L0_xattn_in = {k: v for k, v in _L0_xattn_all.items() if k in ('Wq', 'bq', 'Wk', 'Wv', 'bv', 'Wo', 'bo')}
    del _L0_xattn_all

    def _L1_xattn_setup():
        import jax, jax.numpy as jnp
        import numpy as np
        EPS = 1e-06
        H = 16

        def _ln(x):
            mu = jnp.mean(x, axis=-1, keepdims=True)
            var = jnp.mean(jnp.square(x - mu), axis=-1, keepdims=True)
            return (x - mu) / jnp.sqrt(var + EPS)

        def _mod(x, shift, scale):
            return x * (1.0 + scale[:, None, :]) + shift[:, None, :]

        def _heads(x, qkv_w, qkv_b):
            B, N, C = x.shape
            hd = C // H
            qkv = (x @ qkv_w + qkv_b).reshape(B, N, 3, H, hd).transpose(2, 0, 3, 1, 4)
            return (qkv[0], qkv[1], qkv[2])

        def _attend(q, k, v):
            sc = q.shape[-1] ** (-0.5)
            a = jax.nn.softmax(jnp.einsum('bhnd,bhmd->bhnm', q, k) * sc, axis=-1)
            o = jnp.einsum('bhnm,bhmd->bhnd', a, v)
            B, h, N, hd = o.shape
            return o.transpose(0, 2, 1, 3).reshape(B, N, h * hd)

        def _mha(x, qkv_w, qkv_b, proj_w, proj_b):
            q, k, v = _heads(x, qkv_w, qkv_b)
            return _attend(q, k, v) @ proj_w + proj_b
        key = jax.random.key(seed)
        ks = jax.random.split(key, 16)
        B, T, D = (2, 256, 128)
        Dh = 4 * D
        s = 0.02
        return {'x': jax.random.normal(ks[0], (B, T, D), jnp.float32), 'c': jax.random.normal(ks[1], (B, 2, D), jnp.float32), 'attn_qkv_w': jax.random.normal(ks[2], (D, 3 * D), jnp.float32) * s, 'attn_qkv_b': jnp.zeros((3 * D,), jnp.float32), 'attn_proj_w': jax.random.normal(ks[3], (D, D), jnp.float32) * s, 'attn_proj_b': jnp.zeros((D,), jnp.float32), 'crs_qkv_w': jax.random.normal(ks[4], (D, 3 * D), jnp.float32) * s, 'crs_qkv_b': jnp.zeros((3 * D,), jnp.float32), 'crs_proj_w': jax.random.normal(ks[5], (D, D), jnp.float32) * s, 'crs_proj_b': jnp.zeros((D,), jnp.float32), 'mlp_fc1_w': jax.random.normal(ks[6], (D, Dh), jnp.float32) * s, 'mlp_fc1_b': jnp.zeros((Dh,), jnp.float32), 'mlp_fc2_w': jax.random.normal(ks[7], (Dh, D), jnp.float32) * s, 'mlp_fc2_b': jnp.zeros((D,), jnp.float32), 'ada_w': jax.random.normal(ks[8], (D, 9 * D), jnp.float32) * s, 'ada_b': jnp.zeros((9 * D,), jnp.float32)}
    _L1_xattn_all = _L1_xattn_setup()
    _L1_xattn_in = {k: v for k, v in _L1_xattn_all.items() if k in ('attn_qkv_w', 'attn_qkv_b', 'attn_proj_w', 'attn_proj_b', 'crs_qkv_w', 'crs_qkv_b', 'crs_proj_w', 'crs_proj_b', 'mlp_fc1_w', 'mlp_fc1_b', 'mlp_fc2_w', 'mlp_fc2_b', 'ada_w', 'ada_b')}
    del _L1_xattn_all

    def _L2_xattn_setup():
        import jax, jax.numpy as jnp
        import numpy as np
        D_MODEL = 128
        N_HEADS = 16
        D_K = D_MODEL // N_HEADS
        LN_EPS = 1e-05

        def _attention(query, key_value, W_qkv, b_qkv, W_o, b_o, ln_gamma, ln_beta):
            B, Sq, _ = query.shape
            Skv = key_value.shape[1]
            Wq, Wk, Wv = (W_qkv[:D_MODEL], W_qkv[D_MODEL:2 * D_MODEL], W_qkv[2 * D_MODEL:])
            bq, bk, bv = (b_qkv[:D_MODEL], b_qkv[D_MODEL:2 * D_MODEL], b_qkv[2 * D_MODEL:])
            Q = (query @ Wq.T + bq).reshape(B, Sq, N_HEADS, D_K).transpose(0, 2, 1, 3)
            K = (key_value @ Wk.T + bk).reshape(B, Skv, N_HEADS, D_K).transpose(0, 2, 1, 3)
            V = (key_value @ Wv.T + bv).reshape(B, Skv, N_HEADS, D_K).transpose(0, 2, 1, 3)
            scores = jnp.einsum('bhqd,bhkd->bhqk', Q.astype(jnp.float32), K.astype(jnp.float32))
            scores = scores / np.sqrt(D_K)
            attn = jax.nn.softmax(scores, axis=-1)
            context = jnp.einsum('bhqk,bhkd->bhqd', attn, V.astype(jnp.float32)).astype(query.dtype)
            context = context.transpose(0, 2, 1, 3).reshape(B, Sq, D_MODEL)
            output = context @ W_o.T + b_o
            x = output + query
            mu = jnp.mean(x, axis=-1, keepdims=True)
            var = jnp.mean(jnp.square(x - mu), axis=-1, keepdims=True)
            return (x - mu) / jnp.sqrt(var + LN_EPS) * ln_gamma + ln_beta
        key = jax.random.key(seed)
        ks = jax.random.split(key, 8)
        B, Sq, Skv = (2, 256, 256)
        scale = 1.0 / np.sqrt(D_MODEL)
        return {'query': jax.random.normal(ks[0], (B, Sq, D_MODEL), dtype=jnp.float32), 'key_value': jax.random.normal(ks[1], (B, Skv, D_MODEL), dtype=jnp.float32), 'W_qkv': jax.random.normal(ks[2], (3 * D_MODEL, D_MODEL), dtype=jnp.float32) * scale, 'b_qkv': jax.random.normal(ks[3], (3 * D_MODEL,), dtype=jnp.float32) * 0.01, 'W_o': jax.random.normal(ks[4], (D_MODEL, D_MODEL), dtype=jnp.float32) * scale, 'b_o': jax.random.normal(ks[5], (D_MODEL,), dtype=jnp.float32) * 0.01, 'ln_gamma': jnp.ones((D_MODEL,), dtype=jnp.float32), 'ln_beta': jnp.zeros((D_MODEL,), dtype=jnp.float32)}
    _L2_xattn_all = _L2_xattn_setup()
    _L2_xattn_in = {k: v for k, v in _L2_xattn_all.items() if k in ('W_qkv', 'b_qkv', 'W_o', 'b_o', 'ln_gamma', 'ln_beta')}
    del _L2_xattn_all

    def _L3_xattn_setup():
        import jax, jax.numpy as jnp
        import numpy as np
        D_MODEL = 128
        NUM_HEADS = 16
        HEAD_DIM = D_MODEL // NUM_HEADS
        SCALE = HEAD_DIM ** (-0.5)
        LN_EPS = 1e-05
        Q_EPS = 1e-05

        def bit_quant(W):
            gamma = jnp.mean(jnp.abs(W))
            Wq = jnp.clip(jnp.round(W / (gamma + Q_EPS)), -1.0, 1.0) * gamma
            return W + jax.lax.stop_gradient(Wq - W)

        def layer_norm(x, gamma, beta):
            mu = jnp.mean(x, axis=-1, keepdims=True)
            var = jnp.mean(jnp.square(x - mu), axis=-1, keepdims=True)
            return (x - mu) * jax.lax.rsqrt(var + LN_EPS) * gamma + beta
        key = jax.random.key(seed)
        ks = jax.random.split(key, 8)
        B, T, T_ctx, C = (4, 128, 256, D_MODEL)
        w_std = C ** (-0.5)
        return {'x': jax.random.normal(ks[0], (B, T, C), jnp.float32), 'context': jax.random.normal(ks[1], (B, T_ctx, C), jnp.float32), 'Wq': jax.random.normal(ks[2], (C, C), jnp.float32) * w_std, 'bq': jnp.zeros((C,), jnp.float32), 'Wk': jax.random.normal(ks[3], (C, C), jnp.float32) * w_std, 'bk': jnp.zeros((C,), jnp.float32), 'Wv': jax.random.normal(ks[4], (C, C), jnp.float32) * w_std, 'bv': jnp.zeros((C,), jnp.float32), 'Wo': jax.random.normal(ks[5], (C, C), jnp.float32) * w_std, 'bo': jnp.zeros((C,), jnp.float32), 'ln_gamma': jnp.ones((C,), jnp.float32), 'ln_beta': jnp.zeros((C,), jnp.float32)}
    _L3_xattn_all = _L3_xattn_setup()
    _L3_xattn_in = {k: v for k, v in _L3_xattn_all.items() if k in ('Wq', 'bq', 'Wk', 'bk', 'Wv', 'bv', 'Wo', 'bo', 'ln_gamma', 'ln_beta')}
    del _L3_xattn_all
    return {'x': x, 'ctx_1024': ctx_1024, 'pos_BxS2': pos_BxS2, 'L0_xattn_Wq': _L0_xattn_in['Wq'], 'L0_xattn_bq': _L0_xattn_in['bq'], 'L0_xattn_Wk': _L0_xattn_in['Wk'], 'L0_xattn_Wv': _L0_xattn_in['Wv'], 'L0_xattn_bv': _L0_xattn_in['bv'], 'L0_xattn_Wo': _L0_xattn_in['Wo'], 'L0_xattn_bo': _L0_xattn_in['bo'], 'L1_xattn_attn_qkv_w': _L1_xattn_in['attn_qkv_w'], 'L1_xattn_attn_qkv_b': _L1_xattn_in['attn_qkv_b'], 'L1_xattn_attn_proj_w': _L1_xattn_in['attn_proj_w'], 'L1_xattn_attn_proj_b': _L1_xattn_in['attn_proj_b'], 'L1_xattn_crs_qkv_w': _L1_xattn_in['crs_qkv_w'], 'L1_xattn_crs_qkv_b': _L1_xattn_in['crs_qkv_b'], 'L1_xattn_crs_proj_w': _L1_xattn_in['crs_proj_w'], 'L1_xattn_crs_proj_b': _L1_xattn_in['crs_proj_b'], 'L1_xattn_mlp_fc1_w': _L1_xattn_in['mlp_fc1_w'], 'L1_xattn_mlp_fc1_b': _L1_xattn_in['mlp_fc1_b'], 'L1_xattn_mlp_fc2_w': _L1_xattn_in['mlp_fc2_w'], 'L1_xattn_mlp_fc2_b': _L1_xattn_in['mlp_fc2_b'], 'L1_xattn_ada_w': _L1_xattn_in['ada_w'], 'L1_xattn_ada_b': _L1_xattn_in['ada_b'], 'L2_xattn_W_qkv': _L2_xattn_in['W_qkv'], 'L2_xattn_b_qkv': _L2_xattn_in['b_qkv'], 'L2_xattn_W_o': _L2_xattn_in['W_o'], 'L2_xattn_b_o': _L2_xattn_in['b_o'], 'L2_xattn_ln_gamma': _L2_xattn_in['ln_gamma'], 'L2_xattn_ln_beta': _L2_xattn_in['ln_beta'], 'L3_xattn_Wq': _L3_xattn_in['Wq'], 'L3_xattn_bq': _L3_xattn_in['bq'], 'L3_xattn_Wk': _L3_xattn_in['Wk'], 'L3_xattn_bk': _L3_xattn_in['bk'], 'L3_xattn_Wv': _L3_xattn_in['Wv'], 'L3_xattn_bv': _L3_xattn_in['bv'], 'L3_xattn_Wo': _L3_xattn_in['Wo'], 'L3_xattn_bo': _L3_xattn_in['bo'], 'L3_xattn_ln_gamma': _L3_xattn_in['ln_gamma'], 'L3_xattn_ln_beta': _L3_xattn_in['ln_beta']}

def reference(x, ctx_1024, pos_BxS2, L0_xattn_Wq, L0_xattn_bq, L0_xattn_Wk, L0_xattn_Wv, L0_xattn_bv, L0_xattn_Wo, L0_xattn_bo, L1_xattn_attn_qkv_w, L1_xattn_attn_qkv_b, L1_xattn_attn_proj_w, L1_xattn_attn_proj_b, L1_xattn_crs_qkv_w, L1_xattn_crs_qkv_b, L1_xattn_crs_proj_w, L1_xattn_crs_proj_b, L1_xattn_mlp_fc1_w, L1_xattn_mlp_fc1_b, L1_xattn_mlp_fc2_w, L1_xattn_mlp_fc2_b, L1_xattn_ada_w, L1_xattn_ada_b, L2_xattn_W_qkv, L2_xattn_b_qkv, L2_xattn_W_o, L2_xattn_b_o, L2_xattn_ln_gamma, L2_xattn_ln_beta, L3_xattn_Wq, L3_xattn_bq, L3_xattn_Wk, L3_xattn_bk, L3_xattn_Wv, L3_xattn_bv, L3_xattn_Wo, L3_xattn_bo, L3_xattn_ln_gamma, L3_xattn_ln_beta):
    import jax
    import jax.numpy as jnp

    def _L0_xattn_ref(query, key, query_pos, key_pos, Wq, bq, Wk, Wv, bv, Wo, bo):
        import jax, jax.numpy as jnp
        import numpy as np
        NUM_HEADS = 16
        ROPE_BASE = 10000.0
        MAX_POS = 512

        def _rope_tables(head_dim):
            inv_freq = 1.0 / ROPE_BASE ** (np.arange(0, head_dim, 2, dtype=np.float32) / head_dim)
            freqs = np.arange(MAX_POS, dtype=np.float32)[:, None] * inv_freq[None, :]
            emb = np.concatenate([freqs, freqs], axis=-1)
            return (jnp.asarray(np.cos(emb)), jnp.asarray(np.sin(emb)))

        def _rotate_half(x):
            d = x.shape[-1] // 2
            return jnp.concatenate([-x[..., d:], x[..., :d]], axis=-1)

        def _apply_rope(x, pos, cos_t, sin_t):
            cos = cos_t[pos][:, None]
            sin = sin_t[pos][:, None]
            return x * cos + _rotate_half(x) * sin
        B, N, C = query.shape
        M = key.shape[1]
        H = NUM_HEADS
        D = C // H
        scale = D ** (-0.5)
        cos_t, sin_t = _rope_tables(D)
        value = key
        identity = query
        q = (query @ Wq.T + bq).reshape(B, N, H, D).transpose(0, 2, 1, 3)
        k = (key @ Wk.T).reshape(B, M, H, D).transpose(0, 2, 1, 3)
        v = (value @ Wv.T + bv).reshape(B, M, H, D).transpose(0, 2, 1, 3)
        q = _apply_rope(q, query_pos, cos_t, sin_t)
        k = _apply_rope(k, key_pos, cos_t, sin_t)
        attn = jnp.einsum('bhnd,bhmd->bhnm', q, k) * scale
        attn = jax.nn.softmax(attn, axis=-1)
        x = jnp.einsum('bhnm,bhmd->bhnd', attn, v)
        x = x.transpose(0, 2, 1, 3).reshape(B, N, C)
        x = x @ Wo.T + bo
        return x + identity

    def _L1_xattn_ref(x, c, attn_qkv_w, attn_qkv_b, attn_proj_w, attn_proj_b, crs_qkv_w, crs_qkv_b, crs_proj_w, crs_proj_b, mlp_fc1_w, mlp_fc1_b, mlp_fc2_w, mlp_fc2_b, ada_w, ada_b):
        import jax, jax.numpy as jnp
        import numpy as np
        EPS = 1e-06
        H = 16

        def _ln(x):
            mu = jnp.mean(x, axis=-1, keepdims=True)
            var = jnp.mean(jnp.square(x - mu), axis=-1, keepdims=True)
            return (x - mu) / jnp.sqrt(var + EPS)

        def _mod(x, shift, scale):
            return x * (1.0 + scale[:, None, :]) + shift[:, None, :]

        def _heads(x, qkv_w, qkv_b):
            B, N, C = x.shape
            hd = C // H
            qkv = (x @ qkv_w + qkv_b).reshape(B, N, 3, H, hd).transpose(2, 0, 3, 1, 4)
            return (qkv[0], qkv[1], qkv[2])

        def _attend(q, k, v):
            sc = q.shape[-1] ** (-0.5)
            a = jax.nn.softmax(jnp.einsum('bhnd,bhmd->bhnm', q, k) * sc, axis=-1)
            o = jnp.einsum('bhnm,bhmd->bhnd', a, v)
            B, h, N, hd = o.shape
            return o.transpose(0, 2, 1, 3).reshape(B, N, h * hd)

        def _mha(x, qkv_w, qkv_b, proj_w, proj_b):
            q, k, v = _heads(x, qkv_w, qkv_b)
            return _attend(q, k, v) @ proj_w + proj_b
        mod = jax.nn.silu(c) @ ada_w + ada_b
        sh_msa, sc_msa, g_msa, sh_mca, sc_mca, g_mca, sh_mlp, sc_mlp, g_mlp = jnp.split(mod, 9, axis=2)
        B, T, D = x.shape
        h = T // 2
        x0, x1 = (x[:, :h], x[:, h:])
        x0 = x0 + g_msa[:, 0][:, None, :] * _mha(_mod(_ln(x0), sh_msa[:, 0], sc_msa[:, 0]), attn_qkv_w, attn_qkv_b, attn_proj_w, attn_proj_b)
        x1 = x1 + g_msa[:, 1][:, None, :] * _mha(_mod(_ln(x1), sh_msa[:, 1], sc_msa[:, 1]), attn_qkv_w, attn_qkv_b, attn_proj_w, attn_proj_b)
        xm = _mod(_ln(x0), sh_mca[:, 0], sc_mca[:, 0])
        ym = _mod(_ln(x1), sh_mca[:, 1], sc_mca[:, 1])
        qx, kx, vx = _heads(xm, crs_qkv_w, crs_qkv_b)
        qy, ky, vy = _heads(ym, crs_qkv_w, crs_qkv_b)
        ox = _attend(qx, ky, vy) @ crs_proj_w + crs_proj_b
        oy = _attend(qy, kx, vx) @ crs_proj_w + crs_proj_b
        x = x + jnp.concatenate((g_mca[:, 0][:, None, :] * ox, g_mca[:, 1][:, None, :] * oy), axis=1)

        def mlp(z):
            return jax.nn.gelu(z @ mlp_fc1_w + mlp_fc1_b, approximate=True) @ mlp_fc2_w + mlp_fc2_b
        m0 = mlp(_mod(_ln(x[:, :h]), sh_mlp[:, 0], sc_mlp[:, 0]))
        m1 = mlp(_mod(_ln(x[:, h:]), sh_mlp[:, 1], sc_mlp[:, 1]))
        x = x + jnp.concatenate((g_mlp[:, 0][:, None, :] * m0, g_mlp[:, 1][:, None, :] * m1), axis=1)
        return x

    def _L2_xattn_ref(query, key_value, W_qkv, b_qkv, W_o, b_o, ln_gamma, ln_beta):
        import jax, jax.numpy as jnp
        import numpy as np
        D_MODEL = 128
        N_HEADS = 16
        D_K = D_MODEL // N_HEADS
        LN_EPS = 1e-05

        def _attention(query, key_value, W_qkv, b_qkv, W_o, b_o, ln_gamma, ln_beta):
            B, Sq, _ = query.shape
            Skv = key_value.shape[1]
            Wq, Wk, Wv = (W_qkv[:D_MODEL], W_qkv[D_MODEL:2 * D_MODEL], W_qkv[2 * D_MODEL:])
            bq, bk, bv = (b_qkv[:D_MODEL], b_qkv[D_MODEL:2 * D_MODEL], b_qkv[2 * D_MODEL:])
            Q = (query @ Wq.T + bq).reshape(B, Sq, N_HEADS, D_K).transpose(0, 2, 1, 3)
            K = (key_value @ Wk.T + bk).reshape(B, Skv, N_HEADS, D_K).transpose(0, 2, 1, 3)
            V = (key_value @ Wv.T + bv).reshape(B, Skv, N_HEADS, D_K).transpose(0, 2, 1, 3)
            scores = jnp.einsum('bhqd,bhkd->bhqk', Q.astype(jnp.float32), K.astype(jnp.float32))
            scores = scores / np.sqrt(D_K)
            attn = jax.nn.softmax(scores, axis=-1)
            context = jnp.einsum('bhqk,bhkd->bhqd', attn, V.astype(jnp.float32)).astype(query.dtype)
            context = context.transpose(0, 2, 1, 3).reshape(B, Sq, D_MODEL)
            output = context @ W_o.T + b_o
            x = output + query
            mu = jnp.mean(x, axis=-1, keepdims=True)
            var = jnp.mean(jnp.square(x - mu), axis=-1, keepdims=True)
            return (x - mu) / jnp.sqrt(var + LN_EPS) * ln_gamma + ln_beta
        return _attention(query, key_value, W_qkv, b_qkv, W_o, b_o, ln_gamma, ln_beta)

    def _L3_xattn_ref(x, context, Wq, bq, Wk, bk, Wv, bv, Wo, bo, ln_gamma, ln_beta):
        import jax, jax.numpy as jnp
        import numpy as np
        D_MODEL = 128
        NUM_HEADS = 16
        HEAD_DIM = D_MODEL // NUM_HEADS
        SCALE = HEAD_DIM ** (-0.5)
        LN_EPS = 1e-05
        Q_EPS = 1e-05

        def bit_quant(W):
            gamma = jnp.mean(jnp.abs(W))
            Wq = jnp.clip(jnp.round(W / (gamma + Q_EPS)), -1.0, 1.0) * gamma
            return W + jax.lax.stop_gradient(Wq - W)

        def layer_norm(x, gamma, beta):
            mu = jnp.mean(x, axis=-1, keepdims=True)
            var = jnp.mean(jnp.square(x - mu), axis=-1, keepdims=True)
            return (x - mu) * jax.lax.rsqrt(var + LN_EPS) * gamma + beta
        B, T, C = x.shape
        T_ctx = context.shape[1]
        residual = x
        xn = layer_norm(x, ln_gamma, ln_beta)
        q = xn @ bit_quant(Wq).T + bq
        k = context @ bit_quant(Wk).T + bk
        v = context @ bit_quant(Wv).T + bv
        q = q.reshape(B, T, NUM_HEADS, HEAD_DIM)
        k = k.reshape(B, T_ctx, NUM_HEADS, HEAD_DIM)
        v = v.reshape(B, T_ctx, NUM_HEADS, HEAD_DIM)
        scores = jnp.einsum('bqhd,bkhd->bhqk', q, k) * SCALE
        probs = jax.nn.softmax(scores, axis=-1)
        out = jnp.einsum('bhqk,bkhd->bqhd', probs, v).reshape(B, T, C)
        return residual + (out @ bit_quant(Wo).T + bo)
    x = _L0_xattn_ref(x, ctx_1024, pos_BxS2, pos_BxS2, L0_xattn_Wq, L0_xattn_bq, L0_xattn_Wk, L0_xattn_Wv, L0_xattn_bv, L0_xattn_Wo, L0_xattn_bo)
    x = _L1_xattn_ref(x, ctx_1024, L1_xattn_attn_qkv_w, L1_xattn_attn_qkv_b, L1_xattn_attn_proj_w, L1_xattn_attn_proj_b, L1_xattn_crs_qkv_w, L1_xattn_crs_qkv_b, L1_xattn_crs_proj_w, L1_xattn_crs_proj_b, L1_xattn_mlp_fc1_w, L1_xattn_mlp_fc1_b, L1_xattn_mlp_fc2_w, L1_xattn_mlp_fc2_b, L1_xattn_ada_w, L1_xattn_ada_b)
    x = _L2_xattn_ref(x, ctx_1024, L2_xattn_W_qkv, L2_xattn_b_qkv, L2_xattn_W_o, L2_xattn_b_o, L2_xattn_ln_gamma, L2_xattn_ln_beta)
    x = _L3_xattn_ref(x, ctx_1024, L3_xattn_Wq, L3_xattn_bq, L3_xattn_Wk, L3_xattn_bk, L3_xattn_Wv, L3_xattn_bv, L3_xattn_Wo, L3_xattn_bo, L3_xattn_ln_gamma, L3_xattn_ln_beta)
    return x

_drawn_inputs = setup_inputs


def setup_inputs(seed=0):
    import zlib

    import numpy as np

    out = dict(_drawn_inputs(seed))
    spreads = {'L0_xattn_bq': (0.0, 0.521),
     'L0_xattn_bv': (0.0, 0.1),
     'L0_xattn_bo': (0.0, 0.1),
     'L1_xattn_attn_qkv_b': (0.0, 0.8),
     'L1_xattn_attn_proj_b': (0.0, 0.8),
     'L1_xattn_crs_qkv_b': (0.0, 0.8),
     'L1_xattn_crs_proj_b': (0.0, 0.673),
     'L1_xattn_mlp_fc1_b': (0.0, 0.8),
     'L1_xattn_mlp_fc2_b': (0.0, 0.605),
     'L1_xattn_ada_b': (0.0, 0.704),
     'L2_xattn_ln_gamma': (1.0, 0.2),
     'L2_xattn_ln_beta': (0.0, 0.1),
     'L3_xattn_bq': (0.0, 0.8),
     'L3_xattn_bk': (0.0, 2.0),
     'L3_xattn_bv': (0.0, 0.1),
     'L3_xattn_bo': (0.0, 0.1),
     'L3_xattn_ln_gamma': (1.0, 0.6),
     'L3_xattn_ln_beta': (0.0, 0.8)}
    factors = {'L1_xattn_attn_qkv_w': 8.0,
     'L1_xattn_attn_proj_w': 8.0,
     'L1_xattn_crs_qkv_w': 8.0,
     'L1_xattn_crs_proj_w': 8.0,
     'L1_xattn_mlp_fc1_w': 8.0,
     'L1_xattn_mlp_fc2_w': 7.199,
     'L1_xattn_ada_w': 3.766,
     'L2_xattn_b_qkv': 56.152,
     'L2_xattn_b_o': 40.314}
    for name, (base, spread) in spreads.items():
        noise = np.random.default_rng([zlib.crc32(name.encode()), seed]).standard_normal(out[name].shape)
        drawn = base * np.exp(spread * noise) if base else spread * noise
        out[name] = jnp.asarray(drawn.astype(out[name].dtype))
    for name, factor in factors.items():
        out[name] = (out[name] * factor).astype(out[name].dtype)
    return out
```

```python
from contextlib import ExitStack

import numpy as np

import concourse.bass as bass
import concourse.mybir as mybir

F32 = mybir.dt.float32
BF16 = mybir.dt.bfloat16
I32 = mybir.dt.int32
ALU = mybir.AluOpType
ACT = mybir.ActivationFunctionType
AX = mybir.AxisListType

B, T, D = 4, 256, 128
H, DH = 16, 8
P = 128
NT = T // P
PAIRS = H // 2
SCALE = float(DH) ** -0.5
PHASES = 5
UNITS = PHASES * B
MAX_POS = 512
POS_CHUNKS = MAX_POS // P
PARTS = 3
SLOTS = ((0, 2), (1, 1), (2, 0), (0, 1), (1, 0), (0, 0))
SLOT_ROWS = 2 * DH
MAX_ROW = SLOT_ROWS * len(SLOTS)
MAX_ROWS = 4
STACK_BUFS = 3
BANK = 512
CHUNK = 2 * BANK

W_NAMES = ["q0", "q0r", "k0", "k0r", "v0", "o0",
           "q1", "k1", "v1", "o1", "q2", "k2", "v2", "o2",
           "fc1a", "fc1b", "fc1c", "fc1d", "fc2a", "fc2b", "fc2c", "fc2d",
           "ada0", "ada1", "ada2", "ada3", "ada4", "ada5", "ada6", "ada7", "ada8",
           "q3", "k3", "v3", "o3", "q4", "k4", "v4", "o4"]
W_AT = {n: i for i, n in enumerate(W_NAMES)}
W_GROUPS = (("q0", "o0"), ("q1", "fc2d"), ("ada0", "ada8"), ("q3", "o4"))
V_NAMES = (["bq0", "bq0r", "bv0", "bq1", "bk1", "bv1", "bq2", "bk2", "bv2", "bq3", "bk3", "bv3",
            "bq4", "bk4", "bv4", "g4", "b4"] + [f"fc1_{i}" for i in range(4)] + [f"ada_{i}" for i in range(9)])
V_AT = {n: i for i, n in enumerate(V_NAMES)}
R_NAMES = ["bo0", "bo1", "bo2", "bfc2", "bo3", "g3", "b3", "bo4", "gate1", "gate2", "gate3"]
R_AT = {n: i for i, n in enumerate(R_NAMES)}
C_IDENT, C_IOTA, C_ROPE = 0, P, P + POS_CHUNKS
C_COLS = C_ROPE + POS_CHUNKS * 2 * D


def halves(phase):
    return phase in (1, 2)


def n_banks(u):
    return PAIRS if halves(u // B) else 2 * PAIRS


def n_chunks(u):
    return PAIRS // 2 if halves(u // B) else PAIRS


def finish_steps(u):
    phase = u // B
    steps = ["unstack", "heads_t", "out_proj"]
    if phase < 4:
        steps.append("norm_t")
    if phase == 2:
        steps += ["fc1_lo", "fc1_hi", "fc2", "x_t"]
    return steps


def make_schedule():
    s = []

    def small(*steps):
        for kind, u in steps:
            if 0 <= u < UNITS or kind in ("mod", "gate", "gamma", "rope"):
                s.append(("small", kind, u))

    def banks(u, lo, hi):
        if u < UNITS:
            n = n_banks(u)
            s.extend(("max", u, i) for i in range(int(lo * n), int(hi * n)))

    small(("rope", 0), ("q", 0), ("k", 0), ("v", 0), ("rope", 1), ("q", 1), ("k", 1), ("v", 1))
    banks(0, 0, 1)
    small(("max_t", 0))
    banks(1, 0, .25)
    setup = [("mod", 0)] + [("gate", i) for i in range(2 * B)] + [("gamma", 0)]
    for u in range(UNITS + 1):
        n = n_chunks(u) if u < UNITS else 4
        at = {}
        fin = [(k, u - 1) for k in finish_steps(u - 1)] if u >= 1 else []
        prep = [("q", u + 2), ("k", u + 2), ("v", u + 2)] if u + 2 < UNITS else []
        late = []
        if u >= 2 and (u - 2) // B == 2:
            late = [(k, u - 2) for k in finish_steps(u - 2)[4:]]
            if u == UNITS:
                late = []
        if u >= 1 and (u - 1) // B == 2:
            fin = fin[:4]
        if u == 0:
            prep = [("rope", 2)] + prep
        if u == 1:
            prep = [("rope", 3)] + prep
        if n == 8:
            if late:
                order = {0: late[:2], 1: late[2:3] + fin[:1], 2: late[3:], 3: fin[1:2] + prep[:1],
                         4: prep[1:2] + fin[2:3], 5: prep[2:], 6: fin[3:]}
            else:
                order = {0: prep[:-1], 1: prep[-1:] + fin[:1], 2: fin[1:2], 3: fin[2:3], 5: fin[3:4]}
            at[6] = [("max_t", u + 1)] + order.pop(6, [])
            at.update(order)
        else:
            if late:
                at = {0: late[:2] + fin[:1], 1: late[2:] + fin[1:2], 2: prep + fin[2:3],
                      3: [("max_t", u + 1)] + fin[3:]}
            else:
                at = {0: prep[:2] + fin[:1], 1: prep[2:] + fin[1:2], 2: fin[2:3] + [("max_t", u + 1)], 3: fin[3:]}
        if u < B and setup:
            for c in range(1, 8):
                if setup and c % 2 == 0:
                    at.setdefault(c, [])
                    at[c] = at[c] + [setup.pop(0)]
        for c in range(n):
            if u < UNITS:
                s.append(("score", u, c))
            if c < n - 2:
                banks(u + 1, .25 + .75 * c / (n - 2), .25 + .75 * (c + .5) / (n - 2))
            if c == 0 and u >= 1:
                s.append(("value", u - 1, 3))
            elif u < UNITS and c >= 1:
                if n == 8 and c % 2 == 0:
                    s.append(("value", u, c // 2 - 1))
                if n == 4:
                    s.append(("value", u, c - 1))
            small(*at.get(c, []))
            if c < n - 2:
                banks(u + 1, .25 + .75 * (c + .5) / (n - 2), .25 + .75 * (c + 1) / (n - 2))
            else:
                banks(u + 2, (c - n + 2) * .125, (c - n + 3) * .125)
    return s


def build(nc, a):
    steps = make_schedule()
    order = {}
    seen = {}
    for st in steps:
        assert st not in order, st
        order[st] = seen.get(st[0], 0)
        seen[st[0]] = order[st] + 1

    def no(*step):
        return order[step]

    with ExitStack() as ctx:
        def sb(name, shape, dt=F32):
            return ctx.enter_context(nc.sbuf_tensor(name, shape, dt))

        def sem(name):
            return ctx.enter_context(nc.semaphore(name))

        w = sb("w", [P, len(W_NAMES), D])
        vec = sb("vec", [P, len(V_NAMES)])
        rows = sb("rows", [P, len(R_NAMES), D])
        const = sb("const", [P, C_COLS])
        ident = const[:, C_IDENT:C_IDENT + P]
        ident16 = sb("ident16", [P, P], BF16)
        mean_mat = sb("mean_mat", [P, P])
        pos_f = sb("pos_f", [P, B * T])
        onehot = sb("onehot", [P, 2, POS_CHUNKS, T], BF16)
        rope_parts = sb("rope_parts", [P, PARTS, POS_CHUNKS * 2 * D], BF16)
        rope_cs = sb("rope_cs", [P, B, 2 * T])
        x = sb("x", [P, B, NT, D])
        src_t = sb("src_t", [P, B, T])
        ctx_t = sb("ctx_t", [P, B, T])
        silu = sb("silu", [P, 4, 2 * B])
        silu_rep = sb("silu_rep", [P, 2 * B, P])
        mods = sb("mods", [P, 6, 2 * B])
        gates = sb("gates", [P, 2 * B, 3, D])
        gate_bias = sb("gate_bias", [P, 3, 2 * B, D])
        quant = sb("quant", [P, 4, D])
        quant2 = sb("quant2", [P, 4, D])
        quant_s = sb("quant_s", [P, 3, 4])
        q_f = sb("q_f", [P, 2, 2, T])
        rope_a = sb("rope_a", [P, T])
        rope_b = sb("rope_b", [P, T])
        split_r = sb("split_r", [P, 2, T])
        q_parts = sb("q_parts", [P, 2, PARTS, T], BF16)
        k_parts = sb("k_parts", [P, 2, PARTS, 2, T], BF16)
        q_stack = sb("q_stack", [P, STACK_BUFS, PAIRS, T], BF16)
        k_stack = sb("k_stack", [P, STACK_BUFS, H, T], BF16)
        v_cols = sb("v_cols", [P, STACK_BUFS, NT, H, 32])
        zero_rows = sb("zero_rows", [MAX_ROWS, PAIRS * T], BF16)
        neg_max = sb("neg_max", [P, 2, NT, 2, PAIRS])
        max_parts = sb("max_parts", [P, 2, NT, 2, 2, PAIRS], BF16)
        max_rows = sb("max_rows", [32, 2, T], BF16)
        probs = sb("probs", [P, 4, CHUNK])
        pos_i = probs[:, 0, :].bitcast(I32)
        pos_neg = probs[:, 1, :]
        rope_rest = probs[:, 2, :]
        heads_raw = sb("heads_raw", [P, BANK])
        inv_sum = sb("inv_sum", [P, 2 * H])
        heads = sb("heads", [P, NT, D])
        heads_t = sb("heads_t", [P, T])
        base = sb("base", [P, 2, NT, D])
        base_mlp = sb("base_mlp", [P, 2, NT, D])
        gated = sb("gated", [P, NT, D])
        stats = sb("stats", [P, NT, 6])
        mean_var = sb("mean_var", [P, NT, 2])
        var_eps = sb("var_eps", [P, NT])
        minus_half = sb("minus_half", [P, NT])
        rstd = sb("rstd", [P, NT])
        normed = sb("normed", [P, NT, D])
        hidden = sb("hidden", [P, 4, T])

        ps_max = [ctx.enter_context(nc.psum_tensor(f"ps_max{i}", [P, BANK], F32)) for i in range(2)]
        ps_score = [ctx.enter_context(nc.psum_tensor(f"ps_score{i}", [P, CHUNK], F32)) for i in range(2)]
        ps_heads = ctx.enter_context(nc.psum_tensor("ps_heads", [P, BANK], F32))
        ps_small = ctx.enter_context(nc.psum_tensor("ps_small", [P, BANK], F32))
        ps_small16 = ps_small[:, :].bitcast(BF16)

        const_loaded = sem("const_loaded")
        w_loaded = [sem(f"w_loaded{i}") for i in range(len(W_GROUPS))]
        ctx_loaded = sem("ctx_loaded")
        src_loaded = sem("src_loaded")
        x_loaded = sem("x_loaded")
        rows_loaded = sem("rows_loaded")
        pos_loaded = sem("pos_loaded")
        q_placed = [sem(f"q_placed{i}") for i in range(STACK_BUFS)]
        k_placed = [sem(f"k_placed{i}") for i in range(STACK_BUFS)]
        max_placed = [sem(f"max_placed{i}") for i in range(STACK_BUFS)]
        out_stored = sem("out_stored")
        cleared = sem("cleared")
        v_cleared = sem("v_cleared")
        stack_cleared = sem("stack_cleared")
        dve_const = sem("dve_const")
        rope_split = sem("rope_split")
        onehot_ready = sem("onehot_ready")
        silu_exp = sem("silu_exp")
        silu_ready = sem("silu_ready")
        quant_abs = sem("quant_abs")
        quant_ready = sem("quant_ready")
        gate_bias_ready = sem("gate_bias_ready")
        small_ready = sem("small_ready")
        small_used = sem("small_used")
        max_scored = sem("max_scored")
        max_taken = sem("max_taken")
        max_split = sem("max_split")
        scored = sem("scored")
        exped = sem("exped")
        valued = sem("valued")
        heads_copied = sem("heads_copied")
        roped = sem("roped")
        q_split = sem("q_split")
        k_split = sem("k_split")
        base_ready = sem("base_ready")
        base_mlp_ready = sem("base_mlp_ready")
        x_updated = sem("x_updated")
        mlp_added = sem("mlp_added")
        var_ready = sem("var_ready")
        rstd_ready = sem("rstd_ready")
        norm_ready = sem("norm_ready")
        dve_chain = sem("dve_chain")
        pool_chain = sem("pool_chain")

        block = ctx.enter_context(nc.Block())

        def W(name, n=1):
            return w[:, W_AT[name]:W_AT[name] + n, :].rearrange("p a b -> p (a b)")

        def V(name):
            return vec[:, V_AT[name]:V_AT[name] + 1]

        def row2(name):
            return rows[:, R_AT[name]:R_AT[name] + 1, :].broadcast_to([P, NT, D])

        def chunks_until(u):
            return sum(n_chunks(v) for v in range(u + 1))

        def banks_until(u):
            return no("max", u, n_banks(u) - 1) + 1

        def group_of_chunk(n):
            u = 0
            while n >= n_chunks(u):
                n -= n_chunks(u)
                u += 1
            return 4 * u + (n // 2 if n_chunks(u) == 8 else n)

        def until(seq, u):
            return seq[u % STACK_BUFS], u // STACK_BUFS + 1

        def kv_source(u):
            return src_t if halves(u // B) else ctx_t

        def keys_tile(phase, s):
            return s if phase == 1 else 1 - s

        def new_x(u):
            if u // B in (0, 4):
                return small_used, no("small", "out_proj", u) + 1
            return x_updated, u - B + 1

        @block.sync
        def _(sp):
            def load_w(g):
                lo, hi = W_AT[W_GROUPS[g][0]], W_AT[W_GROUPS[g][1]] + 1
                sp.dma_start(w[:, lo:hi, :], a["w"][:, lo * D:hi * D].rearrange("p (a b) -> p a b", b=D)
                             ).then_inc(w_loaded[g], 16)

            sp.dma_start(const[:, :], a["const"]).then_inc(const_loaded, 16)
            load_w(0)
            sp.dma_start(src_t[:, :, :], a["x_t"].rearrange("b c t -> c b t")).then_inc(src_loaded, 16)
            sp.dma_start(x[:, :, :, :].rearrange("p b n c -> p (b n) c"),
                         a["x"].rearrange("b (n p) c -> p (b n) c", p=P)).then_inc(x_loaded, 16)
            load_w(2)
            load_w(1)
            load_w(3)
            sp.wait_ge(cleared, 2)
            sp.wait_ge(stack_cleared, STACK_BUFS)
            for st in steps:
                if st[0] == "small" and st[1] in ("q", "k"):
                    _, kind, u = st
                    buf = u % STACK_BUFS
                    if u >= STACK_BUFS:
                        sp.wait_ge(scored, chunks_until(u - STACK_BUFS))
                    sp.wait_ge(q_split if kind == "q" else k_split, u + 1)
                    for slot, (q_part, k_part) in enumerate(SLOTS):
                        r = SLOT_ROWS * slot
                        if kind == "q":
                            sp.dma_start(q_stack[r:r + SLOT_ROWS, buf, :, :], q_parts[:, u % 2, q_part, :]
                                         ).then_inc(q_placed[buf], 16)
                        else:
                            sp.dma_start(k_stack[r:r + SLOT_ROWS, buf, :, :].rearrange("p h t -> p (h t)"),
                                         k_parts[:, u % 2, k_part, :, :].rearrange("p a t -> p (a t)")
                                         ).then_inc(k_placed[buf], 16)
                    if kind == "q":
                        sp.dma_start(q_stack[MAX_ROW:MAX_ROW + MAX_ROWS, buf, :, :].rearrange("p e t -> p (e t)"),
                                     zero_rows[:, :]).then_inc(q_placed[buf], 16)
                if st[0] == "small" and st[1] == "max_t":
                    u = st[2]
                    sp.wait_ge(small_used, no(*st) + 1)
                    sp.dma_start(q_stack[MAX_ROW:MAX_ROW + MAX_ROWS, u % STACK_BUFS, :, :], max_rows[:, u % 2, :]
                                 ).then_inc(max_placed[u % STACK_BUFS], 16)
                if st[0] == "small" and st[1] == "out_proj" and st[2] // B == PHASES - 1:
                    b = st[2] % B
                    sp.wait_ge(small_used, no(*st) + 1)
                    sp.dma_start(a["out"][b].rearrange("(n p) c -> p n c", p=P), x[:, b, :, :]
                                 ).then_inc(out_stored, 16)
            sp.wait_ge(out_stored, 16 * B)

        @block.gpsimd
        def _(pool):
            chain = [0]
            norms = 0

            def link(ins):
                chain[0] += 1
                ins.then_inc(pool_chain, 1)
                pool.wait_ge(pool_chain, chain[0])

            link(nc.gpsimd.memset(minus_half[:, :], -0.5))
            nc.gpsimd.memset(zero_rows[:, :], 0.0).then_inc(cleared, 1)
            nc.gpsimd.memset(k_parts[:, :, :, :, :].rearrange("p b j a t -> p (b j a t)"), 0.0).then_inc(cleared, 1)
            pool.wait_ge(cleared, 2)
            for buf in range(STACK_BUFS):
                flat = v_cols[:, buf, :, :, :].rearrange("p n h c -> p (n h c)")
                link(nc.gpsimd.memset(flat, 0.0))
                for i in range(2):
                    v = v_cols[:, buf, :, :, :].rearrange("p n (g r) c -> p (n g) r c", g=2)[:, :, 4 * i:4 * i + 4, 16 * i + 8:16 * i + 16]
                    last = nc.gpsimd.memset(v, 1.0)
                last.then_inc(v_cleared, 1)

            for st in steps:
                if st[0] == "small" and st[1] in ("q", "k"):
                    _, kind, u = st
                    which = 0 if kind == "q" else 1
                    if u // B:
                        pool.wait_ge(small_used, no(*st) + 1)
                    else:
                        pool.wait_ge(roped, 2 * u + which + 1)
                    if u >= 2:
                        s_, n_ = until(q_placed if kind == "q" else k_placed, u - 2)
                        pool.wait_ge(s_, 16 * (len(SLOTS) + (kind == "q")) * n_)
                    full = q_f[:, u % 2, which, :]
                    for par in ((None,) if kind == "q" else (0, 1)):
                        half = slice(0, P) if par is None else slice(par * 64, par * 64 + 64)
                        part = [q_parts[:, u % 2, j, :] if par is None else k_parts[half, u % 2, j, par, :]
                                for j in range(PARTS)]
                        rest = split_r[half, which, :]
                        link(nc.gpsimd.tensor_copy(part[0], full[half, :]))
                        link(nc.gpsimd.tensor_tensor(rest, full[half, :], part[0], ALU.subtract))
                        link(nc.gpsimd.tensor_copy(part[1], rest))
                        last = nc.gpsimd.tensor_tensor(part[2], rest, part[1], ALU.subtract)
                        if par == 0:
                            link(last)
                    last.then_inc(q_split if kind == "q" else k_split, 1)
                    if kind == "k":
                        pool.wait_ge(k_split, u + 1)
                if st[0] == "score" and st[2] == 0:
                    u = st[1]
                    phase, b = divmod(u, B)
                    if phase == 0 and b == 0:
                        pool.wait_ge(x_loaded, 16)
                        pool.wait_ge(rows_loaded, 16)
                    if phase:
                        pool.wait_ge(*new_x(u - B))
                    if phase == 3:
                        pool.wait_ge(mlp_added, b + 1)
                    if u >= 2:
                        pool.wait_ge(*new_x(u - 2))
                    if phase in (1, 2):
                        if u == B:
                            pool.wait_ge(small_used, no("small", "gate", 2 * B - 1) + 1)
                            for g in range(3):
                                bias = rows[:, R_AT[("bo1", "bo2", "bfc2")[g]], :].unsqueeze(1).broadcast_to([P, 2 * B, D])
                                link(nc.gpsimd.tensor_tensor(gate_bias[:, g, :, :], gates[:, :, g, :], bias, ALU.mult))
                        add = gate_bias[:, phase - 1, 2 * b:2 * b + 2, :]
                    else:
                        add = row2({0: "bo0", 3: "bo3", 4: "bo4"}[phase])
                    nc.gpsimd.tensor_tensor(base[:, u % 2, :, :], x[:, b, :, :], add, ALU.add).then_inc(base_ready, 1)
                if st[0] == "small" and st[1] == "out_proj" and st[2] // B < 4:
                    for _ in range(2 if st[2] // B == 3 else 1):
                        pool.wait_ge(var_ready, norms + 1)
                        nc.gpsimd.tensor_tensor(rstd[:, :], var_eps[:, :], minus_half[:, :], ALU.pow
                                                ).then_inc(rstd_ready, 1)
                        norms += 1
                if st[0] == "small" and st[1] == "norm_t" and st[2] // B == 2:
                    u = st[2]
                    b = u % B
                    pool.wait_ge(*new_x(u))
                    if b >= 2:
                        pool.wait_ge(mlp_added, b - 1)
                    nc.gpsimd.tensor_tensor(base_mlp[:, b % 2, :, :], x[:, b, :, :], gate_bias[:, 2, 2 * b:2 * b + 2, :],
                                            ALU.add).then_inc(base_mlp_ready, 1)

        @block.tensor
        def _(pe):
            def mm(out, lhs_t, rhs, start=True, stop=True, **k):
                return nc.tensor.matmul(out, lhs_t, rhs, start=start, stop=stop, **k)

            pe.wait_ge(const_loaded, 16)
            for st in steps:
                if st[0] == "max":
                    _, u, i = st
                    n = no(*st)
                    phase = u // B
                    buf = u % STACK_BUFS
                    if i == 0:
                        s_, n_ = until(q_placed, u)
                        pe.wait_ge(s_, 16 * (len(SLOTS) + 1) * n_)
                        s_, n_ = until(k_placed, u)
                        pe.wait_ge(s_, 16 * len(SLOTS) * n_)
                    if n >= 2:
                        pe.wait_ge(max_taken, n - 1)
                    out = ps_max[n % 2]
                    if halves(phase):
                        for s in range(NT):
                            kt = keys_tile(phase, s)
                            last = mm(out[:, s * 2 * P:(s + 1) * 2 * P].rearrange("p (a b) -> p a b", a=2),
                                      q_stack[:, buf, i, s * P:(s + 1) * P],
                                      k_stack[:, buf, 2 * i:2 * i + 2, kt * P:(kt + 1) * P])
                    else:
                        pair, qt = divmod(i, NT)
                        last = mm(out[:, :], q_stack[:, buf, pair, qt * P:(qt + 1) * P],
                                  k_stack[:, buf, 2 * pair:2 * pair + 2, :].rearrange("p a b -> p (a b)"))
                    last.then_inc(max_scored, 1)
                elif st[0] == "score":
                    _, u, c = st
                    n = no(*st)
                    phase = u // B
                    buf = u % STACK_BUFS
                    if c == 0:
                        s_, n_ = until(max_placed, u)
                        pe.wait_ge(s_, 16 * n_)
                    if n >= 2:
                        pe.wait_ge(exped, n - 1)
                    out = ps_score[n % 2]
                    if halves(phase):
                        for hl in range(4):
                            for s in range(NT):
                                h = 4 * c + hl
                                kt = keys_tile(phase, s)
                                col = (hl * NT + s) * P
                                last = mm(out[:, col:col + P], k_stack[:, buf, h, kt * P:(kt + 1) * P],
                                          q_stack[:, buf, h // 2, s * P:(s + 1) * P])
                    else:
                        for hl in range(2):
                            for kt in range(NT):
                                col = (hl * NT + kt) * T
                                last = mm(out[:, col:col + T], k_stack[:, buf, 2 * c + hl, kt * P:(kt + 1) * P],
                                          q_stack[:, buf, c, :])
                    last.then_inc(scored, 1)
                elif st[0] == "value":
                    _, u, k = st
                    phase = u // B
                    g, i = divmod(k, 2)
                    first = chunks_until(u) - n_chunks(u)
                    buf = u % STACK_BUFS
                    if k == 0:
                        pe.wait_ge(small_used, no("small", "v", u) + 1)
                        if u:
                            pe.wait_ge(heads_copied, u)
                    if halves(phase):
                        pe.wait_ge(exped, first + k + 1)
                        pr = probs[:, (first + k) % 4, :]
                        for s in range(NT):
                            for j in range(4):
                                h = 4 * k + j
                                col = (j * NT + s) * P
                                last = mm(ps_heads[32 * j:32 * j + 32, g * T + s * P:g * T + (s + 1) * P],
                                          v_cols[:, buf, keys_tile(phase, s), h, :], pr[:, col:col + P],
                                          start=(i == 0 and s == 0), stop=(i == 1 and s == 1),
                                          skip_group_check=True, tile_position=(0, 32 * j))
                    else:
                        pe.wait_ge(exped, first + 2 * k + 2)
                        for kt in range(NT):
                            for j in range(4):
                                h = 4 * k + j
                                pr = probs[:, (first + 2 * k + j // 2) % 4, :]
                                col = ((j % 2) * NT + kt) * T
                                last = mm(ps_heads[32 * j:32 * j + 32, g * T:(g + 1) * T],
                                          v_cols[:, buf, kt, h, :], pr[:, col:col + T],
                                          start=(i == 0 and kt == 0), stop=(i == 1 and kt == 1),
                                          skip_group_check=True, tile_position=(0, 32 * j))
                    last.then_inc(valued, 1)
                else:
                    _, kind, u = st
                    n = no(*st)
                    phase, b = divmod(u, B)
                    if n:
                        pe.wait_ge(small_used, n)
                    out = ps_small
                    if kind == "rope":
                        pe.wait_ge(rope_split, 1)
                        pe.wait_ge(onehot_ready, u + 1)
                        tab = rope_parts[:, :, :].rearrange("p j (c f r) -> p j c f r", c=POS_CHUNKS, f=2)
                        for f in range(2):
                            for c in range(POS_CHUNKS):
                                for j in range(PARTS):
                                    last = mm(out[:, f * T:(f + 1) * T], tab[:, j, c, f, :], onehot[:, u % 2, c, :],
                                              start=(c == 0 and j == 0), stop=(c == POS_CHUNKS - 1 and j == PARTS - 1))
                    elif kind == "mod":
                        pe.wait_ge(w_loaded[2], 16)
                        pe.wait_ge(silu_ready, 2)
                        for i, k in enumerate((0, 1, 3, 4, 6, 7)):
                            last = mm(out[:, 2 * B * i:2 * B * (i + 1)], W(f"ada{k}"), silu[:, 3, :])
                    elif kind == "gate":
                        last = mm(out[:, 0:3 * D].rearrange("p (a b) -> p a b", a=3), silu_rep[:, u, :],
                                  w[:, W_AT["ada2"]:W_AT["ada8"] + 1:3, :])
                    elif kind == "gamma":
                        pe.wait_ge(quant_abs, 1)
                        pe.wait_ge(dve_const, 2)
                        last = mm(out[:, 0:4], mean_mat[:, :], quant_s[:, 0, :])
                    elif kind in ("q", "k"):
                        if u == 0 and kind == "q":
                            pe.wait_ge(w_loaded[0], 16)
                            pe.wait_ge(src_loaded, 16)
                        if u == 0 and kind == "k":
                            pe.wait_ge(ctx_loaded, 16)
                        if u == B and kind == "q":
                            pe.wait_ge(w_loaded[1], 16)
                        if u == 3 * B and kind == "q":
                            pe.wait_ge(w_loaded[3], 16)
                        if u == 4 * B and kind == "q":
                            pe.wait_ge(quant_ready, 1)
                        src = (src_t if kind == "q" else kv_source(u))[:, b, :]
                        last = mm(out[:, 0:T], W(f"{kind}{phase}"), src)
                        if phase == 0:
                            last = mm(out[:, T:2 * T], W(f"{kind}0r"), src)
                    elif kind == "v":
                        for kt in range(NT):
                            last = mm(out[:, kt * D:(kt + 1) * D], kv_source(u)[:, b, kt * P:(kt + 1) * P], W(f"v{phase}"))
                    elif kind == "max_t":
                        pe.wait_ge(max_split, u + 1)
                        pe.wait_ge(dve_const, 1)
                        for qt in range(NT):
                            last = nc.tensor.transpose(ps_small16[0:32, qt * P:(qt + 1) * P],
                                                       max_parts[:, u % 2, qt, :, :, :].rearrange("p a j e -> p (a j e)"),
                                                       ident16[:, :])
                    elif kind == "unstack":
                        pe.wait_ge(heads_copied, u + 1)
                        for qt in range(NT):
                            for g in range(2):
                                last = nc.tensor.transpose(out[:, (qt * 2 + g) * P:(qt * 2 + g + 1) * P],
                                                           heads_raw[:, g * T + qt * P:g * T + (qt + 1) * P], ident)
                    elif kind == "heads_t":
                        for qt in range(NT):
                            last = nc.tensor.transpose(out[:, qt * P:(qt + 1) * P], heads[:, qt, :], ident)
                    elif kind == "out_proj":
                        for qt in range(NT):
                            last = mm(out[:, qt * D:(qt + 1) * D], heads_t[:, qt * P:(qt + 1) * P], W(f"o{phase}"))
                    elif kind == "norm_t":
                        pe.wait_ge(norm_ready, u + 1)
                        for qt in range(NT):
                            last = nc.tensor.transpose(out[:, qt * P:(qt + 1) * P], normed[:, qt, :], ident)
                    elif kind in ("fc1_lo", "fc1_hi"):
                        for j in range(2):
                            f = 2 * (kind == "fc1_hi") + j
                            last = mm(out[:, j * T:(j + 1) * T], W(f"fc1{'abcd'[f]}"), src_t[:, b, :])
                    elif kind == "fc2":
                        for qt in range(NT):
                            for f in range(4):
                                last = mm(out[:, qt * D:(qt + 1) * D], hidden[:, f, qt * P:(qt + 1) * P],
                                          W(f"fc2{'abcd'[f]}"), start=(f == 0), stop=(f == 3))
                    elif kind == "x_t":
                        pe.wait_ge(mlp_added, b + 1)
                        for qt in range(NT):
                            last = nc.tensor.transpose(out[:, qt * P:(qt + 1) * P], x[:, b, qt, :], ident)
                    last.then_inc(small_ready, 1)

        @block.scalar
        def _(act):
            act.dma_start(vec[:, :], a["vec"]).then_inc(rows_loaded, 16)
            act.dma_start(pos_i, a["pos"].rearrange("b t -> (b t)").partition_broadcast(P)).then_inc(pos_loaded, 16)
            act.dma_start(ctx_t[:, :, :], a["ctx_t"].rearrange("b c t -> c b t")).then_inc(ctx_loaded, 16)
            act.dma_start(rows[:, :, :].rearrange("p r c -> p (r c)"), a["rows"].partition_broadcast(P)
                          ).then_inc(rows_loaded, 16)
            act.wait_ge(ctx_loaded, 16)
            nc.scalar.activation(silu[:, 0, :].rearrange("p (b s) -> p b s", b=B), ctx_t[:, :, 0:2], ACT.Exp,
                                 scale=-1.0).then_inc(silu_exp, 1)
            act.wait_ge(rows_loaded, 32)
            for st in steps:
                if st[0] == "score":
                    _, u, c = st
                    n = no(*st)
                    act.wait_ge(scored, n + 1)
                    if n >= 4:
                        act.wait_ge(valued, group_of_chunk(n - 4) + 1)
                    nc.scalar.activation(probs[:, n % 4, :], ps_score[n % 2][:, :], ACT.Exp, scale=SCALE
                                         ).then_inc(exped, 1)
                elif st[0] == "value" and st[2] == 3:
                    u = st[1]
                    act.wait_ge(valued, 4 * u + 4)
                    if u:
                        act.wait_ge(small_ready, no("small", "unstack", u - 1) + 1)
                    nc.scalar.activation(heads_raw[:, :], ps_heads[:, :], ACT.Copy).then_inc(heads_copied, 1)
                elif st[0] == "small":
                    _, kind, u = st
                    n = no(*st)
                    phase, b = divmod(u, B)
                    if kind == "rope":
                        act.wait_ge(small_ready, n + 1)
                        nc.scalar.activation(rope_cs[:, u, :], ps_small[:, :], ACT.Copy).then_inc(small_used, 1)
                    elif kind in ("q", "k") and phase:
                        act.wait_ge(small_ready, n + 1)
                        act.wait_ge(q_split if kind == "q" else k_split, u - 1)
                        nc.scalar.activation(q_f[:, u % 2, 0 if kind == "q" else 1, :], ps_small[:, 0:T], ACT.Identity,
                                             bias=V(f"b{kind}{phase}")).then_inc(small_used, 1)
                    elif kind == "v":
                        act.wait_ge(small_ready, n + 1)
                        if u < STACK_BUFS:
                            act.wait_ge(v_cleared, u + 1)
                        else:
                            act.wait_ge(valued, 4 * (u - STACK_BUFS) + 4)
                        dst = v_cols[:, u % STACK_BUFS, :, :, :].rearrange("p n (g r) c -> p (n g) r c", g=2)
                        src = ps_small[:, 0:NT * D].rearrange("p (m r c) -> p m r c", m=2 * NT, c=DH)
                        for i in range(2):
                            last = nc.scalar.activation(dst[:, :, 4 * i:4 * i + 4, 16 * i:16 * i + 8],
                                                        src[:, :, 4 * i:4 * i + 4, :], ACT.Copy)
                        last.then_inc(small_used, 1)
                    elif kind == "heads_t":
                        act.wait_ge(small_ready, n + 1)
                        nc.scalar.activation(heads_t[:, :], ps_small[:, 0:T], ACT.Identity, bias=V(f"bv{phase}")
                                             ).then_inc(small_used, 1)
                    elif kind == "norm_t":
                        act.wait_ge(small_ready, n + 1)
                        if phase == 3:
                            nc.scalar.activation(src_t[:, b, :], ps_small[:, 0:T], ACT.Identity, bias=V("b4"),
                                                 scale=V("g4")).then_inc(small_used, 1)
                        else:
                            for s in range(NT):
                                last = nc.scalar.activation(src_t[:, b, s * P:(s + 1) * P], ps_small[:, s * P:(s + 1) * P],
                                                            ACT.Identity,
                                                            bias=mods[:, 2 * phase, 2 * b + s:2 * b + s + 1],
                                                            scale=mods[:, 2 * phase + 1, 2 * b + s:2 * b + s + 1])
                            last.then_inc(small_used, 1)
                    elif kind in ("fc1_lo", "fc1_hi"):
                        act.wait_ge(small_ready, n + 1)
                        for j in range(2):
                            f = 2 * (kind == "fc1_hi") + j
                            last = nc.scalar.activation(hidden[:, f, :], ps_small[:, j * T:(j + 1) * T],
                                                        ACT.Gelu_apprx_tanh, bias=V(f"fc1_{f}"))
                        last.then_inc(small_used, 1)
                    elif kind == "x_t":
                        act.wait_ge(small_ready, n + 1)
                        nc.scalar.activation(src_t[:, b, :], ps_small[:, 0:T], ACT.Copy).then_inc(small_used, 1)

        @block.vector
        def _(dve):
            chain = [0]

            def link(ins):
                chain[0] += 1
                ins.then_inc(dve_chain, 1)
                dve.wait_ge(dve_chain, chain[0])

            def place_onehot(b):
                pf = pos_f[:, b * T:(b + 1) * T]
                for c in range(POS_CHUNKS):
                    last = nc.vector.tensor_scalar(onehot[:, b % 2, c, :], pf, const[:, C_IOTA + c:C_IOTA + c + 1],
                                                   None, ALU.is_equal)
                last.then_inc(onehot_ready, 1)

            norms = [0]

            def layer_norm(src, eps, out, done):
                for qt in range(NT):
                    last = nc.vector.bn_stats(stats[:, qt, :], src[:, qt, :])
                link(last)
                for qt in range(NT):
                    last = nc.vector.bn_aggr(mean_var[:, qt, :], stats[:, qt, :])
                link(last)
                k = norms[0]
                norms[0] += 1
                nc.vector.tensor_scalar(var_eps[:, :], mean_var[:, :, 1], eps, None, ALU.add).then_inc(var_ready, 1)
                dve.wait_ge(rstd_ready, k + 1)
                for qt in range(NT):
                    last = nc.vector.tensor_scalar(out[:, qt, :], src[:, qt, :], mean_var[:, qt, 0:1],
                                                   rstd[:, qt:qt + 1], ALU.subtract, ALU.mult)
                if done is None:
                    link(last)
                else:
                    last.then_inc(done, 1)

            dve.wait_ge(const_loaded, 16)
            tab = const[:, C_ROPE:C_COLS]
            link(nc.vector.tensor_copy(rope_parts[:, 0, :], tab))
            link(nc.vector.tensor_tensor(rope_rest, tab, rope_parts[:, 0, :], ALU.subtract))
            link(nc.vector.tensor_copy(rope_parts[:, 1, :], rope_rest))
            nc.vector.tensor_tensor(rope_parts[:, 2, :], rope_rest, rope_parts[:, 1, :], ALU.subtract
                                    ).then_inc(rope_split, 1)
            dve.wait_ge(pos_loaded, 16)
            link(nc.vector.tensor_copy(pos_f[:, :], pos_i))
            link(nc.vector.tensor_scalar(pos_neg, pos_f[:, :], 0.0, float(MAX_POS), ALU.is_lt, ALU.mult))
            link(nc.vector.tensor_tensor(pos_f[:, :], pos_f[:, :], pos_neg, ALU.add))
            link(nc.vector.tensor_scalar(pos_f[:, :], pos_f[:, :], 0.0, float(MAX_POS - 1), ALU.max, ALU.min))
            place_onehot(0)
            place_onehot(1)
            for buf in range(STACK_BUFS):
                nc.vector.memset(q_stack[:, buf, :, :].rearrange("p a b -> p (a b)").bitcast(F32), 0.0)
                link(nc.vector.memset(k_stack[:, buf, :, :].rearrange("p a b -> p (a b)").bitcast(F32), 0.0))
                link(nc.vector.memset(k_stack[MAX_ROW:MAX_ROW + MAX_ROWS, buf, 1::2, :], 1.0))
                nc.vector.memset(k_stack[MAX_ROW:MAX_ROW + MAX_ROWS // 2, buf, 0::2, :], 1.0)
                nc.vector.memset(k_stack[MAX_ROW:MAX_ROW + MAX_ROWS // 2, buf, 1::2, :], 0.0).then_inc(stack_cleared, 1)
            nc.vector.tensor_copy(ident16[:, :], ident).then_inc(dve_const, 1)
            nc.vector.memset(mean_mat[:, :], 1.0 / (D * D)).then_inc(dve_const, 1)

            def setup_rest():
                dve.wait_ge(silu_exp, 1)
                link(nc.vector.tensor_scalar(silu[:, 1, :], silu[:, 0, :], 1.0, None, ALU.add))
                link(nc.vector.reciprocal(silu[:, 2, :], silu[:, 1, :]))
                link(nc.vector.tensor_tensor(silu[:, 3, :].rearrange("p (b s) -> p b s", b=B), ctx_t[:, :, 0:2],
                                             silu[:, 2, :].rearrange("p (b s) -> p b s", b=B), ALU.mult))
                nc.vector.tensor_copy(silu_rep[:, :, :], silu[:, 3, :].unsqueeze(2).broadcast_to([P, 2 * B, P])
                                      ).then_inc(silu_ready, 2)
                dve.wait_ge(w_loaded[3], 16)
                nc.vector.tensor_reduce(quant_s[:, 0, :], w[:, W_AT["q4"]:W_AT["o4"] + 1, :], AX.X, ALU.add,
                                        apply_absolute_value=True).then_inc(quant_abs, 1)

            def quantise():
                wt = w[:, W_AT["q4"]:W_AT["o4"] + 1, :]
                link(nc.vector.tensor_scalar(quant_s[:, 2, :], quant_s[:, 1, :], 1e-5, None, ALU.add))
                link(nc.vector.reciprocal(quant_s[:, 0, :], quant_s[:, 2, :]))
                link(nc.vector.tensor_tensor(quant[:, :, :], wt, quant_s[:, 0, :].unsqueeze(2).broadcast_to([P, 4, D]),
                                             ALU.mult))
                link(nc.vector.tensor_scalar(quant2[:, :, :], quant[:, :, :], -0.5, None, ALU.is_lt))
                link(nc.vector.scalar_tensor_tensor(quant[:, :, :], quant[:, :, :], 0.5, quant2[:, :, :],
                                                    ALU.is_gt, ALU.subtract))
                link(nc.vector.tensor_tensor(quant2[:, :, :], quant[:, :, :],
                                             quant_s[:, 1, :].unsqueeze(2).broadcast_to([P, 4, D]), ALU.mult))
                link(nc.vector.tensor_tensor(quant[:, :, :], quant2[:, :, :], wt, ALU.subtract))
                nc.vector.tensor_tensor(wt, wt, quant[:, :, :], ALU.add).then_inc(quant_ready, 1)

            for st in steps:
                if st[0] == "max":
                    _, u, i = st
                    n = no(*st)
                    if i == 0 and u >= 2:
                        dve.wait_ge(max_split, u - 1)
                    dve.wait_ge(max_scored, n + 1)
                    if halves(u // B):
                        src = ps_max[n % 2][:, :].rearrange("p (s a k) -> p s a k", s=NT, a=2)
                        dst = neg_max[:, u % 2, :, :, i]
                    else:
                        pair, qt = divmod(i, NT)
                        src = ps_max[n % 2][:, :].rearrange("p (a k) -> p a k", a=2)
                        dst = neg_max[:, u % 2, qt, :, pair]
                    nc.vector.tensor_reduce(dst, src, AX.X, ALU.max, negate=True).then_inc(max_taken, 1)
                    if i == n_banks(u) - 1:
                        dve.wait_ge(max_taken, n + 1)
                        if u >= 2:
                            dve.wait_ge(small_ready, no("small", "max_t", u - 2) + 1)
                        m = neg_max[:, u % 2, :, :, :].rearrange("p n a e -> p (n a) e")
                        mp = max_parts[:, u % 2, :, :, :, :].rearrange("p n a j e -> p (n a) j e")
                        link(nc.vector.tensor_copy(mp[:, :, 0, :], m))
                        nc.vector.tensor_tensor(mp[:, :, 1, :], m, mp[:, :, 0, :], ALU.subtract).then_inc(max_split, 1)
                elif st[0] == "small":
                    _, kind, u = st
                    n = no(*st)
                    phase, b = divmod(u, B)
                    if kind in ("q", "k") and phase == 0:
                        dve.wait_ge(small_ready, n + 1)
                        dve.wait_ge(small_used, no("small", "rope", u) + 1)
                        if u >= 2:
                            dve.wait_ge(q_split if kind == "q" else k_split, u - 1)
                        if 2 * u + (kind == "k"):
                            dve.wait_ge(roped, 2 * u + (kind == "k"))
                        cos, sin = rope_cs[:, u, 0:T], rope_cs[:, u, T:2 * T]
                        if kind == "q":
                            if u == 0:
                                dve.wait_ge(rows_loaded, 32)
                            nc.vector.scalar_tensor_tensor(rope_a[:, :], ps_small[:, 0:T], V("bq0"), cos, ALU.add, ALU.mult)
                            last = nc.vector.scalar_tensor_tensor(rope_b[:, :], ps_small[:, T:2 * T], V("bq0r"), sin,
                                                                  ALU.add, ALU.mult)
                        else:
                            nc.vector.tensor_tensor(rope_a[:, :], ps_small[:, 0:T], cos, ALU.mult)
                            last = nc.vector.tensor_tensor(rope_b[:, :], ps_small[:, T:2 * T], sin, ALU.mult)
                        last.then_inc(small_used, 1)
                        dve.wait_ge(small_used, n + 1)
                        nc.vector.tensor_tensor(q_f[:, u % 2, 0 if kind == "q" else 1, :], rope_a[:, :], rope_b[:, :],
                                                ALU.add).then_inc(roped, 1)
                        if kind == "k" and u + 2 < B:
                            place_onehot(u + 2)
                        if kind == "k" and u == 1:
                            setup_rest()
                    elif kind == "mod":
                        dve.wait_ge(small_ready, n + 1)
                        for k in range(6):
                            last = nc.vector.tensor_scalar(mods[:, k, :], ps_small[:, 2 * B * k:2 * B * (k + 1)],
                                                           V(f"ada_{(0, 1, 3, 4, 6, 7)[k]}"), float(k % 2), ALU.add, ALU.add)
                        last.then_inc(small_used, 1)
                    elif kind == "gate":
                        dve.wait_ge(small_ready, n + 1)
                        nc.vector.tensor_tensor(gates[:, u, :, :], ps_small[:, 0:3 * D].rearrange("p (a b) -> p a b", a=3),
                                                rows[:, R_AT["gate1"]:R_AT["gate3"] + 1, :], ALU.add).then_inc(small_used, 1)
                    elif kind == "gamma":
                        dve.wait_ge(small_ready, n + 1)
                        nc.vector.tensor_copy(quant_s[:, 1, :], ps_small[:, 0:4]).then_inc(small_used, 1)
                        dve.wait_ge(small_used, n + 1)
                        quantise()
                    elif kind == "max_t":
                        dve.wait_ge(small_ready, n + 1)
                        if u >= 2:
                            s_, n_ = until(max_placed, u - 2)
                            dve.wait_ge(s_, 16 * n_)
                        nc.vector.tensor_copy(max_rows[:, u % 2, :], ps_small16[0:32, 0:T]).then_inc(small_used, 1)
                    elif kind == "unstack":
                        dve.wait_ge(small_ready, n + 1)
                        src = ps_small[:, :].rearrange("p (m e) -> p m e", e=2 * DH)
                        link(nc.vector.reciprocal(inv_sum[:, :], src[:, :, DH]))
                        nc.vector.tensor_tensor(heads[:, :, :].rearrange("p n (h e) -> p (n h) e", e=DH), src[:, :, 0:DH],
                                                inv_sum[:, :].unsqueeze(2).broadcast_to([P, 2 * H, DH]), ALU.mult
                                                ).then_inc(small_used, 1)
                    elif kind == "out_proj":
                        dve.wait_ge(small_ready, n + 1)
                        dve.wait_ge(base_ready, u + 1)
                        ps = ps_small[:, 0:NT * D].rearrange("p (n c) -> p n c", n=NT)
                        bs = base[:, u % 2, :, :]
                        xb = x[:, b, :, :]
                        if phase in (1, 2):
                            nc.vector.tensor_tensor(gated[:, :, :], ps, gates[:, 2 * b:2 * b + 2, phase - 1, :], ALU.mult
                                                    ).then_inc(small_used, 1)
                            dve.wait_ge(small_used, n + 1)
                            to = gated[:, :, :] if phase == 1 else xb
                            nc.vector.tensor_tensor(to, gated[:, :, :], bs, ALU.add).then_inc(x_updated, 1)
                            dve.wait_ge(*new_x(u))
                            layer_norm(to, 1e-6, normed, norm_ready)
                        elif phase == 0:
                            nc.vector.tensor_tensor(xb, ps, bs, ALU.add).then_inc(small_used, 1)
                            dve.wait_ge(small_used, n + 1)
                            layer_norm(xb, 1e-6, normed, norm_ready)
                        elif phase == 3:
                            nc.vector.tensor_tensor(gated[:, :, :], ps, bs, ALU.add).then_inc(small_used, 1)
                            dve.wait_ge(small_used, n + 1)
                            layer_norm(gated[:, :, :], 1e-5, normed, None)
                            link(nc.vector.tensor_tensor(gated[:, :, :], normed[:, :, :], row2("g3"), ALU.mult))
                            nc.vector.tensor_tensor(xb, gated[:, :, :], row2("b3"), ALU.add).then_inc(x_updated, 1)
                            dve.wait_ge(*new_x(u))
                            layer_norm(xb, 1e-5, normed, norm_ready)
                        else:
                            nc.vector.tensor_tensor(x[:, b, :, :], ps, bs, ALU.add).then_inc(small_used, 1)
                    elif kind == "fc2":
                        dve.wait_ge(small_ready, n + 1)
                        dve.wait_ge(base_mlp_ready, b + 1)
                        ps = ps_small[:, 0:NT * D].rearrange("p (n c) -> p n c", n=NT)
                        nc.vector.tensor_tensor(gated[:, :, :], ps, gates[:, 2 * b:2 * b + 2, 2, :], ALU.mult
                                                ).then_inc(small_used, 1)
                        dve.wait_ge(small_used, n + 1)
                        nc.vector.tensor_tensor(x[:, b, :, :], gated[:, :, :], base_mlp[:, b % 2, :, :], ALU.add
                                                ).then_inc(mlp_added, 1)


def host_layout(inp):
    i = {k: np.asarray(v) for k, v in inp.items()}
    par, d, pair = np.meshgrid(np.arange(2), np.arange(DH), np.arange(PAIRS), indexing="ij")
    stack = (DH * (2 * pair + par) + d).ravel()
    rot = (DH * (2 * pair + par) + (d + DH // 2) % DH).ravel()
    g, j, ii, dd = np.meshgrid(np.arange(2), np.arange(4), np.arange(2), np.arange(DH), indexing="ij")
    headrow = (DH * (8 * g + 4 * ii + j) + dd).ravel()

    def col(wt, k):
        return wt[:, k * D:(k + 1) * D]

    w = {"q0": i["L0_xattn_Wq"].T[:, stack], "q0r": i["L0_xattn_Wq"].T[:, rot], "k0": i["L0_xattn_Wk"].T[:, stack],
         "k0r": i["L0_xattn_Wk"].T[:, rot], "v0": i["L0_xattn_Wv"].T, "o0": i["L0_xattn_Wo"].T[headrow]}
    v = {"bq0": i["L0_xattn_bq"][stack], "bq0r": i["L0_xattn_bq"][rot], "bv0": i["L0_xattn_bv"][headrow]}
    for p, n in ((1, "attn"), (2, "crs")):
        qkv, bias = i[f"L1_xattn_{n}_qkv_w"], i[f"L1_xattn_{n}_qkv_b"].reshape(3, D)
        w.update({f"q{p}": col(qkv, 0)[:, stack], f"k{p}": col(qkv, 1)[:, stack], f"v{p}": col(qkv, 2),
                  f"o{p}": i[f"L1_xattn_{n}_proj_w"][headrow]})
        v.update({f"bq{p}": bias[0][stack], f"bk{p}": bias[1][stack], f"bv{p}": bias[2][headrow]})
    for k in range(4):
        w[f"fc1{'abcd'[k]}"] = col(i["L1_xattn_mlp_fc1_w"], k)
        w[f"fc2{'abcd'[k]}"] = i["L1_xattn_mlp_fc2_w"][k * D:(k + 1) * D]
        v[f"fc1_{k}"] = i["L1_xattn_mlp_fc1_b"][k * D:(k + 1) * D]
    for k in range(9):
        w[f"ada{k}"] = col(i["L1_xattn_ada_w"], k)
        v[f"ada_{k}"] = i["L1_xattn_ada_b"][k * D:(k + 1) * D]
    qkv, bias = i["L2_xattn_W_qkv"].T, i["L2_xattn_b_qkv"].reshape(3, D)
    w.update({"q3": col(qkv, 0)[:, stack], "k3": col(qkv, 1)[:, stack], "v3": col(qkv, 2), "o3": i["L2_xattn_W_o"].T[headrow]})
    v.update({"bq3": bias[0][stack], "bk3": bias[1][stack], "bv3": bias[2][headrow]})
    w.update({"q4": i["L3_xattn_Wq"].T[:, stack], "k4": i["L3_xattn_Wk"].T[:, stack], "v4": i["L3_xattn_Wv"].T,
              "o4": i["L3_xattn_Wo"].T[headrow]})
    v.update({"bq4": i["L3_xattn_bq"][stack], "bk4": i["L3_xattn_bk"][stack], "bv4": i["L3_xattn_bv"][headrow],
              "g4": i["L3_xattn_ln_gamma"], "b4": i["L3_xattn_ln_beta"]})
    ada_b = i["L1_xattn_ada_b"].reshape(9, D)
    r = {"bo0": i["L0_xattn_bo"], "bo1": i["L1_xattn_attn_proj_b"], "bo2": i["L1_xattn_crs_proj_b"],
         "bfc2": i["L1_xattn_mlp_fc2_b"], "bo3": i["L2_xattn_b_o"], "g3": i["L2_xattn_ln_gamma"],
         "b3": i["L2_xattn_ln_beta"], "bo4": i["L3_xattn_bo"], "gate1": ada_b[2], "gate2": ada_b[5], "gate3": ada_b[8]}
    return {"x": i["x"], "x_t": np.ascontiguousarray(i["x"].transpose(0, 2, 1)),
            "ctx_t": np.ascontiguousarray(i["ctx_1024"].transpose(0, 2, 1)), "pos": i["pos_BxS2"],
            "w": np.concatenate([w[n] for n in W_NAMES], axis=1),
            "vec": np.stack([v[n] for n in V_NAMES], axis=1),
            "rows": np.concatenate([r[n] for n in R_NAMES])}


def constants():
    inv_freq = 1.0 / 10000.0 ** (np.arange(0, DH, 2, dtype=np.float32) / DH)
    freqs = np.arange(MAX_POS, dtype=np.float32)[:, None] * inv_freq[None, :]
    emb = np.concatenate([freqs, freqs], axis=-1)
    cos, sin = np.cos(emb), np.sin(emb)
    sin[:, :DH // 2] = -sin[:, :DH // 2]
    d = np.tile(np.repeat(np.arange(DH), PAIRS), 2)
    tab = np.stack([cos[:, d], sin[:, d]], axis=1).reshape(POS_CHUNKS, P, 2 * D).transpose(1, 0, 2).reshape(P, -1)
    iota = np.arange(MAX_POS, dtype=np.float32).reshape(POS_CHUNKS, P).T
    return np.concatenate([np.eye(P, dtype=np.float32), iota, tab.astype(np.float32)], axis=1).astype(np.float32)


def kernel(**inputs):
    import numpy as _np
    import concourse.bacc as _bacc
    from concourse import mybir as _mybir
    from concourse.bass_utils import run_bass_kernel_spmd as _run

    nc = _bacc.Bacc("TRN2", target_bir_lowering=False, num_devices=1)
    arrays, aps = {}, {}
    for name, v in {**host_layout(inputs), "const": constants()}.items():
        v = _np.ascontiguousarray(v)
        arrays[f"in_{name}"] = v
        aps[name] = nc.dram_tensor(f"in_{name}", v.shape, _mybir.dt.from_np(v.dtype), kind="ExternalInput").ap()
    aps["out"] = nc.dram_tensor("out_0", (B, T, D), F32, kind="ExternalOutput").ap()
    build(nc, aps)
    r = _run(nc, [arrays], core_ids=[0])
    return r.results[0]["out_0"]
```

```python
from contextlib import ExitStack

import numpy as np

import concourse.bass as bass
import concourse.mybir as mybir

F32 = mybir.dt.float32
BF16 = mybir.dt.bfloat16
I32 = mybir.dt.int32
ALU = mybir.AluOpType
ACT = mybir.ActivationFunctionType
AX = mybir.AxisListType

B, T, D = 4, 256, 128
H, DH = 16, 8
P = 128
NT = T // P
PAIRS = H // 2
SCALE = float(DH) ** -0.5
PHASES = 5
UNITS = PHASES * B
MAX_POS = 512
POS_CHUNKS = MAX_POS // P
PARTS = 3
SLOTS = ((0, 2), (1, 1), (2, 0), (0, 1), (1, 0), (0, 0))
SLOT_ROWS = 2 * DH
MAX_ROW = SLOT_ROWS * len(SLOTS)
MAX_ROWS = 4
SCORE_ROWS = MAX_ROW + MAX_ROWS
STACK_BUFS = 3
BANK = 512
CHUNK = BANK
SMALL_BUFS, MAX_BUFS, SCORE_BUFS = 2, 2, 3
PROB_BUFS = 8

W_NAMES = ["q0", "q0r", "k0", "k0r", "v0", "o0",
           "q1", "k1", "v1", "o1", "q2", "k2", "v2", "o2",
           "fc1a", "fc1b", "fc1c", "fc1d", "fc2a", "fc2b", "fc2c", "fc2d",
           "ada0", "ada1", "ada2", "ada3", "ada4", "ada5", "ada6", "ada7", "ada8",
           "q3", "k3", "v3", "o3", "q4", "k4", "v4", "o4"]
W_AT = {n: i for i, n in enumerate(W_NAMES)}
W_GROUPS = (("q0", "o0"), ("q1", "fc2d"), ("ada0", "ada8"), ("q3", "o4"))
V_NAMES = (["bq0", "bq0r", "bv0", "bq1", "bk1", "bv1", "bq2", "bk2", "bv2", "bq3", "bk3", "bv3",
            "bq4", "bk4", "bv4", "g4", "b4"] + [f"fc1_{i}" for i in range(4)] + [f"ada_{i}" for i in range(9)])
V_AT = {n: i for i, n in enumerate(V_NAMES)}
R_NAMES = ["bo0", "bo1", "bo2", "bfc2", "bo3", "g3", "b3", "bo4", "gate1", "gate2", "gate3"]
R_AT = {n: i for i, n in enumerate(R_NAMES)}
C_IDENT, C_IOTA = 0, P
C_COLS = P + POS_CHUNKS
ROPE_ROWS = PARTS * DH
ROPE_COLS = POS_CHUNKS * ROPE_ROWS + 2 * D


def halves(phase):
    return phase in (1, 2)


def n_banks(u):
    return PAIRS if halves(u // B) else 2 * PAIRS


def n_chunks(u):
    return PAIRS if halves(u // B) else H


def group_of_chunk(n):
    u = 0
    while n >= n_chunks(u):
        n -= n_chunks(u)
        u += 1
    return u, n * 4 // n_chunks(u)


OFF_PE = {"rstd": None, "norm": None, "stack_max": None, "split_q": "pool", "split_k": "pool",
          "stack_q": "dma", "stack_k": "dma"}


class Plan:

    def __init__(self):
        self.steps, self.done, self.count = [], {}, {"small": 0, "max": 0, "score": 0}
        self.free = dict(pe=0, act=0, dve=0, pool=0, dma=0)

    def run(self, engine, after, cost):
        self.free[engine] = max(self.free[engine], after) + cost
        return self.free[engine]

    def waits(self, st):
        kind, u = (st[1], st[2]) if st[0] == "small" else st[:2]
        phase = u // B
        need = []
        if kind in ("split_q", "split_k"):
            return [("part", kind[-1], u)]
        if kind == "stack_max":
            return [("max_t", u)]
        if kind in ("stack_q", "stack_k"):
            return [("split" + kind[5:], u, kind == "stack_k")]
        if st[0] == "small" and self.count["small"] >= SMALL_BUFS:
            need.append(("bank", "small", self.count["small"] - SMALL_BUFS))
        if kind == "max":
            need += [("placed", "q", u), ("placed", "k", u)]
            if self.count["max"] >= MAX_BUFS:
                need.append(("bank", "max", self.count["max"] - MAX_BUFS))
            if u >= 2 and st[2] == 0:
                need.append(("max_t", u - 2))
        elif kind == "max_t":
            need += [("split", u)] + [("placed", "max", u - 2)] * (u >= 2) + [("score", u - 3, n_chunks(u - 3) - 1)] * (u >= 3)
        elif kind == "score":
            need.append(("placed", "max", u))
            n = self.count["score"]
            if n >= SCORE_BUFS:
                need.append(("bank", "score", n - SCORE_BUFS))
            if n >= PROB_BUFS:
                need.append(("value", *group_of_chunk(n - PROB_BUFS)))
            if st[2] == 0 and phase:
                need.append(("new_x", u - B))
                if phase == 3:
                    need.append(("mlp_added", u - B))
            if st[2] == 0 and u == B:
                need += [("gate", i) for i in range(2 * B)]
            if st[2] == 0 and u >= 2:
                need.append(("new_x", u - 2))
        elif kind == "value":
            need.append(("exp", u, (st[2] + 1) * n_chunks(u) // 4 - 1))
            if st[2] == 0:
                need += [("v", u)] + [("raw", u - 1)] * (u > 0)
            if st[2] == 3 and u:
                need.append(("unstack", u - 1))
        elif kind in ("q", "k", "v"):
            if phase == 0 and kind != "v":
                need.append(("rope", u))
            if phase and (kind == "q" or halves(phase)):
                need.append(("x_t" if (u - B) // B == 2 else "norm_t", u - B))
            if u // B < 2:
                need.append(("loads",) if phase else ("loads0",))
            if phase == 4:
                need.append(("quant",))
            if kind != "v" and u >= 2:
                need.append(("placed", kind, u - 2))
            if u >= STACK_BUFS:
                need.append(("value", u - 3, 3) if kind == "v" else ("score", u - 3, n_chunks(u - 3) - 1))
        elif kind == "pick":
            need.append(("onehot", u))
        elif kind == "rope":
            need.append(("pick", u // 2))
        elif kind == "gamma":
            need.append(("quant_abs",))
        elif kind in ("mod", "gate"):
            need.append(("silu",))
        elif kind == "unstack":
            need += [("raw", u)] + [("heads_t", u - 1)] * (u > 0)
        elif kind == "heads_t":
            need += [("unstack", u)] + [("out_proj", u - 1)] * (u > 0)
        elif kind == "out_proj":
            need.append(("heads_t", u))
            if u and (u - 1) // B < 4:
                need.append(("norm", u - 1, (u - 1) // B == 3))
        elif kind == "rstd":
            need.append(("var", u, st[2]))
        elif kind == "norm":
            need.append(("rstd", u, st[2]))
            if u:
                need.append(("norm_t", u - 1))
        elif kind == "norm_t":
            need.append(("norm", u, phase == 3))
            if u == 0:
                need.append(("mod", 0))
            if phase == 2:
                need.append(("v", u))
            if phase == 2 and u % B >= 2:
                need.append(("mlp_added", u - 2))
        elif kind in ("fc1_lo", "fc1_hi"):
            need.append(("norm_t", u))
        elif kind == "fc2":
            need.append(("fc1_hi", u))
        elif kind == "x_t":
            need.append(("mlp_added", u))
        return need

    def start(self, st):
        t = self.free.get(OFF_PE.get(st[0], "pe"), 0)
        for name in self.waits(st):
            if name not in self.done:
                return None
            t = max(t, self.done[name])
        return t

    def append(self, st, t):
        kind, u = (st[1], st[2]) if st[0] == "small" else st[:2]
        phase = u // B
        done, run = self.done, self.run
        self.steps.append(st)
        short = halves(phase)
        if kind == "norm":
            t = run("dve", t, 550)
            done["norm", u, st[2]] = t
            if phase == 3 and st[2] == 0:
                t = run("dve", t, 1700)
                done["new_x", u] = t
                done["var", u, 1] = t
            return
        if kind == "rstd":
            done["rstd", u, st[2]] = run("pool", t, 700)
            return
        if kind in ("split_q", "split_k"):
            done[kind, u, st[2]] = run("pool", t, 2100)
            return
        if kind == "stack_max":
            done["placed", "max", u] = run("dma", t, 650) + 2000
            return
        if kind in ("stack_q", "stack_k"):
            done["placed", kind[-1], u] = run("dma", t, 6 * 650) + 2000
            return
        pe = {"max": 216, "score": 260, "value": 510 if short else 1020, "q": 440, "k": 440, "v": 430, "rope": 500, "pick": 900,
              "max_t": 60, "unstack": 250, "heads_t": 120, "norm_t": 120, "x_t": 120, "out_proj": 430, "fc1_lo": 860,
              "fc1_hi": 860, "fc2": 1720, "mod": 300, "gate": 640, "gamma": 100}[kind]
        if phase == 0 and kind in ("q", "k"):
            pe *= 2
        t = run("pe", t, pe) + 180
        if st[0] in self.count:
            n = self.count[st[0]]
            self.count[st[0]] += 1
        if kind == "max":
            t = run("dve", t, 600)
            if st[2] == n_banks(u) - 1:
                done["split", u] = run("dve", t, 400) + 180
        elif kind == "score":
            t = run("act", t, 480)
            done["exp", u, st[2]] = t + 180
            done["score", u, st[2]] = t
            if st[2] == 0:
                run("pool", 0, 700)
        elif kind == "value":
            done["value", u, st[2]] = t
            if st[2] == 3:
                done["raw", u] = run("act", t, 480) + 180
        elif kind in ("q", "k"):
            if phase == 0:
                t = run("dve", t, 720)
                full = run("dve", t, 400)
                part = run("act", full, 650)
            else:
                t = part = run("act", t, 720 if kind == "q" else 1080)
            done["part", kind, u] = part
            done[kind, u] = t
        elif kind == "v":
            done["v", u] = t = run("act", t, 350) + 100
        elif kind == "max_t":
            t = run("dve", t, 220)
            done["max_t", u] = t
        elif kind == "unstack":
            done["unstack", u] = t = run("dve", t, 800) + 100
        elif kind == "out_proj":
            t = run("dve", t, 350)
            last = run("dve", t, (350 if phase in (1, 2) else 0) + (750 if phase < 4 else 0))
            done["new_x", u] = t if phase in (0, 3) else last
            done["out_proj", u] = t
            if phase < 4:
                done["var", u, 0] = last
        elif kind == "fc2":
            t = run("dve", t, 350)
            done["mlp_added", u] = run("dve", t, 350) + 150
        elif kind in ("gate", "mod", "gamma"):
            t = run("dve", t, 400)
            done[kind, u] = t
            if kind == "gate":
                run("pool", t, 950)
            if kind == "gamma":
                done["quant",] = run("dve", t, 5000)
        else:
            cost = {"heads_t": 370, "norm_t": 450, "x_t": 300, "fc1_lo": 1400, "fc1_hi": 1400, "rope": 480, "pick": 480}[kind]
            done[kind, u] = t = run("act", t, cost) + 150
        if st[0] in self.count:
            done["bank", st[0], n] = t


def make_schedule():
    units = range(UNITS)
    streams = [
        [s for u in units for s in [(k, u, i) for i in range(2) for k in ("rstd", "norm")] + [("small", "norm_t", u)]
         if u // B < 4 and (s[0] == "small" or s[2] == 0 or u // B == 3)],
        [("small", k, u) for u in units for k in ("unstack", "heads_t", "out_proj")],
        [("small", k, u) for u in units if u // B == 2 for k in ("fc1_lo", "fc1_hi", "fc2", "x_t")],
        [s for u in units for s in (("split_k", u, 0), ("split_k", u, 1), ("split_q", u, 0))],
        [("stack_max", u, 0) for u in units],
        [s for u in units for s in (("stack_k", u, 0), ("stack_q", u, 0))],
        [("small", "max_t", u) for u in units],
        [("small", k, u) for u in units for k in ("k", "q", "v")],
        [("max", u, i) for u in units for i in range(n_banks(u))],
        [("value", u, k) for u in units for k in range(4)],
        [("score", u, c) for u in units for c in range(n_chunks(u))],
        [("small", *s) for i in range(B // 2) for s in (("pick", i), ("rope", 2 * i), ("rope", 2 * i + 1))],
        [("small", "mod", 0)] + [("small", "gate", i) for i in range(2 * B)] + [("small", "gamma", 0)],
    ]
    plan = Plan()
    plan.done.update({("onehot", 0): 7000, ("onehot", 1): 10000, ("silu",): 12000, ("loads",): 20000, ("quant_abs",): 30000,
                      ("loads0",): 9500})
    at = [0] * len(streams)
    while True:
        ready = []
        for rank, (stream, i) in enumerate(zip(streams, at)):
            if i < len(stream):
                t = plan.start(stream[i])
                if t is not None:
                    ready.append((t, rank))
        if not ready:
            break
        now = max(plan.free["pe"], min(ready)[0])
        t, rank = min(ready, key=lambda r: (max(r[0], now), r[1]))
        plan.append(streams[rank][at[rank]], t)
        at[rank] += 1
    assert at == [len(x) for x in streams], [x[i] for x, i in zip(streams, at) if i < len(x)]
    return plan.steps


def build(nc, a):
    steps = make_schedule()
    order = {}
    seen = {}
    for st in steps:
        assert st not in order, st
        order[st] = seen.get(st[0], 0)
        seen[st[0]] = order[st] + 1

    def no(*step):
        return order[step]

    with ExitStack() as ctx:
        def sb(name, shape, dt=F32):
            return ctx.enter_context(nc.sbuf_tensor(name, shape, dt))

        def sem(name):
            return ctx.enter_context(nc.semaphore(name))

        w = sb("w", [P, len(W_NAMES), D])
        vec = sb("vec", [P, len(V_NAMES)])
        rows = sb("rows", [P, len(R_NAMES), D])
        const = sb("const", [P, C_COLS])
        ident = const[:, C_IDENT:C_IDENT + P]
        ident16 = sb("ident16", [P, P], BF16)
        mean_mat = sb("mean_mat", [P, P])
        pos_i = sb("pos_i", [P, B * T], I32)
        pos_f = sb("pos_f", [P, B * T])
        pos_neg = sb("pos_neg", [P, B * T])
        onehot = sb("onehot", [P, POS_CHUNKS, B * T], BF16)
        rope_table = sb("rope_table", [P, ROPE_COLS], BF16)
        rope_picked = sb("rope_picked", [ROPE_ROWS, B // 2, 2 * T], BF16)
        rope_cs = sb("rope_cs", [P, B, 2 * T])
        x = sb("x", [P, B, NT, D])
        src_t = sb("src_t", [P, B, T])
        ctx_t = sb("ctx_t", [P, B, T])
        silu = sb("silu", [P, 4, 2 * B])
        silu_rep = sb("silu_rep", [P, 2 * B, P])
        mods = sb("mods", [P, 6, 2 * B])
        gates = sb("gates", [P, 2 * B, 3, D])
        gate_bias = sb("gate_bias", [P, 2 * B, 3, D])
        quant = sb("quant", [P, 4, D])
        quant2 = sb("quant2", [P, 4, D])
        quant_s = sb("quant_s", [P, 3, 4])
        q_f = sb("q_f", [P, 2, 2, T])
        rope_a = sb("rope_a", [P, T])
        rope_b = sb("rope_b", [P, T])
        split_r = sb("split_r", [P, 2, T])
        q_parts = sb("q_parts", [P, 2, PARTS, T], BF16)
        k_parts = sb("k_parts", [P, 2, PARTS, 2, T], BF16)
        q_stack = sb("q_stack", [P, STACK_BUFS, PAIRS, T], BF16)
        k_stack = sb("k_stack", [P, STACK_BUFS, H, T], BF16)
        v_cols = sb("v_cols", [P, STACK_BUFS, NT, H, 32])
        neg_max = sb("neg_max", [P, 2, NT, 2, PAIRS])
        max_parts = sb("max_parts", [P, 2, NT, 2, 2, PAIRS], BF16)
        max_rows = sb("max_rows", [32, 2, T], BF16)
        probs = sb("probs", [P, PROB_BUFS, CHUNK])
        heads_raw = sb("heads_raw", [P, BANK])
        inv_sum = sb("inv_sum", [P, 2 * H])
        heads = sb("heads", [P, NT, D])
        heads_t = sb("heads_t", [P, T])
        base = sb("base", [P, 2, NT, D])
        base_mlp = sb("base_mlp", [P, 2, NT, D])
        gated = sb("gated", [P, NT, D])
        gated_mlp = sb("gated_mlp", [P, NT, D])
        stats = sb("stats", [P, NT, 6])
        mean_var = sb("mean_var", [P, NT, 2])
        var_eps = sb("var_eps", [P, NT])
        minus_half = sb("minus_half", [P, NT])
        rstd = sb("rstd", [P, NT])
        normed = sb("normed", [P, NT, D])
        hidden = sb("hidden", [P, 4, T])

        ps_max = [ctx.enter_context(nc.psum_tensor(f"ps_max{i}", [P, BANK], F32)) for i in range(MAX_BUFS)]
        ps_score = [ctx.enter_context(nc.psum_tensor(f"ps_score{i}", [P, BANK], F32)) for i in range(SCORE_BUFS)]
        ps_heads = ctx.enter_context(nc.psum_tensor("ps_heads", [P, BANK], F32))
        ps_smalls = [ctx.enter_context(nc.psum_tensor(f"ps_small{i}", [P, BANK], F32)) for i in range(SMALL_BUFS)]

        const_loaded = sem("const_loaded")
        w_loaded = [sem(f"w_loaded{i}") for i in range(len(W_GROUPS))]
        ctx_loaded = sem("ctx_loaded")
        src_loaded = sem("src_loaded")
        x_loaded = sem("x_loaded")
        rows_loaded = sem("rows_loaded")
        pos_loaded = sem("pos_loaded")
        q_placed = [sem(f"q_placed{i}") for i in range(STACK_BUFS)]
        k_placed = [sem(f"k_placed{i}") for i in range(STACK_BUFS)]
        max_placed = [sem(f"max_placed{i}") for i in range(STACK_BUFS)]
        out_stored = sem("out_stored")
        k_cleared = sem("k_cleared")
        v_cleared = sem("v_cleared")
        ones_set = sem("ones_set")
        dve_const = sem("dve_const")
        rope_loaded = sem("rope_loaded")
        onehot_ready = sem("onehot_ready")
        silu_exp = sem("silu_exp")
        silu_ready = sem("silu_ready")
        quant_abs = sem("quant_abs")
        quant_ready = sem("quant_ready")
        gate_bias_ready = sem("gate_bias_ready")
        small_ready = sem("small_ready")
        small_used = [sem(f"small_used{i}") for i in range(SMALL_BUFS)]
        max_scored = sem("max_scored")
        max_taken = sem("max_taken")
        max_split = sem("max_split")
        scored = sem("scored")
        exped = sem("exped")
        valued = sem("valued")
        heads_copied = sem("heads_copied")
        first_part = sem("first_part")
        roped = sem("roped")
        q_split = sem("q_split")
        k_split = sem("k_split")
        base_ready = sem("base_ready")
        base_mlp_ready = sem("base_mlp_ready")
        x_updated = sem("x_updated")
        mlp_added = sem("mlp_added")
        var_ready = sem("var_ready")
        rstd_ready = sem("rstd_ready")
        norm_ready = sem("norm_ready")
        dve_chain = sem("dve_chain")
        pool_chain = sem("pool_chain")

        block = ctx.enter_context(nc.Block())

        def W(name, n=1):
            return w[:, W_AT[name]:W_AT[name] + n, :].rearrange("p a b -> p (a b)")

        def V(name):
            return vec[:, V_AT[name]:V_AT[name] + 1]

        def row2(name):
            return rows[:, R_AT[name]:R_AT[name] + 1, :].broadcast_to([P, NT, D])

        def chunks_until(u):
            return sum(n_chunks(v) for v in range(u + 1))

        def banks_until(u):
            return no("max", u, n_banks(u) - 1) + 1

        def used(n):
            return small_used[n % SMALL_BUFS], n // SMALL_BUFS + 1

        def operands(kind, u):
            if kind in ("q", "k", "v") and u >= B and (kind == "q" or halves(u // B)):
                return [("x_t" if (u - B) // B == 2 else "norm_t", u - B)]
            return {"rope": [("pick", u // 2)], "heads_t": [("unstack", u)], "out_proj": [("heads_t", u)], "fc1_lo": [("norm_t", u)],
                    "fc2": [("fc1_lo", u), ("fc1_hi", u)]}.get(kind, [])

        def until(seq, u):
            return seq[u % STACK_BUFS], u // STACK_BUFS + 1

        def kv_source(u):
            return src_t if halves(u // B) else ctx_t

        def keys_tile(phase, s):
            return s if phase == 1 else 1 - s

        def part_views(kind, u):
            if kind == "q":
                return [(slice(0, P), [q_parts[:, u % 2, j, :] for j in range(PARTS)])]
            return [(slice(64 * par, 64 * par + 64), [k_parts[64 * par:64 * par + 64, u % 2, j, par, :] for j in range(PARTS)])
                    for par in range(2)]

        def turn(kind, u):
            other = "k" if kind == "q" else "q"
            return 1 if no("small", kind, u) < no("small", other, u) else 2

        def split_done(kind, u):
            return (q_split, u + 1) if kind == "q" else (k_split, 2 * (u + 1))

        def new_x(u):
            if u // B in (0, 4):
                return used(no("small", "out_proj", u))
            return x_updated, u - B + 1

        @block.sync
        def _(sp):
            def load_w(g):
                lo, hi = W_AT[W_GROUPS[g][0]], W_AT[W_GROUPS[g][1]] + 1
                sp.dma_start(w[:, lo:hi, :], a["w"][:, lo * D:hi * D].rearrange("p (a b) -> p a b", b=D)
                             ).then_inc(w_loaded[g], 16)

            sp.dma_start(const[:, :], a["const"]).then_inc(const_loaded, 16)
            load_w(0)
            sp.dma_start(src_t[:, :, :], a["x_t"].rearrange("b c t -> c b t")).then_inc(src_loaded, 16)
            sp.dma_start(x[:, :, :, :].rearrange("p b n c -> p (b n) c"),
                         a["x"].rearrange("b (n p) c -> p (b n) c", p=P)).then_inc(x_loaded, 16)
            load_w(2)
            load_w(1)
            load_w(3)
            for st in steps:
                if st[0] in ("stack_q", "stack_k"):
                    kind, u = st[0][-1], st[1]
                    buf = u % STACK_BUFS
                    if u >= STACK_BUFS:
                        sp.wait_ge(scored, chunks_until(u - STACK_BUFS))
                    sp.wait_ge(*split_done(kind, u))
                    for slot, (q_part, k_part) in enumerate(SLOTS):
                        r = SLOT_ROWS * slot
                        if kind == "q":
                            sp.dma_start(q_stack[r:r + SLOT_ROWS, buf, :, :], q_parts[:, u % 2, q_part, :]
                                         ).then_inc(q_placed[buf], 16)
                        else:
                            sp.dma_start(k_stack[r:r + SLOT_ROWS, buf, :, :].rearrange("p h t -> p (h t)"),
                                         k_parts[:, u % 2, k_part, :, :].rearrange("p a t -> p (a t)")
                                         ).then_inc(k_placed[buf], 16)
                if st[0] == "stack_max":
                    u = st[1]
                    sp.wait_ge(*used(no("small", "max_t", u)))
                    sp.dma_start(q_stack[MAX_ROW:MAX_ROW + MAX_ROWS, u % STACK_BUFS, :, :], max_rows[:, u % 2, :]
                                 ).then_inc(max_placed[u % STACK_BUFS], 16)
                if st[0] == "small" and st[1] == "out_proj" and st[2] // B == PHASES - 1:
                    b = st[2] % B
                    sp.wait_ge(*used(no(*st)))
                    sp.dma_start(a["out"][b].rearrange("(n p) c -> p n c", p=P), x[:, b, :, :]
                                 ).then_inc(out_stored, 16)
            sp.wait_ge(out_stored, 16 * B)

        @block.gpsimd
        def _(pool):
            chain = [0]

            def link(ins):
                chain[0] += 1
                ins.then_inc(pool_chain, 1)
                pool.wait_ge(pool_chain, chain[0])

            link(nc.gpsimd.memset(minus_half[:, :], -0.5))
            for par in range(2):
                rows_ = slice(64 * (1 - par), 64 * (1 - par) + 64)
                link(nc.gpsimd.memset(k_parts[rows_, :, :, par, :].rearrange("p b j t -> p (b j) t"), 0.0))
            nc.gpsimd.memset(minus_half[:, :], -0.5).then_inc(k_cleared, 1)
            pool.wait_ge(k_cleared, 1)

            def set_buffers(buf):
                r = slice(MAX_ROW, MAX_ROW + MAX_ROWS)
                r_even = slice(MAX_ROW, MAX_ROW + MAX_ROWS // 2)
                link(nc.gpsimd.memset(k_stack[r, buf, 1::2, :], 1.0))
                link(nc.gpsimd.memset(k_stack[r_even, buf, 1::2, :].bitcast(F32), 0.0))
                link(nc.gpsimd.memset(k_stack[r, buf, 0::2, :].bitcast(F32), 0.0))
                nc.gpsimd.memset(k_stack[r_even, buf, 0::2, :], 1.0).then_inc(ones_set, 1)
                pool.wait_ge(ones_set, buf + 1)
                link(nc.gpsimd.memset(v_cols[:, buf, :, :, :].rearrange("p n h c -> p (n h c)"), 0.0))
                for i in range(2):
                    v = v_cols[:, buf, :, :, :].rearrange("p n (g r) c -> p (n g) r c", g=2)[:, :, 4 * i:4 * i + 4, 16 * i + 8:16 * i + 16]
                    last = nc.gpsimd.memset(v, 1.0)
                last.then_inc(v_cleared, 1)
                pool.wait_ge(v_cleared, buf + 1)

            for buf in range(STACK_BUFS):
                set_buffers(buf)

            for st in steps:
                if st[0] in ("split_q", "split_k"):
                    kind, u, half = st[0][-1], st[1], st[2]
                    which = 0 if kind == "q" else 1
                    if half == 0:
                        if u // B:
                            pool.wait_ge(*used(no("small", kind, u)))
                        else:
                            pool.wait_ge(first_part, 2 * u + turn(kind, u))
                        if u >= 2:
                            s_, n_ = until(q_placed if kind == "q" else k_placed, u - 2)
                            pool.wait_ge(s_, 16 * len(SLOTS) * n_)
                    lines, part = part_views(kind, u)[half]
                    full, rest = q_f[lines, u % 2, which, :], split_r[lines, which, :]
                    link(nc.gpsimd.tensor_tensor(rest, full, part[0], ALU.subtract))
                    link(nc.gpsimd.tensor_tensor(part[1], full, part[0], ALU.subtract))
                    done = split_done(kind, u)
                    nc.gpsimd.tensor_tensor(part[2], rest, part[1], ALU.subtract).then_inc(done[0], 1)
                    pool.wait_ge(done[0], done[1] - (kind == "k" and half == 0))
                if st[:2] == ("small", "gate"):
                    i = st[2]
                    pool.wait_ge(*used(no(*st)))
                    if i == 0:
                        pool.wait_ge(rows_loaded, 32)
                    nc.gpsimd.tensor_tensor(gate_bias[:, i, :, :], gates[:, i, :, :],
                                            rows[:, R_AT["bo1"]:R_AT["bfc2"] + 1, :], ALU.mult).then_inc(gate_bias_ready, 1)
                    pool.wait_ge(gate_bias_ready, i + 1)
                if st[0] == "score" and st[2] == 0:
                    u = st[1]
                    phase, b = divmod(u, B)
                    if phase == 0 and b == 0:
                        pool.wait_ge(x_loaded, 16)
                        pool.wait_ge(rows_loaded, 16)
                    if phase:
                        pool.wait_ge(*new_x(u - B))
                    if phase == 3:
                        pool.wait_ge(mlp_added, b + 1)
                    if u >= 2:
                        pool.wait_ge(*new_x(u - 2))
                    if phase in (1, 2):
                        if u == B:
                            pool.wait_ge(gate_bias_ready, 2 * B)
                        add = gate_bias[:, 2 * b:2 * b + 2, phase - 1, :]
                    else:
                        add = row2({0: "bo0", 3: "bo3", 4: "bo4"}[phase])
                    nc.gpsimd.tensor_tensor(base[:, u % 2, :, :], x[:, b, :, :], add, ALU.add).then_inc(base_ready, 1)
                    pool.wait_ge(base_ready, u + 1)
                if st[0] == "rstd":
                    pool.wait_ge(var_ready, no(*st) + 1)
                    nc.gpsimd.tensor_tensor(rstd[:, :], var_eps[:, :], minus_half[:, :], ALU.pow).then_inc(rstd_ready, 1)
                    pool.wait_ge(rstd_ready, no(*st) + 1)
                if st[0] == "small" and st[1] == "norm_t" and st[2] // B == 2:
                    u = st[2]
                    b = u % B
                    pool.wait_ge(*new_x(u))
                    if b >= 2:
                        pool.wait_ge(mlp_added, b - 1)
                    nc.gpsimd.tensor_tensor(base_mlp[:, b % 2, :, :], x[:, b, :, :], gate_bias[:, 2 * b:2 * b + 2, 2, :],
                                            ALU.add).then_inc(base_mlp_ready, 1)
                    pool.wait_ge(base_mlp_ready, b + 1)

        @block.tensor
        def _(pe):
            def mm(out, lhs_t, rhs, start=True, stop=True, **k):
                return nc.tensor.matmul(out, lhs_t, rhs, start=start, stop=stop, **k)

            pe.wait_ge(const_loaded, 16)
            for st in steps:
                if st[0] == "max":
                    _, u, i = st
                    n = no(*st)
                    phase = u // B
                    buf = u % STACK_BUFS
                    if i == 0:
                        s_, n_ = until(q_placed, u)
                        pe.wait_ge(s_, 16 * len(SLOTS) * n_)
                        s_, n_ = until(k_placed, u)
                        pe.wait_ge(s_, 16 * len(SLOTS) * n_)
                    if n >= 2:
                        pe.wait_ge(max_taken, n - 1)
                    out = ps_max[n % 2]
                    if halves(phase):
                        for s in range(NT):
                            kt = keys_tile(phase, s)
                            last = mm(out[:, s * 2 * P:(s + 1) * 2 * P].rearrange("p (a b) -> p a b", a=2),
                                      q_stack[0:MAX_ROW, buf, i, s * P:(s + 1) * P],
                                      k_stack[0:MAX_ROW, buf, 2 * i:2 * i + 2, kt * P:(kt + 1) * P])
                    else:
                        pair, qt = divmod(i, NT)
                        last = mm(out[:, :], q_stack[0:MAX_ROW, buf, pair, qt * P:(qt + 1) * P],
                                  k_stack[0:MAX_ROW, buf, 2 * pair:2 * pair + 2, :].rearrange("p a b -> p (a b)"))
                    last.then_inc(max_scored, 1)
                elif st[0] == "score":
                    _, u, c = st
                    n = no(*st)
                    phase = u // B
                    buf = u % STACK_BUFS
                    if c == 0:
                        s_, n_ = until(max_placed, u)
                        pe.wait_ge(s_, 16 * n_)
                        if u < STACK_BUFS:
                            pe.wait_ge(ones_set, u + 1)
                    if n >= SCORE_BUFS:
                        pe.wait_ge(exped, n - SCORE_BUFS + 1)
                    out = ps_score[n % SCORE_BUFS]
                    if halves(phase):
                        for hl in range(2):
                            for s in range(NT):
                                h = 2 * c + hl
                                kt = keys_tile(phase, s)
                                col = (hl * NT + s) * P
                                last = mm(out[:, col:col + P], k_stack[0:SCORE_ROWS, buf, h, kt * P:(kt + 1) * P],
                                          q_stack[0:SCORE_ROWS, buf, h // 2, s * P:(s + 1) * P])
                    else:
                        for kt in range(NT):
                            last = mm(out[:, kt * T:(kt + 1) * T], k_stack[0:SCORE_ROWS, buf, c, kt * P:(kt + 1) * P],
                                      q_stack[0:SCORE_ROWS, buf, c // 2, :])
                    last.then_inc(scored, 1)
                elif st[0] == "value":
                    _, u, k = st
                    phase = u // B
                    g, i = divmod(k, 2)
                    first = chunks_until(u) - n_chunks(u)
                    buf = u % STACK_BUFS
                    if k == 0:
                        pe.wait_ge(*used(no("small", "v", u)))
                        if u:
                            pe.wait_ge(heads_copied, u)
                    chunks = n_chunks(u) // 4
                    pe.wait_ge(exped, first + (k + 1) * chunks)
                    if halves(phase):
                        for s in range(NT):
                            for j in range(4):
                                h = 4 * k + j
                                pr = probs[:, (first + h // 2) % PROB_BUFS, :]
                                col = (j % 2 * NT + s) * P
                                last = mm(ps_heads[32 * j:32 * j + 32, g * T + s * P:g * T + (s + 1) * P],
                                          v_cols[:, buf, keys_tile(phase, s), h, :], pr[:, col:col + P],
                                          start=(i == 0 and s == 0), stop=(i == 1 and s == 1),
                                          skip_group_check=True, tile_position=(0, 32 * j))
                    else:
                        for kt in range(NT):
                            for j in range(4):
                                h = 4 * k + j
                                pr = probs[:, (first + h) % PROB_BUFS, :]
                                last = mm(ps_heads[32 * j:32 * j + 32, g * T:(g + 1) * T],
                                          v_cols[:, buf, kt, h, :], pr[:, kt * T:(kt + 1) * T],
                                          start=(i == 0 and kt == 0), stop=(i == 1 and kt == 1),
                                          skip_group_check=True, tile_position=(0, 32 * j))
                    last.then_inc(valued, 1)
                elif st[0] == "small":
                    _, kind, u = st
                    n = no(*st)
                    phase, b = divmod(u, B)
                    if n >= SMALL_BUFS:
                        pe.wait_ge(*used(n - SMALL_BUFS))
                    out = ps_small = ps_smalls[n % SMALL_BUFS]
                    for before in operands(kind, u):
                        pe.wait_ge(*used(no("small", *before)))
                    if kind == "pick":
                        pe.wait_ge(rope_loaded, 16)
                        pe.wait_ge(onehot_ready, u + 1)
                        for c in range(POS_CHUNKS):
                            last = mm(out[0:ROPE_ROWS, :], rope_table[:, c * ROPE_ROWS:(c + 1) * ROPE_ROWS],
                                      onehot[:, c, 2 * u * T:2 * (u + 1) * T], start=(c == 0), stop=(c == POS_CHUNKS - 1))
                    elif kind == "rope":
                        for f in range(2):
                            at = POS_CHUNKS * ROPE_ROWS + f * D
                            last = mm(out[:, f * T:(f + 1) * T], rope_table[0:ROPE_ROWS, at:at + D],
                                      rope_picked[:, u // 2, u % 2 * T:(u % 2 + 1) * T])
                    elif kind == "mod":
                        pe.wait_ge(w_loaded[2], 16)
                        pe.wait_ge(silu_ready, 2)
                        for i, k in enumerate((0, 1, 3, 4, 6, 7)):
                            last = mm(out[:, 2 * B * i:2 * B * (i + 1)], W(f"ada{k}"), silu[:, 3, :])
                    elif kind == "gate":
                        last = mm(out[:, 0:3 * D].rearrange("p (a b) -> p a b", a=3), silu_rep[:, u, :],
                                  w[:, W_AT["ada2"]:W_AT["ada8"] + 1:3, :])
                    elif kind == "gamma":
                        pe.wait_ge(quant_abs, 1)
                        pe.wait_ge(dve_const, 2)
                        last = mm(out[:, 0:4], mean_mat[:, :], quant_s[:, 0, :])
                    elif kind in ("q", "k"):
                        if u == 0:
                            pe.wait_ge(w_loaded[0], 16)
                            pe.wait_ge(src_loaded if kind == "q" else ctx_loaded, 16)
                        if u == B and kind == "q":
                            pe.wait_ge(w_loaded[1], 16)
                        if u == 3 * B and kind == "q":
                            pe.wait_ge(w_loaded[3], 16)
                        if u == 4 * B and kind == "q":
                            pe.wait_ge(quant_ready, 1)
                        src = (src_t if kind == "q" else kv_source(u))[:, b, :]
                        last = mm(out[:, 0:T], W(f"{kind}{phase}"), src)
                        if phase == 0:
                            last = mm(out[:, T:2 * T], W(f"{kind}0r"), src)
                    elif kind == "v":
                        for kt in range(NT):
                            last = mm(out[:, kt * D:(kt + 1) * D], kv_source(u)[:, b, kt * P:(kt + 1) * P], W(f"v{phase}"))
                    elif kind == "max_t":
                        pe.wait_ge(max_split, u + 1)
                        pe.wait_ge(dve_const, 1)
                        for qt in range(NT):
                            last = nc.tensor.transpose(out[:, :].bitcast(BF16)[0:32, qt * P:(qt + 1) * P],
                                                       max_parts[:, u % 2, qt, :, :, :].rearrange("p a j e -> p (a j e)"),
                                                       ident16[:, :])
                    elif kind == "unstack":
                        pe.wait_ge(heads_copied, u + 1)
                        for qt in range(NT):
                            for g in range(2):
                                last = nc.tensor.transpose(out[:, (qt * 2 + g) * P:(qt * 2 + g + 1) * P],
                                                           heads_raw[:, g * T + qt * P:g * T + (qt + 1) * P], ident)
                    elif kind == "heads_t":
                        for qt in range(NT):
                            last = nc.tensor.transpose(out[:, qt * P:(qt + 1) * P], heads[:, qt, :], ident)
                    elif kind == "out_proj":
                        for qt in range(NT):
                            last = mm(out[:, qt * D:(qt + 1) * D], heads_t[:, qt * P:(qt + 1) * P], W(f"o{phase}"))
                    elif kind == "norm_t":
                        pe.wait_ge(norm_ready, u + 1)
                        for qt in range(NT):
                            last = nc.tensor.transpose(out[:, qt * P:(qt + 1) * P], normed[:, qt, :], ident)
                    elif kind in ("fc1_lo", "fc1_hi"):
                        for j in range(2):
                            f = 2 * (kind == "fc1_hi") + j
                            last = mm(out[:, j * T:(j + 1) * T], W(f"fc1{'abcd'[f]}"), src_t[:, b, :])
                    elif kind == "fc2":
                        for qt in range(NT):
                            for f in range(4):
                                last = mm(out[:, qt * D:(qt + 1) * D], hidden[:, f, qt * P:(qt + 1) * P],
                                          W(f"fc2{'abcd'[f]}"), start=(f == 0), stop=(f == 3))
                    elif kind == "x_t":
                        pe.wait_ge(mlp_added, b + 1)
                        for qt in range(NT):
                            last = nc.tensor.transpose(out[:, qt * P:(qt + 1) * P], x[:, b, qt, :], ident)
                    last.then_inc(small_ready, 1)

        @block.scalar
        def _(act):
            act.dma_start(pos_i[:, :], a["pos"].rearrange("b t -> (b t)").partition_broadcast(P)).then_inc(pos_loaded, 16)
            act.dma_start(rope_table[:, :], a["rope"].bitcast(BF16)).then_inc(rope_loaded, 16)
            act.dma_start(vec[:, :], a["vec"]).then_inc(rows_loaded, 16)
            act.dma_start(ctx_t[:, :, :], a["ctx_t"].rearrange("b c t -> c b t")).then_inc(ctx_loaded, 16)
            act.dma_start(rows[:, :, :].rearrange("p r c -> p (r c)"), a["rows"].partition_broadcast(P)
                          ).then_inc(rows_loaded, 16)
            act.wait_ge(ctx_loaded, 16)
            nc.scalar.activation(silu[:, 0, :].rearrange("p (b s) -> p b s", b=B), ctx_t[:, :, 0:2], ACT.Exp,
                                 scale=-1.0).then_inc(silu_exp, 1)
            act.wait_ge(rows_loaded, 32)
            for st in steps:
                if st[0] == "score":
                    _, u, c = st
                    n = no(*st)
                    act.wait_ge(scored, n + 1)
                    if n >= PROB_BUFS:
                        act.wait_ge(valued, no("value", *group_of_chunk(n - PROB_BUFS)) + 1)
                    nc.scalar.activation(probs[:, n % PROB_BUFS, :], ps_score[n % SCORE_BUFS][:, :], ACT.Exp, scale=SCALE
                                         ).then_inc(exped, 1)
                elif st[0] == "value" and st[2] == 3:
                    u = st[1]
                    act.wait_ge(valued, 4 * u + 4)
                    if u:
                        act.wait_ge(small_ready, no("small", "unstack", u - 1) + 1)
                    nc.scalar.activation(heads_raw[:, :], ps_heads[:, :], ACT.Copy).then_inc(heads_copied, 1)
                elif st[0] == "small":
                    _, kind, u = st
                    n = no(*st)
                    ps_small = ps_smalls[n % SMALL_BUFS]
                    phase, b = divmod(u, B)
                    if kind == "pick":
                        act.wait_ge(small_ready, n + 1)
                        nc.scalar.activation(rope_picked[:, u, :], ps_small[0:ROPE_ROWS, :], ACT.Copy
                                             ).then_inc(small_used[n % SMALL_BUFS], 1)
                    elif kind == "rope":
                        act.wait_ge(small_ready, n + 1)
                        nc.scalar.activation(rope_cs[:, u, :], ps_small[:, :], ACT.Copy).then_inc(small_used[n % SMALL_BUFS], 1)
                    elif kind in ("q", "k"):
                        if u >= 2:
                            act.wait_ge(*split_done(kind, u - 2))
                            s_, n_ = until(q_placed if kind == "q" else k_placed, u - 2)
                            act.wait_ge(s_, 16 * len(SLOTS) * n_)
                        if kind == "k" and u == 0:
                            act.wait_ge(k_cleared, 1)
                        f = q_f[:, u % 2, 0 if kind == "q" else 1, :]
                        if phase:
                            act.wait_ge(small_ready, n + 1)
                            nc.scalar.activation(f, ps_small[:, 0:T], ACT.Identity, bias=V(f"b{kind}{phase}"))
                            for half, part in part_views(kind, u):
                                last = nc.scalar.activation(part[0], ps_small[half, 0:T], ACT.Identity,
                                                            bias=V(f"b{kind}{phase}")[half, :])
                            last.then_inc(small_used[n % SMALL_BUFS], 1)
                        else:
                            act.wait_ge(roped, 2 * u + turn(kind, u))
                            for half, part in part_views(kind, u):
                                last = nc.scalar.activation(part[0], f[half, :], ACT.Copy)
                            last.then_inc(first_part, 1)
                    elif kind == "v":
                        act.wait_ge(small_ready, n + 1)
                        if u < STACK_BUFS:
                            act.wait_ge(v_cleared, u + 1)
                        else:
                            act.wait_ge(valued, 4 * (u - STACK_BUFS) + 4)
                        dst = v_cols[:, u % STACK_BUFS, :, :, :].rearrange("p n (g r) c -> p (n g) r c", g=2)
                        src = ps_small[:, 0:NT * D].rearrange("p (m r c) -> p m r c", m=2 * NT, c=DH)
                        for i in range(2):
                            last = nc.scalar.activation(dst[:, :, 4 * i:4 * i + 4, 16 * i:16 * i + 8],
                                                        src[:, :, 4 * i:4 * i + 4, :], ACT.Copy)
                        last.then_inc(small_used[n % SMALL_BUFS], 1)
                    elif kind == "heads_t":
                        act.wait_ge(small_ready, n + 1)
                        nc.scalar.activation(heads_t[:, :], ps_small[:, 0:T], ACT.Identity, bias=V(f"bv{phase}")
                                             ).then_inc(small_used[n % SMALL_BUFS], 1)
                    elif kind == "norm_t":
                        act.wait_ge(small_ready, n + 1)
                        if u == 0:
                            act.wait_ge(*used(no("small", "mod", 0)))
                        if phase == 3:
                            nc.scalar.activation(src_t[:, b, :], ps_small[:, 0:T], ACT.Identity, bias=V("b4"),
                                                 scale=V("g4")).then_inc(small_used[n % SMALL_BUFS], 1)
                        else:
                            for s in range(NT):
                                last = nc.scalar.activation(src_t[:, b, s * P:(s + 1) * P], ps_small[:, s * P:(s + 1) * P],
                                                            ACT.Identity,
                                                            bias=mods[:, 2 * phase, 2 * b + s:2 * b + s + 1],
                                                            scale=mods[:, 2 * phase + 1, 2 * b + s:2 * b + s + 1])
                            last.then_inc(small_used[n % SMALL_BUFS], 1)
                    elif kind in ("fc1_lo", "fc1_hi"):
                        act.wait_ge(small_ready, n + 1)
                        for j in range(2):
                            f = 2 * (kind == "fc1_hi") + j
                            last = nc.scalar.activation(hidden[:, f, :], ps_small[:, j * T:(j + 1) * T],
                                                        ACT.Gelu_apprx_tanh, bias=V(f"fc1_{f}"))
                        last.then_inc(small_used[n % SMALL_BUFS], 1)
                    elif kind == "x_t":
                        act.wait_ge(small_ready, n + 1)
                        nc.scalar.activation(src_t[:, b, :], ps_small[:, 0:T], ACT.Copy).then_inc(small_used[n % SMALL_BUFS], 1)

        @block.vector
        def _(dve):
            chain = [0]

            def link(ins):
                chain[0] += 1
                ins.then_inc(dve_chain, 1)
                dve.wait_ge(dve_chain, chain[0])

            def place_onehot(i):
                cols = slice(2 * i * T, 2 * (i + 1) * T)
                link(nc.vector.tensor_copy(pos_f[:, cols], pos_i[:, cols]))
                link(nc.vector.tensor_scalar(pos_neg[:, cols], pos_f[:, cols], 0.0, float(MAX_POS), ALU.is_lt, ALU.mult))
                link(nc.vector.tensor_tensor(pos_f[:, cols], pos_f[:, cols], pos_neg[:, cols], ALU.add))
                link(nc.vector.tensor_scalar(pos_f[:, cols], pos_f[:, cols], 0.0, float(MAX_POS - 1), ALU.max, ALU.min))
                for c in range(POS_CHUNKS):
                    last = nc.vector.tensor_scalar(onehot[:, c, cols], pos_f[:, cols], const[:, C_IOTA + c:C_IOTA + c + 1],
                                                   None, ALU.is_equal)
                last.then_inc(onehot_ready, 1)

            def norm_stats(src, eps):
                for qt in range(NT):
                    last = nc.vector.bn_stats(stats[:, qt, :], src[:, qt, :])
                link(last)
                for qt in range(NT):
                    last = nc.vector.bn_aggr(mean_var[:, qt, :], stats[:, qt, :])
                link(last)
                nc.vector.tensor_scalar(var_eps[:, :], mean_var[:, :, 1], eps, None, ALU.add).then_inc(var_ready, 1)

            def norm_apply(src):
                for qt in range(NT):
                    last = nc.vector.tensor_scalar(normed[:, qt, :], src[:, qt, :], mean_var[:, qt, 0:1],
                                                   rstd[:, qt:qt + 1], ALU.subtract, ALU.mult)
                return last

            dve.wait_ge(const_loaded, 16)
            dve.wait_ge(pos_loaded, 16)
            place_onehot(0)
            nc.vector.tensor_copy(ident16[:, :], ident).then_inc(dve_const, 1)
            nc.vector.memset(mean_mat[:, :], 1.0 / (D * D)).then_inc(dve_const, 1)
            place_onehot(1)
            dve.wait_ge(silu_exp, 1)
            link(nc.vector.tensor_scalar(silu[:, 1, :], silu[:, 0, :], 1.0, None, ALU.add))
            link(nc.vector.reciprocal(silu[:, 2, :], silu[:, 1, :]))
            link(nc.vector.tensor_tensor(silu[:, 3, :].rearrange("p (b s) -> p b s", b=B), ctx_t[:, :, 0:2],
                                         silu[:, 2, :].rearrange("p (b s) -> p b s", b=B), ALU.mult))
            nc.vector.tensor_copy(silu_rep[:, :, :], silu[:, 3, :].unsqueeze(2).broadcast_to([P, 2 * B, P])
                                  ).then_inc(silu_ready, 2)

            def quantise():
                wt = w[:, W_AT["q4"]:W_AT["o4"] + 1, :]
                link(nc.vector.tensor_scalar(quant_s[:, 2, :], quant_s[:, 1, :], 1e-5, None, ALU.add))
                link(nc.vector.reciprocal(quant_s[:, 0, :], quant_s[:, 2, :]))
                link(nc.vector.tensor_tensor(quant[:, :, :], wt, quant_s[:, 0, :].unsqueeze(2).broadcast_to([P, 4, D]),
                                             ALU.mult))
                link(nc.vector.tensor_scalar(quant2[:, :, :], quant[:, :, :], -0.5, None, ALU.is_lt))
                link(nc.vector.scalar_tensor_tensor(quant[:, :, :], quant[:, :, :], 0.5, quant2[:, :, :],
                                                    ALU.is_gt, ALU.subtract))
                link(nc.vector.tensor_tensor(quant2[:, :, :], quant[:, :, :],
                                             quant_s[:, 1, :].unsqueeze(2).broadcast_to([P, 4, D]), ALU.mult))
                link(nc.vector.tensor_tensor(quant[:, :, :], quant2[:, :, :], wt, ALU.subtract))
                nc.vector.tensor_tensor(wt, wt, quant[:, :, :], ALU.add).then_inc(quant_ready, 1)

            for st in steps:
                if st[0] == "max":
                    _, u, i = st
                    n = no(*st)
                    if i == 0 and u >= 2:
                        dve.wait_ge(max_split, u - 1)
                    dve.wait_ge(max_scored, n + 1)
                    if halves(u // B):
                        src = ps_max[n % 2][:, :].rearrange("p (s a k) -> p s a k", s=NT, a=2)
                        dst = neg_max[:, u % 2, :, :, i]
                    else:
                        pair, qt = divmod(i, NT)
                        src = ps_max[n % 2][:, :].rearrange("p (a k) -> p a k", a=2)
                        dst = neg_max[:, u % 2, qt, :, pair]
                    nc.vector.tensor_reduce(dst, src, AX.X, ALU.max, negate=True).then_inc(max_taken, 1)
                    if i == n_banks(u) - 1:
                        dve.wait_ge(max_taken, n + 1)
                        if u >= 2:
                            dve.wait_ge(small_ready, no("small", "max_t", u - 2) + 1)
                        m = neg_max[:, u % 2, :, :, :].rearrange("p n a e -> p (n a) e")
                        mp = max_parts[:, u % 2, :, :, :, :].rearrange("p n a j e -> p (n a) j e")
                        link(nc.vector.tensor_copy(mp[:, :, 0, :], m))
                        nc.vector.tensor_tensor(mp[:, :, 1, :], m, mp[:, :, 0, :], ALU.subtract).then_inc(max_split, 1)
                elif st[0] == "norm":
                    _, u, which = st
                    phase, b = divmod(u, B)
                    dve.wait_ge(rstd_ready, no(*st) + 1)
                    if u:
                        dve.wait_ge(small_ready, no("small", "norm_t", u - 1) + 1)
                    if phase == 3 and which == 0:
                        link(norm_apply(gated[:, :, :]))
                        link(nc.vector.tensor_tensor(gated[:, :, :], normed[:, :, :], row2("g3"), ALU.mult))
                        nc.vector.tensor_tensor(x[:, b, :, :], gated[:, :, :], row2("b3"), ALU.add).then_inc(x_updated, 1)
                        dve.wait_ge(*new_x(u))
                        norm_stats(x[:, b, :, :], 1e-5)
                    else:
                        norm_apply(gated[:, :, :] if phase == 1 else x[:, b, :, :]).then_inc(norm_ready, 1)
                elif st[0] == "small":
                    _, kind, u = st
                    n = no(*st)
                    ps_small = ps_smalls[n % SMALL_BUFS]
                    phase, b = divmod(u, B)
                    if kind in ("q", "k") and phase == 0:
                        dve.wait_ge(small_ready, n + 1)
                        dve.wait_ge(*used(no("small", "rope", u)))
                        if u >= 2:
                            dve.wait_ge(*split_done(kind, u - 2))
                        if 2 * u + turn(kind, u) > 1:
                            dve.wait_ge(roped, 2 * u + turn(kind, u) - 1)
                        cos, sin = rope_cs[:, u, 0:T], rope_cs[:, u, T:2 * T]
                        if kind == "q":
                            if u == 0:
                                dve.wait_ge(rows_loaded, 32)
                            nc.vector.scalar_tensor_tensor(rope_a[:, :], ps_small[:, 0:T], V("bq0"), cos, ALU.add, ALU.mult)
                            last = nc.vector.scalar_tensor_tensor(rope_b[:, :], ps_small[:, T:2 * T], V("bq0r"), sin,
                                                                  ALU.add, ALU.mult)
                        else:
                            nc.vector.tensor_tensor(rope_a[:, :], ps_small[:, 0:T], cos, ALU.mult)
                            last = nc.vector.tensor_tensor(rope_b[:, :], ps_small[:, T:2 * T], sin, ALU.mult)
                        last.then_inc(small_used[n % SMALL_BUFS], 1)
                        dve.wait_ge(*used(n))
                        nc.vector.tensor_tensor(q_f[:, u % 2, 0 if kind == "q" else 1, :], rope_a[:, :], rope_b[:, :],
                                                ALU.add).then_inc(roped, 1)
                    elif kind == "mod":
                        dve.wait_ge(small_ready, n + 1)
                        for k in range(6):
                            last = nc.vector.tensor_scalar(mods[:, k, :], ps_small[:, 2 * B * k:2 * B * (k + 1)],
                                                           V(f"ada_{(0, 1, 3, 4, 6, 7)[k]}"), float(k % 2), ALU.add, ALU.add)
                        last.then_inc(small_used[n % SMALL_BUFS], 1)
                    elif kind == "gate":
                        dve.wait_ge(small_ready, n + 1)
                        nc.vector.tensor_tensor(gates[:, u, :, :], ps_small[:, 0:3 * D].rearrange("p (a b) -> p a b", a=3),
                                                rows[:, R_AT["gate1"]:R_AT["gate3"] + 1, :], ALU.add
                                                ).then_inc(small_used[n % SMALL_BUFS], 1)
                        if u == 2 * B - 1:
                            dve.wait_ge(w_loaded[3], 16)
                            nc.vector.tensor_reduce(quant_s[:, 0, :], w[:, W_AT["q4"]:W_AT["o4"] + 1, :], AX.X, ALU.add,
                                                    apply_absolute_value=True).then_inc(quant_abs, 1)
                    elif kind == "gamma":
                        dve.wait_ge(small_ready, n + 1)
                        nc.vector.tensor_copy(quant_s[:, 1, :], ps_small[:, 0:4]).then_inc(small_used[n % SMALL_BUFS], 1)
                        dve.wait_ge(*used(n))
                        quantise()
                    elif kind == "max_t":
                        dve.wait_ge(small_ready, n + 1)
                        if u >= 2:
                            s_, n_ = until(max_placed, u - 2)
                            dve.wait_ge(s_, 16 * n_)
                        nc.vector.tensor_copy(max_rows[:, u % 2, :], ps_small[:, :].bitcast(BF16)[0:32, 0:T]).then_inc(small_used[n % SMALL_BUFS], 1)
                    elif kind == "unstack":
                        dve.wait_ge(small_ready, n + 1)
                        src = ps_small[:, :].rearrange("p (m e) -> p m e", e=2 * DH)
                        link(nc.vector.reciprocal(inv_sum[:, :], src[:, :, DH]))
                        nc.vector.tensor_tensor(heads[:, :, :].rearrange("p n (h e) -> p (n h) e", e=DH), src[:, :, 0:DH],
                                                inv_sum[:, :].unsqueeze(2).broadcast_to([P, 2 * H, DH]), ALU.mult
                                                ).then_inc(small_used[n % SMALL_BUFS], 1)
                    elif kind == "out_proj":
                        dve.wait_ge(small_ready, n + 1)
                        dve.wait_ge(base_ready, u + 1)
                        if u == B:
                            dve.wait_ge(*used(no("small", "gate", 2 * B - 1)))
                        ps = ps_small[:, 0:NT * D].rearrange("p (n c) -> p n c", n=NT)
                        bs = base[:, u % 2, :, :]
                        xb = x[:, b, :, :]
                        if phase in (1, 2):
                            nc.vector.tensor_tensor(gated[:, :, :], ps, gates[:, 2 * b:2 * b + 2, phase - 1, :], ALU.mult
                                                    ).then_inc(small_used[n % SMALL_BUFS], 1)
                            dve.wait_ge(*used(n))
                            to = gated[:, :, :] if phase == 1 else xb
                            nc.vector.tensor_tensor(to, gated[:, :, :], bs, ALU.add).then_inc(x_updated, 1)
                            dve.wait_ge(*new_x(u))
                            norm_stats(to, 1e-6)
                        elif phase == 0:
                            nc.vector.tensor_tensor(xb, ps, bs, ALU.add).then_inc(small_used[n % SMALL_BUFS], 1)
                            dve.wait_ge(*used(n))
                            norm_stats(xb, 1e-6)
                        elif phase == 3:
                            nc.vector.tensor_tensor(gated[:, :, :], ps, bs, ALU.add).then_inc(small_used[n % SMALL_BUFS], 1)
                            dve.wait_ge(*used(n))
                            norm_stats(gated[:, :, :], 1e-5)
                        else:
                            nc.vector.tensor_tensor(x[:, b, :, :], ps, bs, ALU.add).then_inc(small_used[n % SMALL_BUFS], 1)
                    elif kind == "fc2":
                        dve.wait_ge(small_ready, n + 1)
                        dve.wait_ge(base_mlp_ready, b + 1)
                        ps = ps_small[:, 0:NT * D].rearrange("p (n c) -> p n c", n=NT)
                        nc.vector.tensor_tensor(gated_mlp[:, :, :], ps, gates[:, 2 * b:2 * b + 2, 2, :], ALU.mult
                                                ).then_inc(small_used[n % SMALL_BUFS], 1)
                        dve.wait_ge(*used(n))
                        nc.vector.tensor_tensor(x[:, b, :, :], gated_mlp[:, :, :], base_mlp[:, b % 2, :, :], ALU.add
                                                ).then_inc(mlp_added, 1)


def host_layout(inp):
    i = {k: np.asarray(v) for k, v in inp.items()}
    par, d, pair = np.meshgrid(np.arange(2), np.arange(DH), np.arange(PAIRS), indexing="ij")
    stack = (DH * (2 * pair + par) + d).ravel()
    rot = (DH * (2 * pair + par) + (d + DH // 2) % DH).ravel()
    g, j, ii, dd = np.meshgrid(np.arange(2), np.arange(4), np.arange(2), np.arange(DH), indexing="ij")
    headrow = (DH * (8 * g + 4 * ii + j) + dd).ravel()

    def col(wt, k):
        return wt[:, k * D:(k + 1) * D]

    w = {"q0": i["L0_xattn_Wq"].T[:, stack], "q0r": i["L0_xattn_Wq"].T[:, rot], "k0": i["L0_xattn_Wk"].T[:, stack],
         "k0r": i["L0_xattn_Wk"].T[:, rot], "v0": i["L0_xattn_Wv"].T, "o0": i["L0_xattn_Wo"].T[headrow]}
    v = {"bq0": i["L0_xattn_bq"][stack], "bq0r": i["L0_xattn_bq"][rot], "bv0": i["L0_xattn_bv"][headrow]}
    for p, n in ((1, "attn"), (2, "crs")):
        qkv, bias = i[f"L1_xattn_{n}_qkv_w"], i[f"L1_xattn_{n}_qkv_b"].reshape(3, D)
        w.update({f"q{p}": col(qkv, 0)[:, stack], f"k{p}": col(qkv, 1)[:, stack], f"v{p}": col(qkv, 2),
                  f"o{p}": i[f"L1_xattn_{n}_proj_w"][headrow]})
        v.update({f"bq{p}": bias[0][stack], f"bk{p}": bias[1][stack], f"bv{p}": bias[2][headrow]})
    for k in range(4):
        w[f"fc1{'abcd'[k]}"] = col(i["L1_xattn_mlp_fc1_w"], k)
        w[f"fc2{'abcd'[k]}"] = i["L1_xattn_mlp_fc2_w"][k * D:(k + 1) * D]
        v[f"fc1_{k}"] = i["L1_xattn_mlp_fc1_b"][k * D:(k + 1) * D]
    for k in range(9):
        w[f"ada{k}"] = col(i["L1_xattn_ada_w"], k)
        v[f"ada_{k}"] = i["L1_xattn_ada_b"][k * D:(k + 1) * D]
    qkv, bias = i["L2_xattn_W_qkv"].T, i["L2_xattn_b_qkv"].reshape(3, D)
    w.update({"q3": col(qkv, 0)[:, stack], "k3": col(qkv, 1)[:, stack], "v3": col(qkv, 2), "o3": i["L2_xattn_W_o"].T[headrow]})
    v.update({"bq3": bias[0][stack], "bk3": bias[1][stack], "bv3": bias[2][headrow]})
    w.update({"q4": i["L3_xattn_Wq"].T[:, stack], "k4": i["L3_xattn_Wk"].T[:, stack], "v4": i["L3_xattn_Wv"].T,
              "o4": i["L3_xattn_Wo"].T[headrow]})
    v.update({"bq4": i["L3_xattn_bq"][stack], "bk4": i["L3_xattn_bk"][stack], "bv4": i["L3_xattn_bv"][headrow],
              "g4": i["L3_xattn_ln_gamma"], "b4": i["L3_xattn_ln_beta"]})
    ada_b = i["L1_xattn_ada_b"].reshape(9, D)
    r = {"bo0": i["L0_xattn_bo"], "bo1": i["L1_xattn_attn_proj_b"], "bo2": i["L1_xattn_crs_proj_b"],
         "bfc2": i["L1_xattn_mlp_fc2_b"], "bo3": i["L2_xattn_b_o"], "g3": i["L2_xattn_ln_gamma"],
         "b3": i["L2_xattn_ln_beta"], "bo4": i["L3_xattn_bo"], "gate1": ada_b[2], "gate2": ada_b[5], "gate3": ada_b[8]}
    return {"x": i["x"], "x_t": np.ascontiguousarray(i["x"].transpose(0, 2, 1)),
            "ctx_t": np.ascontiguousarray(i["ctx_1024"].transpose(0, 2, 1)), "pos": i["pos_BxS2"],
            "w": np.concatenate([w[n] for n in W_NAMES], axis=1),
            "vec": np.stack([v[n] for n in V_NAMES], axis=1),
            "rows": np.concatenate([r[n] for n in R_NAMES])}


def constants():
    iota = np.arange(MAX_POS, dtype=np.float32).reshape(POS_CHUNKS, P).T
    inv_freq = 1.0 / 10000.0 ** (np.arange(0, DH, 2, dtype=np.float32) / DH)
    freqs = np.arange(MAX_POS, dtype=np.float32)[:, None] * inv_freq[None, :]
    rest = np.concatenate([np.cos(freqs), np.sin(freqs)], axis=-1).astype(np.float32)
    table = []
    for _ in range(PARTS):
        bits = rest.view(np.uint32) & np.uint32(0xFFFF0000)
        table.append((bits >> 16).astype(np.uint16))
        rest = rest - bits.view(np.float32)
    table = np.concatenate(table, axis=1).reshape(POS_CHUNKS, P, ROPE_ROWS).transpose(1, 0, 2).reshape(P, -1)
    d = np.tile(np.repeat(np.arange(DH), PAIRS), 2)
    spread = np.zeros((P, 2, D), np.float32)
    for r in range(ROPE_ROWS):
        v = r % DH
        spread[r, v // (DH // 2), :] = d % (DH // 2) == v % (DH // 2)
    spread[:, 1, :] *= np.where(d < DH // 2, -1.0, 1.0)[None, :]
    spread = (spread.reshape(P, 2 * D).view(np.uint32) >> 16).astype(np.uint16)
    return {"const": np.concatenate([np.eye(P, dtype=np.float32), iota], axis=1),
            "rope": np.concatenate([table, spread], axis=1)}


def kernel(**inputs):
    import numpy as _np
    import concourse.bacc as _bacc
    from concourse import mybir as _mybir
    from concourse.bass_utils import run_bass_kernel_spmd as _run

    nc = _bacc.Bacc("TRN2", target_bir_lowering=False, num_devices=1)
    arrays, aps = {}, {}
    for name, v in {**host_layout(inputs), **constants()}.items():
        v = _np.ascontiguousarray(v)
        arrays[f"in_{name}"] = v
        aps[name] = nc.dram_tensor(f"in_{name}", v.shape, _mybir.dt.from_np(v.dtype), kind="ExternalInput").ap()
    aps["out"] = nc.dram_tensor("out_0", (B, T, D), F32, kind="ExternalOutput").ap()
    build(nc, aps)
    r = _run(nc, [arrays], core_ids=[0])
    return r.results[0]["out_0"]
```

```python
from contextlib import ExitStack

import numpy as np

import concourse.bass as bass
import concourse.mybir as mybir

F32 = mybir.dt.float32
BF16 = mybir.dt.bfloat16
I32 = mybir.dt.int32
ALU = mybir.AluOpType
ACT = mybir.ActivationFunctionType
AX = mybir.AxisListType

B, T, D = 4, 256, 128
H, DH = 16, 8
P = 128
NT = T // P
PAIRS = H // 2
SCALE = float(DH) ** -0.5
PHASES = 5
UNITS = PHASES * B
MAX_POS = 512
POS_CHUNKS = MAX_POS // P
PARTS = 3
SLOTS = ((0, 2), (1, 1), (2, 0), (0, 1), (1, 0), (0, 0))
SLOT_ROWS = 2 * DH
MAX_ROW = SLOT_ROWS * len(SLOTS)
MAX_ROWS = 4
SCORE_ROWS = MAX_ROW + MAX_ROWS
STACK_BUFS = 3
LATE_SETUP = (0, 14)
BANK = 512
CHUNK = BANK
SMALL_BUFS, MAX_BUFS, SCORE_BUFS = 2, 2, 3
PROB_BUFS = 8
SPLIT_ON_DVE = (("k", 1, 0), ("k", 2, 0), ("k", 4, 1))
ON_DVE = (("max_split", 0), ("max_split", 1), ("max_split", 2), ("max_split", 3), ("max_split", 4),
          ("max_t", 1), ("max_t", 4),
          ("norm", 0), ("norm", 1), ("norm", 2))

W_NAMES = ["q0", "q0r", "k0", "k0r", "v0", "o0",
           "q1", "k1", "v1", "o1", "q2", "k2", "v2", "o2",
           "fc1a", "fc1b", "fc1c", "fc1d", "fc2a", "fc2b", "fc2c", "fc2d",
           "ada0", "ada1", "ada2", "ada3", "ada4", "ada5", "ada6", "ada7", "ada8",
           "q3", "k3", "v3", "o3", "q4", "k4", "v4", "o4"]
W_AT = {n: i for i, n in enumerate(W_NAMES)}
W_GROUPS = (("q0", "o0"), ("q1", "fc2d"), ("ada0", "ada8"), ("q3", "o4"))
V_NAMES = (["bq0", "bq0r", "bv0", "bq1", "bk1", "bv1", "bq2", "bk2", "bv2", "bq3", "bk3", "bv3",
            "bq4", "bk4", "bv4", "g4", "b4"] + [f"fc1_{i}" for i in range(4)] + [f"ada_{i}" for i in range(9)])
V_AT = {n: i for i, n in enumerate(V_NAMES)}
R_NAMES = ["bo0", "bo1", "bo2", "bfc2", "bo3", "g3", "b3", "bo4", "gate1", "gate2", "gate3"]
R_AT = {n: i for i, n in enumerate(R_NAMES)}
C_IDENT, C_IOTA = 0, P
C_COLS = P + POS_CHUNKS
ROPE_ROWS = PARTS * DH
ROPE_COLS = POS_CHUNKS * ROPE_ROWS + 2 * D


def halves(phase):
    return phase in (1, 2)


def n_banks(u):
    return PAIRS if halves(u // B) else 2 * PAIRS


def n_chunks(u):
    return PAIRS if halves(u // B) else H


def group_of_chunk(n):
    u = 0
    while n >= n_chunks(u):
        n -= n_chunks(u)
        u += 1
    return u, n * 4 // n_chunks(u)


def on_dve(work, u):
    return (work, u // B) in ON_DVE


def splitter(kind, u, half):
    return "dve" if (kind, u // B, half) in SPLIT_ON_DVE or u < 1 else "pool"


OFF_PE = {"norm": None, "apply": None, "stats": None, "max_split": None, "stack_max": None,
          "split_q": "pool", "split_k": "pool", "gate_bias": "pool", "quantise": "pool",
          "stack_q": "dma", "stack_k": "dma"}


class Plan:

    def __init__(self):
        self.steps, self.done, self.count = [], {}, {"small": 0, "max": 0, "score": 0}
        self.free = dict(pe=0, act=0, dve=0, pool=0, dma=0)
        self.gelu = False
        self.warm_at = 0

    def run(self, engine, after, cost, gelu=False):
        if engine == "act" and gelu != self.gelu:
            self.gelu, cost = gelu, cost + 1300
        self.free[engine] = max(self.free[engine], after) + cost
        return self.free[engine]

    def waits(self, st):
        kind, u = (st[1], st[2]) if st[0] == "small" else st[:2]
        phase = u // B
        need = []
        if kind in ("split_q", "split_k"):
            return [("part", kind[-1], u)]
        if kind == "gate_bias":
            return [("gate", u)]
        if kind == "quantise":
            return [("gamma", 0)]
        if kind == "max_split":
            return [("maxima", u, n_banks(u) - 1)] + [("max_t", u - 2)] * (u >= 2)
        if kind == "stack_max":
            return [("max_t", u)]
        if kind in ("stack_q", "stack_k"):
            if st[2] == 0:
                return [("part", kind[-1], u)]
            return [("split" + kind[5:], u, half) for half in range(2 if kind == "stack_k" else 1)]
        if st[0] == "small" and self.count["small"] >= SMALL_BUFS:
            need.append(("bank", "small", self.count["small"] - SMALL_BUFS))
        if kind == "max":
            need += [("placed", "q", u), ("placed", "k", u)]
            if self.count["max"] >= MAX_BUFS:
                need.append(("bank", "max", self.count["max"] - MAX_BUFS))
            if u >= 2 and st[2] == 0:
                need.append(("split", u - 2))
        elif kind == "max_t":
            need += [("split", u)] + [("placed", "max", u - 2)] * (u >= 2)
            need += [("score", u - 3, n_chunks(u - 3) - 1)] * (u >= 3)
        elif kind == "score":
            need.append(("placed", "max", u))
            n = self.count["score"]
            if n >= SCORE_BUFS:
                need.append(("bank", "score", n - SCORE_BUFS))
            if n >= PROB_BUFS:
                need.append(("value", *group_of_chunk(n - PROB_BUFS)))
            if st[2] == 0 and phase:
                need.append(("new_x", u - B))
                if phase == 3:
                    need.append(("mlp_added", u - B))
            if st[2] == 0 and phase == 1:
                need += [("gate_bias", 2 * (u % B) + i) for i in range(2)]
            if st[2] == 0 and u >= 2:
                need.append(("new_x", u - 2))
        elif kind == "value":
            need.append(("exp", u, (st[2] + 1) * n_chunks(u) // 4 - 1))
            if st[2] == 0:
                need += [("v", u)] + [("raw", u - 1)] * (u > 0)
            if st[2] == 3 and u:
                need.append(("unstack", u - 1))
        elif kind in ("q", "k", "v"):
            if phase == 0 and kind != "v":
                need.append(("rope", u))
            if phase and (kind == "q" or halves(phase)):
                need.append(("x_t" if (u - B) // B == 2 else "norm_t", u - B))
            if u // B < 2:
                need.append(("loads",) if phase else ("loads0",))
            if phase == 4:
                need.append(("quant",))
            if kind != "v" and u >= 2:
                need.append(("placed", kind, u - 2))
            if u >= STACK_BUFS:
                need.append(("value", u - 3, 3) if kind == "v" else ("score", u - 3, n_chunks(u - 3) - 1))
        elif kind == "pick":
            need.append(("onehot", u))
        elif kind == "rope":
            need.append(("pick", u // 2))
        elif kind == "gamma":
            need.append(("quant_abs",))
        elif kind in ("mod", "gate"):
            need.append(("silu",) if kind == "mod" else ("score", 0, 0))
        elif kind == "unstack":
            need += [("raw", u)] + [("heads_t", u - 1)] * (u > 0)
        elif kind == "heads_t":
            need += [("unstack", u)] + [("out_proj", u - 1)] * (u > 0)
        elif kind == "out_proj":
            need.append(("heads_t", u))
            if u and (u - 1) // B < 4:
                need.append(("norm", u - 1, int((u - 1) // B == 3)))
        elif kind == "apply":
            need.append(("rstd", u) if on_dve("norm", u) else ("norm", u, 0))
        elif kind == "stats":
            need.append(("normed3", u))
        elif kind == "norm":
            need.append(("var", u, st[2]))
            if u:
                need.append(("norm_t", u - 1))
        elif kind == "norm_t":
            need.append(("norm", u, int(phase == 3)))
            if u == 0:
                need.append(("mod", 0))
            if phase == 2:
                need.append(("v", u))
            if phase == 2 and u % B >= 2:
                need.append(("mlp_added", u - 2))
        elif kind in ("fc1_lo", "fc1_hi"):
            need.append(("norm_t", u))
        elif kind == "fc2":
            need.append(("fc1_hi", u))
        elif kind == "x_t":
            need.append(("mlp_added", u))
        return need

    def start(self, st):
        engine = OFF_PE.get(st[0], "pe")
        if st[0] in ("split_q", "split_k") and splitter(st[0][-1], st[1], st[2]) == "dve":
            engine = None
        t = self.free.get(engine, 0)
        for name in self.waits(st):
            if name not in self.done:
                return None
            t = max(t, self.done[name])
        return t

    def append(self, st, t):
        kind, u = (st[1], st[2]) if st[0] == "small" else st[:2]
        phase = u // B
        done, run = self.done, self.run
        self.steps.append(st)
        short = halves(phase)
        if kind == "norm":
            if on_dve("norm", u):
                done["rstd", u] = run("pool", t, 760) + 60
                return
            t = run("pool", t, 760 + 1150)
            if phase == 3 and st[2] == 0:
                done["new_x", u] = done["normed3", u] = run("pool", t, 1500) + 100
            else:
                done["norm", u, st[2]] = t + 60
            return
        if kind in ("split_q", "split_k"):
            on = splitter(kind[-1], u, st[2])
            done[kind, u, st[2]] = run(on, t, 2200 if on == "pool" else 1100)
            return
        if kind == "max_split":
            done["split", u] = (run("dve", t, 400) if on_dve("max_split", u) else run("pool", t, 700)) + 100
            return
        if kind == "apply":
            if on_dve("norm", u):
                done["norm", u, 0] = run("dve", t, 600) + 60
            return
        if kind == "stats":
            done["var", u, 1] = run("dve", t, 900) + 100
            return
        if kind == "gate_bias":
            done[kind, u] = run("pool", t, 1050)
            return
        if kind == "quantise":
            done[("quant",) if u == 3 else (kind, u)] = run("pool", t, 4000)
            return
        if kind == "stack_max":
            done["placed", "max", u] = run("dma", t, 650) + 2000
            return
        if kind in ("stack_q", "stack_k"):
            done[("placed", kind[-1], u) if st[2] else st] = run("dma", t, 3 * 650) + 2000
            return
        pe = {"max": 216, "score": 218, "value": 590 if short else 1020, "q": 440, "k": 440, "v": 430,
              "rope": 500, "pick": 900,
              "max_t": 60, "unstack": 250, "heads_t": 120, "norm_t": 120, "x_t": 120, "out_proj": 430, "fc1_lo": 860,
              "fc1_hi": 860, "fc2": 1720, "mod": 300, "gate": 640, "gamma": 100}[kind]
        if phase == 0 and kind in ("q", "k"):
            pe *= 2
        if t - self.free["pe"] > 3500:
            self.warm_at = t + 5000
        t = run("pe", t, pe * (1 if t >= self.warm_at else 2)) + 180
        if st[0] in self.count:
            n = self.count[st[0]]
            self.count[st[0]] += 1
        if kind == "max":
            t = run("dve", t, 600)
            done["maxima", u, st[2]] = t
            if (u, st[2]) == LATE_SETUP:
                done["onehot", 1] = run("dve", t, 3000)
                done["silu",] = run("dve", t, 1500)
        elif kind == "score":
            t = run("act", t, 480)
            done["exp", u, st[2]] = t + 180
            done["score", u, st[2]] = t
            if st[2] == 0:
                run("pool", 0, 700)
        elif kind == "value":
            done["value", u, st[2]] = t
            if st[2] == 3:
                done["raw", u] = run("act", t, 480) + 180
        elif kind in ("q", "k"):
            if phase == 0:
                t = run("dve", t, 720)
                full = run("dve", t, 400)
                part = run("act", full, 650)
            else:
                t = part = run("act", t, 720 if kind == "q" else 1080)
            done["part", kind, u] = part
            done[kind, u] = t
        elif kind == "v":
            done["v", u] = t = run("act", t, 350) + 100
        elif kind == "max_t":
            t = run("dve", t, 220) if on_dve("max_t", u) else run("act", t, 270)
            done["max_t", u] = t + 60
        elif kind == "unstack":
            done["unstack", u] = t = run("dve", t, 900) + 120
        elif kind == "out_proj":
            t = run("dve", t, 400)
            last = run("dve", t, (400 if phase in (1, 2) else 0) + (900 if phase < 4 else 0))
            if phase != 3:
                done["new_x", u] = last if phase in (1, 2) else t
            done["out_proj", u] = t
            if phase < 4:
                done["var", u, 0] = last
        elif kind == "fc2":
            t = run("dve", t, 350)
            done["mlp_added", u] = run("dve", t, 350) + 150
        elif kind in ("gate", "mod", "gamma"):
            t = run("dve", t, 400)
            done[kind, u] = t
        else:
            cost = {"heads_t": 370, "norm_t": 480, "x_t": 300, "fc1_lo": 740, "fc1_hi": 740, "rope": 480, "pick": 480}[kind]
            done[kind, u] = t = run("act", t, cost, kind in ("fc1_lo", "fc1_hi")) + 120
        if st[0] in self.count:
            done["bank", st[0], n] = t + 60


def handicap(stream, st):
    if st[0] == "small" and st[1] in ("mod", "gate", "gamma", "pick") or st[0] in ("gate_bias", "quantise"):
        return WEIGHTS[stream][0]
    u = st[2] if st[0] == "small" else st[1]
    return WEIGHTS[stream][u // B + 1 if u else 0]


WEIGHTS = (
    (-130, -180, -210, -130, -40, 1220),
    (-10, 0, 30, -70, -370, 130),
    (210, -2260, 560, -270, -320, -330),
    (-1410, -790, -380, -820, -370, -640),
    (-920, -850, -380, -2380, -2030, -1450),
    (-1980, -1060, -3310, -2940, -4230, -3950),
    (-2590, -2950, -40, -160, -1650, -2180),
    (-250, -440, -550, -240, -80, -110),
    (-3060, -3670, 0, 30, 0, -730),
    (0, 0, 0, -70, 0, -70),
    (70, 200, 400, 150, 200, 190),
    (20, 0, 70, 0, 10, 80),
    (-770, -180, -3370, 2430, -1560, -1290),
    (200, -220, -990, 1710, 1240, 2740),
    (10, -570, 450, -190, 4190, 990),
)


def make_schedule():
    units = range(UNITS)
    streams = [
        [s for u in units[:4 * B] for s in [("norm", u, 0), ("apply", u, 0), ("stats", u, 1), ("norm", u, 1),
                                                ("small", "norm_t", u)]
         if s[0] == "small" or (s[0] != "apply" if u // B == 3 else s[2] == 0)],
        [("small", k, u) for u in units for k in ("unstack", "heads_t", "out_proj")],
        [("small", k, u) for u in units if u // B == 2 for k in ("fc1_lo", "fc1_hi", "fc2", "x_t")],
        [s for u in units for s in (("split_k", u, 0), ("split_k", u, 1), ("split_q", u, 0))],
        [("max_split", u, 0) for u in units],
        [("stack_max", u, 0) for u in units],
        [(k, u, rest) for u in units for rest in range(2) for k in ("stack_k", "stack_q")],
        [("small", "max_t", u) for u in units],
        [("small", k, u) for u in units for k in ("k", "q", "v")],
        [("max", u, i) for u in units for i in range(n_banks(u))],
        [("value", u, k) for u in units for k in range(4)],
        [("score", u, c) for u in units for c in range(n_chunks(u))],
        [("small", *s) for i in range(B // 2) for s in (("pick", i), ("rope", 2 * i), ("rope", 2 * i + 1))],
        [("small", "mod", 0)] + [("small", "gate", i) for i in range(2 * B)] + [("small", "gamma", 0)],
        [("gate_bias", i, 0) for i in range(2 * B)] + [("quantise", i, 0) for i in range(4)],
    ]
    plan = Plan()
    plan.done.update({("onehot", 0): 6500, ("loads0",): 6500, ("loads",): 20000, ("quant_abs",): 30000})
    plan.free.update(dve=11500, pool=14500)
    at = [0] * len(streams)
    while True:
        ready = []
        for rank, (stream, i) in enumerate(zip(streams, at)):
            if i < len(stream):
                t = plan.start(stream[i])
                if t is not None:
                    ready.append((t, rank))
        if not ready:
            break
        now = max(plan.free["pe"], min(ready)[0])
        t, rank = min(ready, key=lambda r: (max(r[0], now) + handicap(r[1], streams[r[1]][at[r[1]]]), r[1]))
        plan.append(streams[rank][at[rank]], t)
        at[rank] += 1
    assert at == [len(x) for x in streams], [x[i] for x, i in zip(streams, at) if i < len(x)]
    return plan.steps


def build(nc, a):
    steps = make_schedule()
    order = {}
    seen = {}
    for st in steps:
        assert st not in order, st
        order[st] = seen.get(st[0], 0)
        seen[st[0]] = order[st] + 1

    def no(*step):
        return order[step]

    with ExitStack() as ctx:
        def sb(name, shape, dt=F32):
            return ctx.enter_context(nc.sbuf_tensor(name, shape, dt))

        def sem(name):
            return ctx.enter_context(nc.semaphore(name))

        w = sb("w", [P, len(W_NAMES), D])
        vec = sb("vec", [P, len(V_NAMES)])
        rows = sb("rows", [P, len(R_NAMES), D])
        const = sb("const", [P, C_COLS])
        ident = const[:, C_IDENT:C_IDENT + P]
        ident16 = sb("ident16", [P, P], BF16)
        mean_mat = sb("mean_mat", [P, P])
        pos_i = sb("pos_i", [P, B * T], I32)
        pos_f = sb("pos_f", [P, B * T])
        pos_neg = sb("pos_neg", [P, B * T])
        onehot = sb("onehot", [P, POS_CHUNKS, B * T], BF16)
        rope_table = sb("rope_table", [P, ROPE_COLS], BF16)
        rope_picked = sb("rope_picked", [ROPE_ROWS, B // 2, 2 * T], BF16)
        rope_cs = sb("rope_cs", [P, B, 2 * T])
        x = sb("x", [P, B, NT, D])
        src_t = sb("src_t", [P, B, T])
        ctx_t = sb("ctx_t", [P, B, T])
        silu = sb("silu", [P, 4, 2 * B])
        silu_rep = sb("silu_rep", [P, 2 * B, P])
        mods = sb("mods", [P, 6, 2 * B])
        gates = sb("gates", [P, 2 * B, 3, D])
        gate_bias = sb("gate_bias", [P, 2 * B, 3, D])
        quant = sb("quant", [P, 2, D])
        quant_s = sb("quant_s", [P, 3, 4])
        q_f = sb("q_f", [P, 2, 2, T])
        rope_a = sb("rope_a", [P, T])
        rope_b = sb("rope_b", [P, T])
        split_r = sb("split_r", [P, 2, 2, T])
        q_parts = sb("q_parts", [P, 2, PARTS, T], BF16)
        k_parts = sb("k_parts", [P, 2, PARTS, 2, T], BF16)
        q_stack = sb("q_stack", [P, STACK_BUFS, PAIRS, T], BF16)
        k_stack = sb("k_stack", [P, STACK_BUFS, H, T], BF16)
        v_cols = sb("v_cols", [P, STACK_BUFS, NT, H, 32])
        neg_max = sb("neg_max", [P, 2, NT, 2, PAIRS])
        max_parts = sb("max_parts", [P, 2, NT, 2, 2, PAIRS], BF16)
        max_rows = sb("max_rows", [32, 2, T], BF16)
        probs = sb("probs", [P, PROB_BUFS, CHUNK])
        heads_raw = sb("heads_raw", [P, BANK])
        inv_sum = sb("inv_sum", [P, 2 * H])
        heads = sb("heads", [P, NT, D])
        heads_t = sb("heads_t", [P, T])
        base = sb("base", [P, 2, NT, D])
        base_mlp = sb("base_mlp", [P, 2, NT, D])
        gated = sb("gated", [P, NT, D])
        gated_mlp = sb("gated_mlp", [P, NT, D])
        stats = sb("stats", [P, NT, 6])
        mean_var = sb("mean_var", [P, NT, 2])
        var_eps = sb("var_eps", [P, NT])
        minus_half = sb("minus_half", [P, NT])
        rstd = sb("rstd", [P, NT])
        normed = sb("normed", [P, NT, D])
        hidden = sb("hidden", [P, 4, T])

        ps_max = [ctx.enter_context(nc.psum_tensor(f"ps_max{i}", [P, BANK], F32)) for i in range(MAX_BUFS)]
        ps_score = [ctx.enter_context(nc.psum_tensor(f"ps_score{i}", [P, BANK], F32)) for i in range(SCORE_BUFS)]
        ps_heads = ctx.enter_context(nc.psum_tensor("ps_heads", [P, BANK], F32))
        ps_smalls = [ctx.enter_context(nc.psum_tensor(f"ps_small{i}", [P, BANK], F32)) for i in range(SMALL_BUFS)]

        const_loaded = sem("const_loaded")
        w_loaded = [sem(f"w_loaded{i}") for i in range(len(W_GROUPS))]
        ctx_loaded = [sem(f"ctx_loaded{i}") for i in range(2)]
        src_loaded = [sem(f"src_loaded{i}") for i in range(2)]
        x_loaded = sem("x_loaded")
        vec_loaded = sem("vec_loaded")
        rows_loaded = sem("rows_loaded")
        pos_loaded = [sem(f"pos_loaded{i}") for i in range(2)]
        q_placed = [sem(f"q_placed{i}") for i in range(STACK_BUFS)]
        k_placed = [sem(f"k_placed{i}") for i in range(STACK_BUFS)]
        max_placed = [sem(f"max_placed{i}") for i in range(STACK_BUFS)]
        out_stored = sem("out_stored")
        k_cleared = sem("k_cleared")
        v_cleared = sem("v_cleared")
        ones_set = sem("ones_set")
        dve_const = sem("dve_const")
        rope_loaded = sem("rope_loaded")
        onehot_ready = sem("onehot_ready")
        silu_exp = sem("silu_exp")
        silu_ready = sem("silu_ready")
        quant_abs = sem("quant_abs")
        gamma_ready = sem("gamma_ready")
        quant_ready = sem("quant_ready")
        gate_bias_ready = sem("gate_bias_ready")
        small_ready = sem("small_ready")
        small_used = [sem(f"small_used{i}") for i in range(SMALL_BUFS)]
        max_scored = sem("max_scored")
        max_taken = sem("max_taken")
        max_split = sem("max_split")
        scored = sem("scored")
        exped = sem("exped")
        valued = sem("valued")
        heads_copied = sem("heads_copied")
        first_part = sem("first_part")
        roped = sem("roped")
        q_split = [sem(f"q_split{i}") for i in range(2)]
        k_split = [[sem(f"k_split{half}{i}") for i in range(2)] for half in range(2)]
        base_ready = sem("base_ready")
        base_mlp_ready = sem("base_mlp_ready")
        x_updated = sem("x_updated")
        mlp_added = sem("mlp_added")
        var_ready = sem("var_ready")
        rstd_ready = sem("rstd_ready")
        norm_ready = sem("norm_ready")
        dve_chain = sem("dve_chain")
        pool_chain = sem("pool_chain")

        block = ctx.enter_context(nc.Block())

        def W(name, n=1):
            return w[:, W_AT[name]:W_AT[name] + n, :].rearrange("p a b -> p (a b)")

        def V(name):
            return vec[:, V_AT[name]:V_AT[name] + 1]

        def row2(name):
            return rows[:, R_AT[name]:R_AT[name] + 1, :].broadcast_to([P, NT, D])

        def chunks_until(u):
            return sum(n_chunks(v) for v in range(u + 1))

        def banks_until(u):
            return no("max", u, n_banks(u) - 1) + 1

        def used(n):
            return small_used[n % SMALL_BUFS], n // SMALL_BUFS + 1

        def operands(kind, u):
            if kind in ("q", "k", "v") and u >= B and (kind == "q" or halves(u // B)):
                return [("x_t" if (u - B) // B == 2 else "norm_t", u - B)]
            return {"rope": [("pick", u // 2)], "heads_t": [("unstack", u)], "out_proj": [("heads_t", u)],
                    "fc1_lo": [("norm_t", u)],
                    "fc2": [("fc1_lo", u), ("fc1_hi", u)]}.get(kind, [])

        def until(seq, u):
            return seq[u % STACK_BUFS], u // STACK_BUFS + 1

        def kv_source(u):
            return src_t if halves(u // B) else ctx_t

        def keys_tile(phase, s):
            return s if phase == 1 else 1 - s

        def part_views(kind, u):
            if kind == "q":
                return [(slice(0, P), [q_parts[:, u % 2, j, :] for j in range(PARTS)])]
            half = [slice(P // 2 * par, P // 2 * (par + 1)) for par in range(2)]
            return [(half[par], [k_parts[half[par], u % 2, j, par, :] for j in range(PARTS)]) for par in range(2)]

        def turn(kind, u):
            other = "k" if kind == "q" else "q"
            return 1 if no("small", kind, u) < no("small", other, u) else 2

        def first_part_done(kind, u):
            return used(no("small", kind, u)) if u // B else (first_part, 2 * u + turn(kind, u))

        def split_done(kind, u, half):
            return (q_split if kind == "q" else k_split[half])[u % 2], u // 2 + 1

        def wait_split(engine, kind, u):
            for half in range(1 if kind == "q" else 2):
                engine.wait_ge(*split_done(kind, u, half))

        def split(engine, ops, link, kind, u, half):
            which = 0 if kind == "q" else 1
            engine.wait_ge(*first_part_done(kind, u))
            if u >= 2:
                s_, n_ = until(q_placed if kind == "q" else k_placed, u - 2)
                engine.wait_ge(s_, 16 * len(SLOTS) * n_)
            lines, part = part_views(kind, u)[half]
            full, rest = q_f[lines, u % 2, which, :], split_r[lines, u % 2, which, :]
            link(ops.tensor_tensor(rest, full, part[0], ALU.subtract))
            link(ops.tensor_tensor(part[1], full, part[0], ALU.subtract))
            done = split_done(kind, u, half)
            ops.tensor_tensor(part[2], rest, part[1], ALU.subtract).then_inc(done[0], 1)
            engine.wait_ge(*done)

        def split_max(engine, ops, link, u):
            engine.wait_ge(max_taken, banks_until(u))
            if u >= 2:
                engine.wait_ge(small_ready, no("small", "max_t", u - 2) + 1)
            m = neg_max[:, u % 2, :, :, :].rearrange("p n a e -> p (n a) e")
            mp = max_parts[:, u % 2, :, :, :, :].rearrange("p n a j e -> p (n a) j e")
            link(ops.tensor_copy(mp[:, :, 0, :], m))
            ops.tensor_tensor(mp[:, :, 1, :], m, mp[:, :, 0, :], ALU.subtract).then_inc(max_split, 1)
            engine.wait_ge(max_split, u + 1)

        def read_max(engine, copy, u):
            n = no("small", "max_t", u)
            engine.wait_ge(small_ready, n + 1)
            if u >= 2:
                s_, n_ = until(max_placed, u - 2)
                engine.wait_ge(s_, 16 * n_)
            copy(max_rows[:, u % 2, :], ps_smalls[n % SMALL_BUFS][:, :].bitcast(BF16)[0:32, 0:T]
                 ).then_inc(small_used[n % SMALL_BUFS], 1)

        def apply_norm(engine, ops, u, src):
            if u:
                engine.wait_ge(small_ready, no("small", "norm_t", u - 1) + 1)
            for qt in range(NT):
                last = ops.tensor_scalar(normed[:, qt, :], src[:, qt, :], mean_var[:, qt, 0:1],
                                         rstd[:, qt:qt + 1], ALU.subtract, ALU.mult)
            return last

        def norm_source(u):
            return gated[:, :, :] if u // B == 1 else x[:, u % B, :, :]

        def new_x(u):
            if u // B in (0, 4):
                return used(no("small", "out_proj", u))
            return x_updated, u - B + 1

        @block.sync
        def _(sp):
            def load_w(g):
                lo, hi = W_AT[W_GROUPS[g][0]], W_AT[W_GROUPS[g][1]] + 1
                sp.dma_start(w[:, lo:hi, :], a["w"][:, lo * D:hi * D].rearrange("p (a b) -> p a b", b=D)
                             ).then_inc(w_loaded[g], 16)

            def load_batches(dst, src, i):
                sp.dma_start(dst[:, 2 * i:2 * i + 2, :], a[src][2 * i:2 * i + 2].rearrange("b c t -> c b t")
                             ).then_inc((src_loaded if src == "x_t" else ctx_loaded)[i], 16)

            sp.dma_start(const[:, :], a["const"]).then_inc(const_loaded, 16)
            load_w(0)
            load_batches(ctx_t, "ctx_t", 0)
            load_batches(src_t, "x_t", 0)
            load_batches(ctx_t, "ctx_t", 1)
            load_batches(src_t, "x_t", 1)
            sp.dma_start(x[:, :, :, :].rearrange("p b n c -> p (b n) c"),
                         a["x"].rearrange("b (n p) c -> p (b n) c", p=P)).then_inc(x_loaded, 16)
            load_w(2)
            load_w(1)
            load_w(3)
            for st in steps:
                if st[0] in ("stack_q", "stack_k"):
                    kind, u, rest = st[0][-1], st[1], st[2]
                    buf = u % STACK_BUFS
                    if u >= STACK_BUFS:
                        sp.wait_ge(scored, chunks_until(u - STACK_BUFS))
                    if rest:
                        wait_split(sp, kind, u)
                    else:
                        sp.wait_ge(*first_part_done(kind, u))
                    for slot, (q_part, k_part) in enumerate(SLOTS):
                        r = SLOT_ROWS * slot
                        if ((q_part if kind == "q" else k_part) > 0) != rest:
                            continue
                        if kind == "q":
                            sp.dma_start(q_stack[r:r + SLOT_ROWS, buf, :, :], q_parts[:, u % 2, q_part, :]
                                         ).then_inc(q_placed[buf], 16)
                        else:
                            sp.dma_start(k_stack[r:r + SLOT_ROWS, buf, :, :].rearrange("p h t -> p (h t)"),
                                         k_parts[:, u % 2, k_part, :, :].rearrange("p a t -> p (a t)")
                                         ).then_inc(k_placed[buf], 16)
                if st[0] == "stack_max":
                    u = st[1]
                    sp.wait_ge(*used(no("small", "max_t", u)))
                    sp.dma_start(q_stack[MAX_ROW:MAX_ROW + MAX_ROWS, u % STACK_BUFS, :, :], max_rows[:, u % 2, :]
                                 ).then_inc(max_placed[u % STACK_BUFS], 16)
                if st[0] == "small" and st[1] == "out_proj" and st[2] // B == PHASES - 1:
                    b = st[2] % B
                    sp.wait_ge(*used(no(*st)))
                    sp.dma_start(a["out"][b].rearrange("(n p) c -> p n c", p=P), x[:, b, :, :]
                                 ).then_inc(out_stored, 16)
            sp.wait_ge(out_stored, 16 * B)

        @block.gpsimd
        def _(pool):
            chain = [0]

            def link(ins):
                chain[0] += 1
                ins.then_inc(pool_chain, 1)
                pool.wait_ge(pool_chain, chain[0])

            link(nc.gpsimd.memset(minus_half[:, :], -0.5))
            for par in range(2):
                rows_ = slice(64 * (1 - par), 64 * (1 - par) + 64)
                link(nc.gpsimd.memset(k_parts[rows_, :, :, par, :].rearrange("p b j t -> p (b j) t"), 0.0))
            nc.gpsimd.memset(minus_half[:, :], -0.5).then_inc(k_cleared, 1)
            pool.wait_ge(k_cleared, 1)

            two_ones = float(np.array([0x3F803F80], np.uint32).view(np.float32)[0])
            r = slice(MAX_ROW, MAX_ROW + MAX_ROWS)
            r_even = slice(MAX_ROW, MAX_ROW + MAX_ROWS // 2)
            for buf in range(STACK_BUFS):
                link(nc.gpsimd.memset(k_stack[r, buf, 1::2, :].bitcast(F32), two_ones))
                link(nc.gpsimd.memset(k_stack[r_even, buf, 1::2, :].bitcast(F32), 0.0))
                link(nc.gpsimd.memset(k_stack[r, buf, 0::2, :].bitcast(F32), 0.0))
                nc.gpsimd.memset(k_stack[r_even, buf, 0::2, :].bitcast(F32), two_ones).then_inc(ones_set, 1)
                pool.wait_ge(ones_set, buf + 1)

            def quantise(i):
                at = W_AT["q4"] + i
                wt, ratio, low = w[:, at, :], quant[:, 0, :], quant[:, 1, :]
                gamma, scale = quant_s[:, 1, i:i + 1], quant_s[:, 2, i:i + 1]
                link(nc.gpsimd.tensor_scalar(ratio, wt, scale, None, ALU.mult))
                link(nc.gpsimd.tensor_scalar(low, ratio, -0.5, None, ALU.is_lt))
                link(nc.gpsimd.tensor_scalar(ratio, ratio, 0.5, None, ALU.is_gt))
                link(nc.gpsimd.tensor_tensor(ratio, ratio, low, ALU.subtract))
                link(nc.gpsimd.tensor_scalar(low, ratio, gamma, None, ALU.mult))
                link(nc.gpsimd.tensor_tensor(ratio, low, wt, ALU.subtract))
                nc.gpsimd.tensor_tensor(wt, wt, ratio, ALU.add).then_inc(quant_ready, 1)
                pool.wait_ge(quant_ready, i + 1)

            for st in steps:
                if st[0] in ("split_q", "split_k") and splitter(st[0][-1], st[1], st[2]) == "pool":
                    split(pool, nc.gpsimd, link, st[0][-1], st[1], st[2])
                if st[0] == "max_split" and not on_dve("max_split", st[1]):
                    split_max(pool, nc.gpsimd, link, st[1])
                if st[0] == "quantise":
                    pool.wait_ge(gamma_ready, 1)
                    quantise(st[1])
                if st[0] == "gate_bias":
                    i = st[1]
                    pool.wait_ge(*used(no("small", "gate", i)))
                    if i == 0:
                        pool.wait_ge(rows_loaded, 16)
                    nc.gpsimd.tensor_tensor(gate_bias[:, i, :, :], gates[:, i, :, :],
                                            rows[:, R_AT["bo1"]:R_AT["bfc2"] + 1, :], ALU.mult).then_inc(gate_bias_ready, 1)
                    pool.wait_ge(gate_bias_ready, i + 1)
                if st[0] == "score" and st[2] == 0:
                    u = st[1]
                    phase, b = divmod(u, B)
                    if phase == 0 and b == 0:
                        pool.wait_ge(x_loaded, 16)
                        pool.wait_ge(rows_loaded, 16)
                    if phase:
                        pool.wait_ge(*new_x(u - B))
                    if phase == 3:
                        pool.wait_ge(mlp_added, b + 1)
                    if u >= 2:
                        pool.wait_ge(*new_x(u - 2))
                    if phase in (1, 2):
                        if phase == 1:
                            pool.wait_ge(gate_bias_ready, 2 * b + 2)
                        add = gate_bias[:, 2 * b:2 * b + 2, phase - 1, :]
                    else:
                        add = row2({0: "bo0", 3: "bo3", 4: "bo4"}[phase])
                    nc.gpsimd.tensor_tensor(base[:, u % 2, :, :], x[:, b, :, :], add, ALU.add).then_inc(base_ready, 1)
                    pool.wait_ge(base_ready, u + 1)
                if st[0] == "norm":
                    _, u, which = st
                    phase, b = divmod(u, B)
                    pool.wait_ge(var_ready, no(*st) + 1)
                    nc.gpsimd.tensor_tensor(rstd[:, :], var_eps[:, :], minus_half[:, :], ALU.pow).then_inc(rstd_ready, 1)
                    pool.wait_ge(rstd_ready, no(*st) + 1)
                    if on_dve("norm", u):
                        continue
                    last = apply_norm(pool, nc.gpsimd, u,
                                      gated[:, :, :] if phase == 3 and which == 0 else norm_source(u))
                    if phase == 3 and which == 0:
                        link(last)
                        link(nc.gpsimd.tensor_tensor(gated[:, :, :], normed[:, :, :], row2("g3"), ALU.mult))
                        nc.gpsimd.tensor_tensor(x[:, b, :, :], gated[:, :, :], row2("b3"), ALU.add).then_inc(x_updated, 1)
                        pool.wait_ge(*new_x(u))
                    else:
                        last.then_inc(norm_ready, 1)
                        pool.wait_ge(norm_ready, u + 1)
                if st[0] == "small" and st[1] == "norm_t" and st[2] // B == 2:
                    u = st[2]
                    b = u % B
                    pool.wait_ge(*new_x(u))
                    if b >= 2:
                        pool.wait_ge(mlp_added, b - 1)
                    nc.gpsimd.tensor_tensor(base_mlp[:, b % 2, :, :], x[:, b, :, :], gate_bias[:, 2 * b:2 * b + 2, 2, :],
                                            ALU.add).then_inc(base_mlp_ready, 1)
                    pool.wait_ge(base_mlp_ready, b + 1)

        @block.tensor
        def _(pe):
            def mm(out, lhs_t, rhs, start=True, stop=True, **k):
                return nc.tensor.matmul(out, lhs_t, rhs, start=start, stop=stop, **k)

            pe.wait_ge(const_loaded, 16)
            for st in steps:
                if st[0] == "max":
                    _, u, i = st
                    n = no(*st)
                    phase = u // B
                    buf = u % STACK_BUFS
                    if i == 0:
                        s_, n_ = until(q_placed, u)
                        pe.wait_ge(s_, 16 * len(SLOTS) * n_)
                        s_, n_ = until(k_placed, u)
                        pe.wait_ge(s_, 16 * len(SLOTS) * n_)
                    if n >= MAX_BUFS:
                        pe.wait_ge(max_taken, n - MAX_BUFS + 1)
                    out = ps_max[n % MAX_BUFS]
                    if halves(phase):
                        for s in range(NT):
                            kt = keys_tile(phase, s)
                            last = mm(out[:, s * 2 * P:(s + 1) * 2 * P].rearrange("p (a b) -> p a b", a=2),
                                      q_stack[0:MAX_ROW, buf, i, s * P:(s + 1) * P],
                                      k_stack[0:MAX_ROW, buf, 2 * i:2 * i + 2, kt * P:(kt + 1) * P])
                    else:
                        pair, qt = divmod(i, NT)
                        last = mm(out[:, :], q_stack[0:MAX_ROW, buf, pair, qt * P:(qt + 1) * P],
                                  k_stack[0:MAX_ROW, buf, 2 * pair:2 * pair + 2, :].rearrange("p a b -> p (a b)"))
                    last.then_inc(max_scored, 1)
                elif st[0] == "score":
                    _, u, c = st
                    n = no(*st)
                    phase = u // B
                    buf = u % STACK_BUFS
                    if c == 0:
                        s_, n_ = until(max_placed, u)
                        pe.wait_ge(s_, 16 * n_)
                        if u < STACK_BUFS:
                            pe.wait_ge(ones_set, u + 1)
                    if n >= SCORE_BUFS:
                        pe.wait_ge(exped, n - SCORE_BUFS + 1)
                    out = ps_score[n % SCORE_BUFS]
                    if halves(phase):
                        for hl in range(2):
                            for s in range(NT):
                                h = 2 * c + hl
                                kt = keys_tile(phase, s)
                                col = (hl * NT + s) * P
                                last = mm(out[:, col:col + P], k_stack[0:SCORE_ROWS, buf, h, kt * P:(kt + 1) * P],
                                          q_stack[0:SCORE_ROWS, buf, h // 2, s * P:(s + 1) * P])
                    else:
                        for kt in range(NT):
                            last = mm(out[:, kt * T:(kt + 1) * T], k_stack[0:SCORE_ROWS, buf, c, kt * P:(kt + 1) * P],
                                      q_stack[0:SCORE_ROWS, buf, c // 2, :])
                    last.then_inc(scored, 1)
                elif st[0] == "value":
                    _, u, k = st
                    phase = u // B
                    g, i = divmod(k, 2)
                    first = chunks_until(u) - n_chunks(u)
                    buf = u % STACK_BUFS
                    if k == 0:
                        pe.wait_ge(*used(no("small", "v", u)))
                        if u:
                            pe.wait_ge(heads_copied, u)
                    chunks = n_chunks(u) // 4
                    pe.wait_ge(exped, first + (k + 1) * chunks)
                    if halves(phase):
                        for s in range(NT):
                            for j in range(4):
                                h = 4 * k + j
                                pr = probs[:, (first + h // 2) % PROB_BUFS, :]
                                col = (j % 2 * NT + s) * P
                                last = mm(ps_heads[32 * j:32 * j + 32, g * T + s * P:g * T + (s + 1) * P],
                                          v_cols[:, buf, keys_tile(phase, s), h, :], pr[:, col:col + P],
                                          start=(i == 0 and s == 0), stop=(i == 1 and s == 1),
                                          skip_group_check=True, tile_position=(0, 32 * j))
                    else:
                        for kt in range(NT):
                            for j in range(4):
                                h = 4 * k + j
                                pr = probs[:, (first + h) % PROB_BUFS, :]
                                last = mm(ps_heads[32 * j:32 * j + 32, g * T:(g + 1) * T],
                                          v_cols[:, buf, kt, h, :], pr[:, kt * T:(kt + 1) * T],
                                          start=(i == 0 and kt == 0), stop=(i == 1 and kt == 1),
                                          skip_group_check=True, tile_position=(0, 32 * j))
                    last.then_inc(valued, 1)
                elif st[0] == "small":
                    _, kind, u = st
                    n = no(*st)
                    phase, b = divmod(u, B)
                    if n >= SMALL_BUFS:
                        pe.wait_ge(*used(n - SMALL_BUFS))
                    out = ps_small = ps_smalls[n % SMALL_BUFS]
                    for before in operands(kind, u):
                        pe.wait_ge(*used(no("small", *before)))
                    if kind == "pick":
                        pe.wait_ge(rope_loaded, 16)
                        pe.wait_ge(onehot_ready, u + 1)
                        for c in range(POS_CHUNKS):
                            last = mm(out[0:ROPE_ROWS, :], rope_table[:, c * ROPE_ROWS:(c + 1) * ROPE_ROWS],
                                      onehot[:, c, 2 * u * T:2 * (u + 1) * T], start=(c == 0), stop=(c == POS_CHUNKS - 1))
                    elif kind == "rope":
                        for f in range(2):
                            at = POS_CHUNKS * ROPE_ROWS + f * D
                            last = mm(out[:, f * T:(f + 1) * T], rope_table[0:ROPE_ROWS, at:at + D],
                                      rope_picked[:, u // 2, u % 2 * T:(u % 2 + 1) * T])
                    elif kind == "mod":
                        pe.wait_ge(w_loaded[2], 16)
                        pe.wait_ge(silu_ready, 2)
                        for i, k in enumerate((0, 1, 3, 4, 6, 7)):
                            last = mm(out[:, 2 * B * i:2 * B * (i + 1)], W(f"ada{k}"), silu[:, 3, :])
                    elif kind == "gate":
                        last = mm(out[:, 0:3 * D].rearrange("p (a b) -> p a b", a=3), silu_rep[:, u, :],
                                  w[:, W_AT["ada2"]:W_AT["ada8"] + 1:3, :])
                    elif kind == "gamma":
                        pe.wait_ge(quant_abs, 1)
                        pe.wait_ge(dve_const, 2)
                        last = mm(out[:, 0:4], mean_mat[:, :], quant_s[:, 0, :])
                    elif kind in ("q", "k"):
                        if phase == 0:
                            if u == 0:
                                pe.wait_ge(w_loaded[0], 16)
                            pe.wait_ge((src_loaded if kind == "q" else ctx_loaded)[b // 2], 16)
                        if u == B:
                            pe.wait_ge(w_loaded[1], 16)
                        if u == 3 * B:
                            pe.wait_ge(w_loaded[3], 16)
                        if u == 4 * B:
                            pe.wait_ge(quant_ready, 4)
                        src = (src_t if kind == "q" else kv_source(u))[:, b, :]
                        last = mm(out[:, 0:T], W(f"{kind}{phase}"), src)
                        if phase == 0:
                            last = mm(out[:, T:2 * T], W(f"{kind}0r"), src)
                    elif kind == "v":
                        for kt in range(NT):
                            last = mm(out[:, kt * D:(kt + 1) * D], kv_source(u)[:, b, kt * P:(kt + 1) * P], W(f"v{phase}"))
                    elif kind == "max_t":
                        pe.wait_ge(max_split, u + 1)
                        pe.wait_ge(dve_const, 1)
                        for qt in range(NT):
                            last = nc.tensor.transpose(out[:, :].bitcast(BF16)[0:32, qt * P:(qt + 1) * P],
                                                       max_parts[:, u % 2, qt, :, :, :].rearrange("p a j e -> p (a j e)"),
                                                       ident16[:, :])
                    elif kind == "unstack":
                        pe.wait_ge(heads_copied, u + 1)
                        for qt in range(NT):
                            for g in range(2):
                                last = nc.tensor.transpose(out[:, (qt * 2 + g) * P:(qt * 2 + g + 1) * P],
                                                           heads_raw[:, g * T + qt * P:g * T + (qt + 1) * P], ident)
                    elif kind == "heads_t":
                        for qt in range(NT):
                            last = nc.tensor.transpose(out[:, qt * P:(qt + 1) * P], heads[:, qt, :], ident)
                    elif kind == "out_proj":
                        for qt in range(NT):
                            last = mm(out[:, qt * D:(qt + 1) * D], heads_t[:, qt * P:(qt + 1) * P], W(f"o{phase}"))
                    elif kind == "norm_t":
                        pe.wait_ge(norm_ready, u + 1)
                        for qt in range(NT):
                            last = nc.tensor.transpose(out[:, qt * P:(qt + 1) * P], normed[:, qt, :], ident)
                    elif kind in ("fc1_lo", "fc1_hi"):
                        for j in range(2):
                            f = 2 * (kind == "fc1_hi") + j
                            last = mm(out[:, j * T:(j + 1) * T], W(f"fc1{'abcd'[f]}"), src_t[:, b, :])
                    elif kind == "fc2":
                        for qt in range(NT):
                            for f in range(4):
                                last = mm(out[:, qt * D:(qt + 1) * D], hidden[:, f, qt * P:(qt + 1) * P],
                                          W(f"fc2{'abcd'[f]}"), start=(f == 0), stop=(f == 3))
                    elif kind == "x_t":
                        pe.wait_ge(mlp_added, b + 1)
                        for qt in range(NT):
                            last = nc.tensor.transpose(out[:, qt * P:(qt + 1) * P], x[:, b, qt, :], ident)
                    last.then_inc(small_ready, 1)

        @block.scalar
        def _(act):
            for i in range(2):
                cols = slice(2 * i * T, 2 * (i + 1) * T)
                act.dma_start(pos_i[:, cols], a["pos"].rearrange("b t -> (b t)")[cols].partition_broadcast(P)
                              ).then_inc(pos_loaded[i], 16)
                if i == 0:
                    act.dma_start(rope_table[:, :], a["rope"].bitcast(BF16)).then_inc(rope_loaded, 16)
                    act.dma_start(vec[:, :], a["vec"]).then_inc(vec_loaded, 16)
            act.dma_start(rows[:, :, :].rearrange("p r c -> p (r c)"), a["rows"].partition_broadcast(P)
                          ).then_inc(rows_loaded, 16)
            for i in range(2):
                act.wait_ge(ctx_loaded[i], 16)
            nc.scalar.activation(silu[:, 0, :].rearrange("p (b s) -> p b s", b=B), ctx_t[:, :, 0:2], ACT.Exp,
                                 scale=-1.0).then_inc(silu_exp, 1)
            act.wait_ge(vec_loaded, 16)
            for st in steps:
                if st[0] == "score":
                    _, u, c = st
                    n = no(*st)
                    act.wait_ge(scored, n + 1)
                    if n >= PROB_BUFS:
                        act.wait_ge(valued, no("value", *group_of_chunk(n - PROB_BUFS)) + 1)
                    nc.scalar.activation(probs[:, n % PROB_BUFS, :], ps_score[n % SCORE_BUFS][:, :], ACT.Exp, scale=SCALE
                                         ).then_inc(exped, 1)
                elif st[0] == "value" and st[2] == 3:
                    u = st[1]
                    act.wait_ge(valued, 4 * u + 4)
                    if u:
                        act.wait_ge(small_ready, no("small", "unstack", u - 1) + 1)
                    nc.scalar.activation(heads_raw[:, :], ps_heads[:, :], ACT.Copy).then_inc(heads_copied, 1)
                elif st[0] == "small":
                    _, kind, u = st
                    n = no(*st)
                    ps_small = ps_smalls[n % SMALL_BUFS]
                    phase, b = divmod(u, B)
                    if kind == "pick":
                        act.wait_ge(small_ready, n + 1)
                        nc.scalar.activation(rope_picked[:, u, :], ps_small[0:ROPE_ROWS, :], ACT.Copy
                                             ).then_inc(small_used[n % SMALL_BUFS], 1)
                    elif kind == "rope":
                        act.wait_ge(small_ready, n + 1)
                        nc.scalar.activation(rope_cs[:, u, :], ps_small[:, :], ACT.Copy
                                             ).then_inc(small_used[n % SMALL_BUFS], 1)
                    elif kind in ("q", "k"):
                        if u >= 2:
                            wait_split(act, kind, u - 2)
                            s_, n_ = until(q_placed if kind == "q" else k_placed, u - 2)
                            act.wait_ge(s_, 16 * len(SLOTS) * n_)
                        if kind == "k" and u == 0:
                            act.wait_ge(k_cleared, 1)
                        f = q_f[:, u % 2, 0 if kind == "q" else 1, :]
                        if phase:
                            act.wait_ge(small_ready, n + 1)
                            nc.scalar.activation(f, ps_small[:, 0:T], ACT.Identity, bias=V(f"b{kind}{phase}"))
                            for half, part in part_views(kind, u):
                                last = nc.scalar.activation(part[0], ps_small[half, 0:T], ACT.Identity,
                                                            bias=V(f"b{kind}{phase}")[half, :])
                            last.then_inc(small_used[n % SMALL_BUFS], 1)
                        else:
                            act.wait_ge(roped, 2 * u + turn(kind, u))
                            for half, part in part_views(kind, u):
                                last = nc.scalar.activation(part[0], f[half, :], ACT.Copy)
                            last.then_inc(first_part, 1)
                    elif kind == "v":
                        act.wait_ge(small_ready, n + 1)
                        if u < STACK_BUFS:
                            act.wait_ge(v_cleared, u + 1)
                        else:
                            act.wait_ge(valued, 4 * (u - STACK_BUFS) + 4)
                        dst = v_cols[:, u % STACK_BUFS, :, :, :].rearrange("p n (g r) c -> p (n g) r c", g=2)
                        src = ps_small[:, 0:NT * D].rearrange("p (m r c) -> p m r c", m=2 * NT, c=DH)
                        for i in range(2):
                            last = nc.scalar.activation(dst[:, :, 4 * i:4 * i + 4, 16 * i:16 * i + 8],
                                                        src[:, :, 4 * i:4 * i + 4, :], ACT.Copy)
                        last.then_inc(small_used[n % SMALL_BUFS], 1)
                    elif kind == "max_t":
                        if not on_dve("max_t", u):
                            read_max(act, lambda dst, src: nc.scalar.activation(dst, src, ACT.Copy), u)
                    elif kind == "heads_t":
                        act.wait_ge(small_ready, n + 1)
                        nc.scalar.activation(heads_t[:, :], ps_small[:, 0:T], ACT.Identity, bias=V(f"bv{phase}")
                                             ).then_inc(small_used[n % SMALL_BUFS], 1)
                    elif kind == "norm_t":
                        act.wait_ge(small_ready, n + 1)
                        if u == 0:
                            act.wait_ge(*used(no("small", "mod", 0)))
                        if phase == 3:
                            nc.scalar.activation(src_t[:, b, :], ps_small[:, 0:T], ACT.Identity, bias=V("b4"),
                                                 scale=V("g4")).then_inc(small_used[n % SMALL_BUFS], 1)
                        else:
                            for s in range(NT):
                                last = nc.scalar.activation(src_t[:, b, s * P:(s + 1) * P], ps_small[:, s * P:(s + 1) * P],
                                                            ACT.Identity,
                                                            bias=mods[:, 2 * phase, 2 * b + s:2 * b + s + 1],
                                                            scale=mods[:, 2 * phase + 1, 2 * b + s:2 * b + s + 1])
                            last.then_inc(small_used[n % SMALL_BUFS], 1)
                    elif kind in ("fc1_lo", "fc1_hi"):
                        act.wait_ge(small_ready, n + 1)
                        for j in range(2):
                            f = 2 * (kind == "fc1_hi") + j
                            last = nc.scalar.activation(hidden[:, f, :], ps_small[:, j * T:(j + 1) * T],
                                                        ACT.Gelu_apprx_tanh, bias=V(f"fc1_{f}"))
                        last.then_inc(small_used[n % SMALL_BUFS], 1)
                    elif kind == "x_t":
                        act.wait_ge(small_ready, n + 1)
                        nc.scalar.activation(src_t[:, b, :], ps_small[:, 0:T], ACT.Copy
                                             ).then_inc(small_used[n % SMALL_BUFS], 1)

        @block.vector
        def _(dve):
            chain = [0]

            def link(ins):
                chain[0] += 1
                ins.then_inc(dve_chain, 1)
                dve.wait_ge(dve_chain, chain[0])

            def place_onehot(i):
                cols = slice(2 * i * T, 2 * (i + 1) * T)
                dve.wait_ge(pos_loaded[i], 16)
                link(nc.vector.tensor_copy(pos_f[:, cols], pos_i[:, cols]))
                link(nc.vector.tensor_scalar(pos_neg[:, cols], pos_f[:, cols], 0.0, float(MAX_POS), ALU.is_lt, ALU.mult))
                link(nc.vector.tensor_tensor(pos_f[:, cols], pos_f[:, cols], pos_neg[:, cols], ALU.add))
                link(nc.vector.tensor_scalar(pos_f[:, cols], pos_f[:, cols], 0.0, float(MAX_POS - 1), ALU.max, ALU.min))
                for c in range(POS_CHUNKS):
                    last = nc.vector.tensor_scalar(onehot[:, c, cols], pos_f[:, cols], const[:, C_IOTA + c:C_IOTA + c + 1],
                                                   None, ALU.is_equal)
                last.then_inc(onehot_ready, 1)

            def norm_stats(src, eps):
                for qt in range(NT):
                    last = nc.vector.bn_stats(stats[:, qt, :], src[:, qt, :])
                link(last)
                for qt in range(NT):
                    last = nc.vector.bn_aggr(mean_var[:, qt, :], stats[:, qt, :])
                link(last)
                nc.vector.tensor_scalar(var_eps[:, :], mean_var[:, :, 1], eps, None, ALU.add).then_inc(var_ready, 1)

            def clear_v(buf):
                link(nc.vector.memset(v_cols[:, buf, :, :, :].rearrange("p n h c -> p (n h c)"), 0.0))
                for i in range(2):
                    v = v_cols[:, buf, :, :, :].rearrange("p n (g r) c -> p (n g) r c", g=2)
                    last = nc.vector.memset(v[:, :, 4 * i:4 * i + 4, 16 * i + 8:16 * i + 16], 1.0)
                last.then_inc(v_cleared, 1)

            clear_v(0)
            dve.wait_ge(const_loaded, 16)
            place_onehot(0)
            nc.vector.tensor_copy(ident16[:, :], ident).then_inc(dve_const, 1)
            nc.vector.memset(mean_mat[:, :], 1.0 / (D * D)).then_inc(dve_const, 1)
            clear_v(1)
            clear_v(2)

            def modulation_input():
                dve.wait_ge(silu_exp, 1)
                link(nc.vector.tensor_scalar(silu[:, 1, :], silu[:, 0, :], 1.0, None, ALU.add))
                link(nc.vector.reciprocal(silu[:, 2, :], silu[:, 1, :]))
                link(nc.vector.tensor_tensor(silu[:, 3, :].rearrange("p (b s) -> p b s", b=B), ctx_t[:, :, 0:2],
                                             silu[:, 2, :].rearrange("p (b s) -> p b s", b=B), ALU.mult))
                nc.vector.tensor_copy(silu_rep[:, :, :], silu[:, 3, :].unsqueeze(2).broadcast_to([P, 2 * B, P])
                                      ).then_inc(silu_ready, 2)

            for st in steps:
                if st[0] == "max":
                    _, u, i = st
                    n = no(*st)
                    if i == 0 and u >= 2:
                        dve.wait_ge(max_split, u - 1)
                    dve.wait_ge(max_scored, n + 1)
                    if halves(u // B):
                        src = ps_max[n % MAX_BUFS][:, :].rearrange("p (s a k) -> p s a k", s=NT, a=2)
                        dst = neg_max[:, u % 2, :, :, i]
                    else:
                        pair, qt = divmod(i, NT)
                        src = ps_max[n % MAX_BUFS][:, :].rearrange("p (a k) -> p a k", a=2)
                        dst = neg_max[:, u % 2, qt, :, pair]
                    nc.vector.tensor_reduce(dst, src, AX.X, ALU.max, negate=True).then_inc(max_taken, 1)
                    if (u, i) == LATE_SETUP:
                        place_onehot(1)
                        modulation_input()
                elif st[0] in ("split_q", "split_k"):
                    if splitter(st[0][-1], st[1], st[2]) == "dve":
                        split(dve, nc.vector, link, st[0][-1], st[1], st[2])
                elif st[0] == "max_split":
                    if on_dve("max_split", st[1]):
                        split_max(dve, nc.vector, link, st[1])
                elif st[0] == "apply":
                    u = st[1]
                    if on_dve("norm", u):
                        dve.wait_ge(rstd_ready, no("norm", u, 0) + 1)
                        apply_norm(dve, nc.vector, u, norm_source(u)).then_inc(norm_ready, 1)
                elif st[0] == "stats":
                    u = st[1]
                    dve.wait_ge(*new_x(u))
                    norm_stats(x[:, u % B, :, :], 1e-5)
                elif st[0] == "small":
                    _, kind, u = st
                    n = no(*st)
                    ps_small = ps_smalls[n % SMALL_BUFS]
                    phase, b = divmod(u, B)
                    if kind in ("q", "k") and phase == 0:
                        dve.wait_ge(small_ready, n + 1)
                        dve.wait_ge(*used(no("small", "rope", u)))
                        if u >= 2:
                            wait_split(dve, kind, u - 2)
                        if 2 * u + turn(kind, u) > 1:
                            dve.wait_ge(roped, 2 * u + turn(kind, u) - 1)
                        cos, sin = rope_cs[:, u, 0:T], rope_cs[:, u, T:2 * T]
                        if kind == "q":
                            if u == 0:
                                dve.wait_ge(vec_loaded, 16)
                            nc.vector.scalar_tensor_tensor(rope_a[:, :], ps_small[:, 0:T], V("bq0"), cos, ALU.add, ALU.mult)
                            last = nc.vector.scalar_tensor_tensor(rope_b[:, :], ps_small[:, T:2 * T], V("bq0r"), sin,
                                                                  ALU.add, ALU.mult)
                        else:
                            nc.vector.tensor_tensor(rope_a[:, :], ps_small[:, 0:T], cos, ALU.mult)
                            last = nc.vector.tensor_tensor(rope_b[:, :], ps_small[:, T:2 * T], sin, ALU.mult)
                        last.then_inc(small_used[n % SMALL_BUFS], 1)
                        dve.wait_ge(*used(n))
                        nc.vector.tensor_tensor(q_f[:, u % 2, 0 if kind == "q" else 1, :], rope_a[:, :], rope_b[:, :],
                                                ALU.add).then_inc(roped, 1)
                    elif kind == "mod":
                        dve.wait_ge(small_ready, n + 1)
                        for k in range(6):
                            last = nc.vector.tensor_scalar(mods[:, k, :], ps_small[:, 2 * B * k:2 * B * (k + 1)],
                                                           V(f"ada_{(0, 1, 3, 4, 6, 7)[k]}"), float(k % 2), ALU.add, ALU.add)
                        last.then_inc(small_used[n % SMALL_BUFS], 1)
                    elif kind == "gate":
                        dve.wait_ge(small_ready, n + 1)
                        if u == 0:
                            dve.wait_ge(rows_loaded, 16)
                        nc.vector.tensor_tensor(gates[:, u, :, :], ps_small[:, 0:3 * D].rearrange("p (a b) -> p a b", a=3),
                                                rows[:, R_AT["gate1"]:R_AT["gate3"] + 1, :], ALU.add
                                                ).then_inc(small_used[n % SMALL_BUFS], 1)
                        if u == 2 * B - 1:
                            dve.wait_ge(w_loaded[3], 16)
                            nc.vector.tensor_reduce(quant_s[:, 0, :], w[:, W_AT["q4"]:W_AT["o4"] + 1, :], AX.X, ALU.add,
                                                    apply_absolute_value=True).then_inc(quant_abs, 1)
                    elif kind == "gamma":
                        dve.wait_ge(small_ready, n + 1)
                        nc.vector.tensor_copy(quant_s[:, 1, :], ps_small[:, 0:4]).then_inc(small_used[n % SMALL_BUFS], 1)
                        dve.wait_ge(*used(n))
                        link(nc.vector.tensor_scalar(quant_s[:, 0, :], quant_s[:, 1, :], 1e-5, None, ALU.add))
                        nc.vector.reciprocal(quant_s[:, 2, :], quant_s[:, 0, :]).then_inc(gamma_ready, 1)
                    elif kind == "max_t":
                        if on_dve("max_t", u):
                            read_max(dve, nc.vector.tensor_copy, u)
                    elif kind == "unstack":
                        dve.wait_ge(small_ready, n + 1)
                        src = ps_small[:, :].rearrange("p (m e) -> p m e", e=2 * DH)
                        link(nc.vector.reciprocal(inv_sum[:, :], src[:, :, DH]))
                        nc.vector.tensor_tensor(heads[:, :, :].rearrange("p n (h e) -> p (n h) e", e=DH), src[:, :, 0:DH],
                                                inv_sum[:, :].unsqueeze(2).broadcast_to([P, 2 * H, DH]), ALU.mult
                                                ).then_inc(small_used[n % SMALL_BUFS], 1)
                    elif kind == "out_proj":
                        dve.wait_ge(small_ready, n + 1)
                        dve.wait_ge(base_ready, u + 1)
                        if 0 < u <= 4 * B:
                            dve.wait_ge(norm_ready, u)
                        if phase == 1:
                            dve.wait_ge(*used(no("small", "gate", 2 * b + 1)))
                        ps = ps_small[:, 0:NT * D].rearrange("p (n c) -> p n c", n=NT)
                        bs = base[:, u % 2, :, :]
                        xb = x[:, b, :, :]
                        if phase in (1, 2):
                            nc.vector.tensor_tensor(gated[:, :, :], ps, gates[:, 2 * b:2 * b + 2, phase - 1, :], ALU.mult
                                                    ).then_inc(small_used[n % SMALL_BUFS], 1)
                            dve.wait_ge(*used(n))
                            to = gated[:, :, :] if phase == 1 else xb
                            nc.vector.tensor_tensor(to, gated[:, :, :], bs, ALU.add).then_inc(x_updated, 1)
                            dve.wait_ge(*new_x(u))
                            norm_stats(to, 1e-6)
                        elif phase == 0:
                            nc.vector.tensor_tensor(xb, ps, bs, ALU.add).then_inc(small_used[n % SMALL_BUFS], 1)
                            dve.wait_ge(*used(n))
                            norm_stats(xb, 1e-6)
                        elif phase == 3:
                            nc.vector.tensor_tensor(gated[:, :, :], ps, bs, ALU.add).then_inc(small_used[n % SMALL_BUFS], 1)
                            dve.wait_ge(*used(n))
                            norm_stats(gated[:, :, :], 1e-5)
                        else:
                            nc.vector.tensor_tensor(x[:, b, :, :], ps, bs, ALU.add).then_inc(small_used[n % SMALL_BUFS], 1)
                    elif kind == "fc2":
                        dve.wait_ge(small_ready, n + 1)
                        dve.wait_ge(base_mlp_ready, b + 1)
                        ps = ps_small[:, 0:NT * D].rearrange("p (n c) -> p n c", n=NT)
                        nc.vector.tensor_tensor(gated_mlp[:, :, :], ps, gates[:, 2 * b:2 * b + 2, 2, :], ALU.mult
                                                ).then_inc(small_used[n % SMALL_BUFS], 1)
                        dve.wait_ge(*used(n))
                        nc.vector.tensor_tensor(x[:, b, :, :], gated_mlp[:, :, :], base_mlp[:, b % 2, :, :], ALU.add
                                                ).then_inc(mlp_added, 1)


def host_layout(inp):
    i = {k: np.asarray(v) for k, v in inp.items()}
    par, d, pair = np.meshgrid(np.arange(2), np.arange(DH), np.arange(PAIRS), indexing="ij")
    stack = (DH * (2 * pair + par) + d).ravel()
    rot = (DH * (2 * pair + par) + (d + DH // 2) % DH).ravel()
    g, j, ii, dd = np.meshgrid(np.arange(2), np.arange(4), np.arange(2), np.arange(DH), indexing="ij")
    headrow = (DH * (8 * g + 4 * ii + j) + dd).ravel()

    def col(wt, k):
        return wt[:, k * D:(k + 1) * D]

    w = {"q0": i["L0_xattn_Wq"].T[:, stack], "q0r": i["L0_xattn_Wq"].T[:, rot], "k0": i["L0_xattn_Wk"].T[:, stack],
         "k0r": i["L0_xattn_Wk"].T[:, rot], "v0": i["L0_xattn_Wv"].T, "o0": i["L0_xattn_Wo"].T[headrow]}
    v = {"bq0": i["L0_xattn_bq"][stack], "bq0r": i["L0_xattn_bq"][rot], "bv0": i["L0_xattn_bv"][headrow]}
    for p, n in ((1, "attn"), (2, "crs")):
        qkv, bias = i[f"L1_xattn_{n}_qkv_w"], i[f"L1_xattn_{n}_qkv_b"].reshape(3, D)
        w.update({f"q{p}": col(qkv, 0)[:, stack], f"k{p}": col(qkv, 1)[:, stack], f"v{p}": col(qkv, 2),
                  f"o{p}": i[f"L1_xattn_{n}_proj_w"][headrow]})
        v.update({f"bq{p}": bias[0][stack], f"bk{p}": bias[1][stack], f"bv{p}": bias[2][headrow]})
    for k in range(4):
        w[f"fc1{'abcd'[k]}"] = col(i["L1_xattn_mlp_fc1_w"], k)
        w[f"fc2{'abcd'[k]}"] = i["L1_xattn_mlp_fc2_w"][k * D:(k + 1) * D]
        v[f"fc1_{k}"] = i["L1_xattn_mlp_fc1_b"][k * D:(k + 1) * D]
    for k in range(9):
        w[f"ada{k}"] = col(i["L1_xattn_ada_w"], k)
        v[f"ada_{k}"] = i["L1_xattn_ada_b"][k * D:(k + 1) * D]
    qkv, bias = i["L2_xattn_W_qkv"].T, i["L2_xattn_b_qkv"].reshape(3, D)
    w.update({"q3": col(qkv, 0)[:, stack], "k3": col(qkv, 1)[:, stack], "v3": col(qkv, 2),
              "o3": i["L2_xattn_W_o"].T[headrow]})
    v.update({"bq3": bias[0][stack], "bk3": bias[1][stack], "bv3": bias[2][headrow]})
    w.update({"q4": i["L3_xattn_Wq"].T[:, stack], "k4": i["L3_xattn_Wk"].T[:, stack], "v4": i["L3_xattn_Wv"].T,
              "o4": i["L3_xattn_Wo"].T[headrow]})
    v.update({"bq4": i["L3_xattn_bq"][stack], "bk4": i["L3_xattn_bk"][stack], "bv4": i["L3_xattn_bv"][headrow],
              "g4": i["L3_xattn_ln_gamma"], "b4": i["L3_xattn_ln_beta"]})
    ada_b = i["L1_xattn_ada_b"].reshape(9, D)
    r = {"bo0": i["L0_xattn_bo"], "bo1": i["L1_xattn_attn_proj_b"], "bo2": i["L1_xattn_crs_proj_b"],
         "bfc2": i["L1_xattn_mlp_fc2_b"], "bo3": i["L2_xattn_b_o"], "g3": i["L2_xattn_ln_gamma"],
         "b3": i["L2_xattn_ln_beta"], "bo4": i["L3_xattn_bo"], "gate1": ada_b[2], "gate2": ada_b[5], "gate3": ada_b[8]}
    return {"x": i["x"], "x_t": np.ascontiguousarray(i["x"].transpose(0, 2, 1)),
            "ctx_t": np.ascontiguousarray(i["ctx_1024"].transpose(0, 2, 1)), "pos": i["pos_BxS2"],
            "w": np.concatenate([w[n] for n in W_NAMES], axis=1),
            "vec": np.stack([v[n] for n in V_NAMES], axis=1),
            "rows": np.concatenate([r[n] for n in R_NAMES])}


def constants():
    iota = np.arange(MAX_POS, dtype=np.float32).reshape(POS_CHUNKS, P).T
    inv_freq = 1.0 / 10000.0 ** (np.arange(0, DH, 2, dtype=np.float32) / DH)
    freqs = np.arange(MAX_POS, dtype=np.float32)[:, None] * inv_freq[None, :]
    rest = np.concatenate([np.cos(freqs), np.sin(freqs)], axis=-1).astype(np.float32)
    table = []
    for _ in range(PARTS):
        bits = rest.view(np.uint32) & np.uint32(0xFFFF0000)
        table.append((bits >> 16).astype(np.uint16))
        rest = rest - bits.view(np.float32)
    table = np.concatenate(table, axis=1).reshape(POS_CHUNKS, P, ROPE_ROWS).transpose(1, 0, 2).reshape(P, -1)
    d = np.tile(np.repeat(np.arange(DH), PAIRS), 2)
    spread = np.zeros((P, 2, D), np.float32)
    for r in range(ROPE_ROWS):
        v = r % DH
        spread[r, v // (DH // 2), :] = d % (DH // 2) == v % (DH // 2)
    spread[:, 1, :] *= np.where(d < DH // 2, -1.0, 1.0)[None, :]
    spread = (spread.reshape(P, 2 * D).view(np.uint32) >> 16).astype(np.uint16)
    return {"const": np.concatenate([np.eye(P, dtype=np.float32), iota], axis=1),
            "rope": np.concatenate([table, spread], axis=1)}


def kernel(**inputs):
    import numpy as _np
    import concourse.bacc as _bacc
    from concourse import mybir as _mybir
    from concourse.bass_utils import run_bass_kernel_spmd as _run

    nc = _bacc.Bacc("TRN2", target_bir_lowering=False, num_devices=1)
    arrays, aps = {}, {}
    for name, v in {**host_layout(inputs), **constants()}.items():
        v = _np.ascontiguousarray(v)
        arrays[f"in_{name}"] = v
        aps[name] = nc.dram_tensor(f"in_{name}", v.shape, _mybir.dt.from_np(v.dtype), kind="ExternalInput").ap()
    aps["out"] = nc.dram_tensor("out_0", (B, T, D), F32, kind="ExternalOutput").ap()
    build(nc, aps)
    r = _run(nc, [arrays], core_ids=[0])
    return r.results[0]["out_0"]
```
